# Optimizing a Trainium2 kernel written in Bass

```python
import numpy as np
import jax
import jax.numpy as jnp

def _softmax(x, axis=-1):
    return jax.nn.softmax(x, axis=axis)

def _gelu(x):
    return jax.nn.gelu(x, approximate=True)

def _silu(x):
    return jax.nn.silu(x)

def _sigmoid(x):
    return jax.nn.sigmoid(x)

def _layernorm(x, axis=-1, eps=1e-05):
    m = jnp.mean(x, axis=axis, keepdims=True)
    v = jnp.var(x, axis=axis, keepdims=True)
    return (x - m) / jnp.sqrt(v + eps)

def _scatter_add(tgt, idx, src, axis=0):
    return tgt.at[idx].add(src)

def _segment_sum(src, seg, n):
    return jax.ops.segment_sum(src, seg, n)
kernel_name = 'mk_gnn_preln_d2_gnn_r8_de98bf'

def setup_inputs(seed: int=0):
    np.random.seed(seed)
    _w = jnp.asarray

    def _rec_inputs():
        import jax
        import jax.numpy as jnp
        _gk = jax.random.key(seed)
        x = -0.000202 + 1 * jax.random.normal(jax.random.fold_in(_gk, 1), (12500, 128), jnp.float32)
        src = jax.random.randint(jax.random.fold_in(_gk, 2), (200000,), 0, 12500, jnp.int32)
        dst = jax.random.randint(jax.random.fold_in(_gk, 3), (200000,), 0, 12500, jnp.int32)
        _o = jnp.argsort(dst, stable=True)
        src = src[_o]
        dst = dst[_o]
        edge_weight1 = jax.random.uniform(jax.random.fold_in(_gk, 13), (200000, 1), jnp.float32, 0.0, 0.999998)
        return (x, src, dst, edge_weight1)
    x, src, dst, edge_weight1 = _rec_inputs()

    def _L0_gnn_setup():
        import jax, jax.numpy as jnp
        import numpy as np
        N, E = (6250, 100000)
        D_IN, D_HID, D_OUT = (128, 256, 128)

        def _sage_layer(h, edge_src, edge_dst, W, b, inv_deg):
            msgs = h[edge_src]
            agg = jax.ops.segment_sum(msgs, edge_dst, num_segments=h.shape[0]) * inv_deg
            y = jnp.concatenate([h, agg], axis=1)
            return y @ W + b
        key = jax.random.key(seed)
        k = jax.random.split(key, 7)
        x = jax.random.normal(k[0], (N, D_IN), dtype=jnp.float32)
        edge_src = jax.random.randint(k[1], (E,), 0, N, dtype=jnp.int32)
        edge_dst = jax.random.randint(k[2], (E,), 0, N, dtype=jnp.int32)
        s1 = 1.0 / np.sqrt(2 * D_IN)
        s2 = 1.0 / np.sqrt(2 * D_HID)
        W1 = jax.random.uniform(k[3], (2 * D_IN, D_HID), jnp.float32, -s1, s1)
        b1 = jax.random.uniform(k[4], (D_HID,), jnp.float32, -s1, s1)
        W2 = jax.random.uniform(k[5], (2 * D_HID, D_OUT), jnp.float32, -s2, s2)
        b2 = jax.random.uniform(k[6], (D_OUT,), jnp.float32, -s2, s2)
        return {'x': x, 'edge_src': edge_src, 'edge_dst': edge_dst, 'W1': W1, 'b1': b1, 'W2': W2, 'b2': b2}
    _L0_gnn_all = _L0_gnn_setup()
    _L0_gnn_in = {k: v for k, v in _L0_gnn_all.items() if k in ('W1', 'b1', 'W2', 'b2')}
    del _L0_gnn_all

    def _L1_gnn_setup():
        import jax, jax.numpy as jnp
        import numpy as np
        N, E, IN_DIM, HID, HEADS, LAYERS = (6250, 40000, 128, 128, 4, 2)
        C = HID // HEADS
        EPS = 1e-05

        def _init(key, shape, fan_in):
            return jax.random.normal(key, shape, dtype=jnp.float32) / np.sqrt(fan_in)

        def _transformer_conv(h, src, tgt, edge_attr, Wq, bq, Wk, bk, Wv, bv, We, Wskip, bskip, Wbeta):
            n = h.shape[0]
            q = (h @ Wq + bq).reshape(n, HEADS, C)
            k = (h @ Wk + bk).reshape(n, HEADS, C)
            v = (h @ Wv + bv).reshape(n, HEADS, C)
            e = (edge_attr @ We).reshape(-1, HEADS, C)
            k_j = k[src] + e
            alpha = jnp.einsum('ehc,ehc->eh', q[tgt], k_j) / jnp.sqrt(jnp.float32(C))
            amax = jax.ops.segment_max(alpha, tgt, num_segments=n)
            ex = jnp.exp(alpha - amax[tgt])
            denom = jax.ops.segment_sum(ex, tgt, num_segments=n)
            a = ex / denom[tgt]
            msg = (v[src] + e) * a[..., None]
            out = jax.ops.segment_sum(msg, tgt, num_segments=n).reshape(n, HID)
            x_r = h @ Wskip + bskip
            beta = jax.nn.sigmoid(jnp.concatenate([out, x_r, out - x_r], axis=-1) @ Wbeta)
            return beta * x_r + (1.0 - beta) * out

        def _batchnorm(h, gamma, beta):
            mu = h.mean(axis=0)
            var = h.var(axis=0)
            return gamma * (h - mu) * jax.lax.rsqrt(var + EPS) + beta
        key = jax.random.key(seed)
        ks = jax.random.split(key, 20)
        x = jax.random.normal(ks[0], (N, IN_DIM), dtype=jnp.float32)
        edge_index = jax.random.randint(ks[1], (2, E), 0, N, dtype=jnp.int64)
        edge_attr = jax.random.uniform(ks[2], (E, 1), dtype=jnp.float32)
        inp = {'x': x, 'edge_index': edge_index, 'edge_attr': edge_attr, 'W_in': _init(ks[3], (IN_DIM, HID), IN_DIM), 'b_in': jnp.zeros((HID,), jnp.float32), 'Wq': _init(ks[4], (LAYERS, HID, HID), HID), 'bq': jnp.zeros((LAYERS, HID), jnp.float32), 'Wk': _init(ks[5], (LAYERS, HID, HID), HID), 'bk': jnp.zeros((LAYERS, HID), jnp.float32), 'Wv': _init(ks[6], (LAYERS, HID, HID), HID), 'bv': jnp.zeros((LAYERS, HID), jnp.float32), 'We': _init(ks[7], (LAYERS, 1, HID), 1), 'Wskip': _init(ks[8], (LAYERS, HID, HID), HID), 'bskip': jnp.zeros((LAYERS, HID), jnp.float32), 'Wbeta': _init(ks[9], (LAYERS, 3 * HID, 1), 3 * HID), 'bn_gamma': jnp.ones((LAYERS, HID), jnp.float32), 'bn_beta': jnp.zeros((LAYERS, HID), jnp.float32)}
        return inp
    _L1_gnn_all = _L1_gnn_setup()
    _L1_gnn_in = {k: v for k, v in _L1_gnn_all.items() if k in ('W_in', 'b_in', 'Wq', 'bq', 'Wk', 'bk', 'Wv', 'bv', 'We', 'Wskip', 'bskip', 'Wbeta', 'bn_gamma', 'bn_beta')}
    del _L1_gnn_all
    return {'x': x, 'src': src, 'dst': dst, 'edge_weight1': edge_weight1, 'L0_gnn_W1': _L0_gnn_in['W1'], 'L0_gnn_b1': _L0_gnn_in['b1'], 'L0_gnn_W2': _L0_gnn_in['W2'], 'L0_gnn_b2': _L0_gnn_in['b2'], 'L1_gnn_W_in': _L1_gnn_in['W_in'], 'L1_gnn_b_in': _L1_gnn_in['b_in'], 'L1_gnn_Wq': _L1_gnn_in['Wq'], 'L1_gnn_bq': _L1_gnn_in['bq'], 'L1_gnn_Wk': _L1_gnn_in['Wk'], 'L1_gnn_bk': _L1_gnn_in['bk'], 'L1_gnn_Wv': _L1_gnn_in['Wv'], 'L1_gnn_bv': _L1_gnn_in['bv'], 'L1_gnn_We': _L1_gnn_in['We'], 'L1_gnn_Wskip': _L1_gnn_in['Wskip'], 'L1_gnn_bskip': _L1_gnn_in['bskip'], 'L1_gnn_Wbeta': _L1_gnn_in['Wbeta'], 'L1_gnn_bn_gamma': _L1_gnn_in['bn_gamma'], 'L1_gnn_bn_beta': _L1_gnn_in['bn_beta']}

def reference(x, src, dst, edge_weight1, L0_gnn_W1, L0_gnn_b1, L0_gnn_W2, L0_gnn_b2, L1_gnn_W_in, L1_gnn_b_in, L1_gnn_Wq, L1_gnn_bq, L1_gnn_Wk, L1_gnn_bk, L1_gnn_Wv, L1_gnn_bv, L1_gnn_We, L1_gnn_Wskip, L1_gnn_bskip, L1_gnn_Wbeta, L1_gnn_bn_gamma, L1_gnn_bn_beta):
    import jax
    import jax.numpy as jnp

    def _L0_gnn_ref(x, edge_src, edge_dst, W1, b1, W2, b2):
        import jax, jax.numpy as jnp
        import numpy as np
        N, E = (6250, 100000)
        D_IN, D_HID, D_OUT = (128, 256, 128)

        def _sage_layer(h, edge_src, edge_dst, W, b, inv_deg):
            msgs = h[edge_src]
            agg = jax.ops.segment_sum(msgs, edge_dst, num_segments=h.shape[0]) * inv_deg
            y = jnp.concatenate([h, agg], axis=1)
            return y @ W + b
        n = x.shape[0]
        deg = jax.ops.segment_sum(jnp.ones_like(edge_dst, dtype=x.dtype), edge_dst, num_segments=n)
        inv_deg = (1.0 / jnp.maximum(deg, 1.0))[:, None]
        h = _sage_layer(x, edge_src, edge_dst, W1, b1, inv_deg)
        h = jax.nn.relu(h)
        h = _sage_layer(h, edge_src, edge_dst, W2, b2, inv_deg)
        return jax.nn.log_softmax(h, axis=1)

    def _L1_gnn_ref(x, edge_index, edge_attr, W_in, b_in, Wq, bq, Wk, bk, Wv, bv, We, Wskip, bskip, Wbeta, bn_gamma, bn_beta):
        import jax, jax.numpy as jnp
        import numpy as np
        N, E, IN_DIM, HID, HEADS, LAYERS = (6250, 40000, 128, 128, 4, 2)
        C = HID // HEADS
        EPS = 1e-05

        def _init(key, shape, fan_in):
            return jax.random.normal(key, shape, dtype=jnp.float32) / np.sqrt(fan_in)

        def _transformer_conv(h, src, tgt, edge_attr, Wq, bq, Wk, bk, Wv, bv, We, Wskip, bskip, Wbeta):
            n = h.shape[0]
            q = (h @ Wq + bq).reshape(n, HEADS, C)
            k = (h @ Wk + bk).reshape(n, HEADS, C)
            v = (h @ Wv + bv).reshape(n, HEADS, C)
            e = (edge_attr @ We).reshape(-1, HEADS, C)
            k_j = k[src] + e
            alpha = jnp.einsum('ehc,ehc->eh', q[tgt], k_j) / jnp.sqrt(jnp.float32(C))
            amax = jax.ops.segment_max(alpha, tgt, num_segments=n)
            ex = jnp.exp(alpha - amax[tgt])
            denom = jax.ops.segment_sum(ex, tgt, num_segments=n)
            a = ex / denom[tgt]
            msg = (v[src] + e) * a[..., None]
            out = jax.ops.segment_sum(msg, tgt, num_segments=n).reshape(n, HID)
            x_r = h @ Wskip + bskip
            beta = jax.nn.sigmoid(jnp.concatenate([out, x_r, out - x_r], axis=-1) @ Wbeta)
            return beta * x_r + (1.0 - beta) * out

        def _batchnorm(h, gamma, beta):
            mu = h.mean(axis=0)
            var = h.var(axis=0)
            return gamma * (h - mu) * jax.lax.rsqrt(var + EPS) + beta
        src, tgt = (edge_index[0], edge_index[1])
        h = jax.nn.relu(x @ W_in + b_in)
        for l in range(LAYERS):
            h_res = h
            h = _transformer_conv(h, src, tgt, edge_attr, Wq[l], bq[l], Wk[l], bk[l], Wv[l], bv[l], We[l], Wskip[l], bskip[l], Wbeta[l])
            h = jax.nn.relu(_batchnorm(h, bn_gamma[l], bn_beta[l]))
            h = h + h_res
        return h
    edge_index = jnp.stack([src, dst])
    h = jnp.maximum(_layernorm(x, axis=-1), 0.0)
    x = x + _L0_gnn_ref(h, src, dst, L0_gnn_W1, L0_gnn_b1, L0_gnn_W2, L0_gnn_b2)
    h = jnp.maximum(_layernorm(x, axis=-1), 0.0)
    x = x + _L1_gnn_ref(h, edge_index, edge_weight1, L1_gnn_W_in, L1_gnn_b_in, L1_gnn_Wq, L1_gnn_bq, L1_gnn_Wk, L1_gnn_bk, L1_gnn_Wv, L1_gnn_bv, L1_gnn_We, L1_gnn_Wskip, L1_gnn_bskip, L1_gnn_Wbeta, L1_gnn_bn_gamma, L1_gnn_bn_beta)
    return x

_drawn_inputs = setup_inputs


def setup_inputs(seed=0):
    import zlib

    import numpy as np

    out = dict(_drawn_inputs(seed))
    spreads = {'L1_gnn_b_in': (0.0, 0.1),
     'L1_gnn_bq': (0.0, 0.8),
     'L1_gnn_bk': (0.0, 0.8),
     'L1_gnn_bv': (0.0, 0.625),
     'L1_gnn_bskip': (0.0, 0.61),
     'L1_gnn_bn_gamma': (1.0, 0.2),
     'L1_gnn_bn_beta': (0.0, 0.277)}
    factors = {'L0_gnn_b1': 8.0, 'L0_gnn_b2': 4.804}
    for name, (base, spread) in spreads.items():
        noise = np.random.default_rng([zlib.crc32(name.encode()), seed]).standard_normal(out[name].shape)
        drawn = base * np.exp(spread * noise) if base else spread * noise
        out[name] = jnp.asarray(drawn.astype(out[name].dtype))
    for name, factor in factors.items():
        out[name] = (out[name] * factor).astype(out[name].dtype)
    return out
```

```python
from contextlib import ExitStack, contextmanager

import concourse.bass as bass
from concourse import mybir

ALU = mybir.AluOpType
ACT = mybir.ActivationFunctionType
AX_X = mybir.AxisListType.X
F32 = mybir.dt.float32
I32 = mybir.dt.int32

P = 128
N = 12500
E = 200000
D = 128
HID = 256
HEADS = 4
C = D // HEADS
LAYERS = 2
EPS = 1e-5
BIG = 1e30

NB = -(-N // P)
NP = NB * P
CH = 16
GR = 4
KG = CH // GR
STEPS = -(-(-(-E // P) + NB - 1) // (P)) * P
STEPS = STEPS if STEPS % (2 * CH) == 0 else STEPS + CH
NC_ = STEPS // CH
PAIRS = NC_ // 2
SJ = STEPS // P
GB = 7
NG = NB // GB
GN = GB * P
QW = D + HEADS
AW = HEADS * (C + 2)
MW = D + 1
RING = 2 * CH
PW = 3 * P + 4
RK = 3
HK = 5
assert NB % GB == 0 and NC_ % 2 == 0 and SJ * P == STEPS


class Chain:

    def __init__(self, eng, sem):
        self.eng, self.sem, self.base, self.n = eng, sem, 0, 0

    def link(self, ins):
        self.n += 1
        ins.then_inc(self.sem, 1)
        self.eng.wait_ge(self.sem, self.base + self.n)

    @contextmanager
    def turns(self, count, per):
        start = self.base + self.n
        with self.eng.Fori(0, count) as i:
            self.base, self.n = start + i * per, 0
            yield i
            assert self.n == per, (self.n, per)
        self.base, self.n = start + count * per, 0


@contextmanager
def room(nc, phase):
    with ExitStack() as ctx:
        def sb(name, shape, dt=F32):
            return ctx.enter_context(nc.sbuf_tensor(f"{phase}_{name}", shape, dt))

        def psum(name, shape):
            return ctx.enter_context(nc.psum_tensor(f"{phase}_{name}", shape, F32))

        sems = []

        def sem(name):
            sems.append(nc.alloc_semaphore(f"{phase}_{name}"))
            return sems[-1]

        yield sb, psum, sem
    nc.clear_and_free_semaphores(sems)
    nc.all_engine_barrier()


class Tables:
    pass


def bc(ap, dim, shape):
    return ap.unsqueeze(dim).to_broadcast(shape)


def declare(nc, t, ctx):
    def dram(name, shape, dt=F32):
        return nc.dram_tensor(name, shape, dt, kind="Internal").ap()

    def sb(name, shape, dt=F32):
        return ctx.enter_context(nc.sbuf_tensor(name, shape, dt))

    t.f_d = dram("finish_steps", [STEPS])
    t.t_d = dram("tile_of_step", [STEPS + 2], I32)
    t.b_d = dram("block_of_step", [NC_, CH], I32)
    t.edge_d = dram("edge_records", [P, NC_, RK * CH])
    t.src_d = dram("source_records", [P, NC_, CH], I32)
    t.step_d = dram("step_records", [STEPS, HK])
    t.pen_d = dram("run_penalties", [STEPS, PW])
    t.h_d = dram("sage_in", [NP, D])
    t.p_d = dram("sage_hidden_projected", [NP, D])
    t.r_d = dram("sage_own_part", [NP, D])
    t.x1_d = dram("x_after_sage", [NP, D])
    t.hT_d = dram("conv_in_transposed", [P, NP])
    t.kv_d = dram("key_value", [NP, 2 * D])
    t.xr_d = dram("conv_skip", [NP, D])
    t.inv = sb("inverse_degree", [P, NB])
    t.iota = sb("iota_row", [P, P])
    t.ident = sb("identity", [P, P])
    t.hselT = sb("head_rows", [HEADS, HEADS * CH])
    t.hsel = sb("head_of_row", [HEADS * CH, HEADS])
    t.tsel = sb("step_of_row", [HEADS * CH, CH])


def declare_sums(nc, t, ctx):
    t.acc = ctx.enter_context(nc.sbuf_tensor("sums", [P, NB * AW], F32))
    t.qreg = ctx.enter_context(nc.sbuf_tensor("query_table", [P, NB * QW], F32))


def setup_phase(nc, t, src, dst, wgt):
    with room(nc, "setup") as (sb, psum, sem):
        dlast = sb("dlast", [P, SJ], I32)
        blast = sb("blast", [P, SJ], I32)
        blastf = sb("blastf", [P, SJ])
        fin = sb("fin", [P, SJ])
        sval = sb("sval", [P, SJ])
        part = sb("part", [P, 1])
        hv = sb("hv", [HEADS, HEADS * CH])
        hv1 = sb("hv1", [HEADS, HEADS * CH])
        fbc = sb("fbc", [P, STEPS])
        below = sb("below", [P, STEPS])
        tf = sb("tf", [P, SJ])
        ti = sb("ti", [P, SJ], I32)
        tpi = sb("tpi", [P, SJ], I32)
        tni = sb("tni", [P, SJ], I32)
        bf = sb("bf", [P, SJ])
        bi = sb("bi", [P, SJ], I32)
        b128 = sb("b128", [P, SJ])
        rows = {k: sb(f"rows_{k}", [P, SJ, P], I32) for k in ("dst", "prev", "next", "src")}
        wrow = sb("wrow", [P, SJ, P])
        df = sb("df", [P, SJ, P])
        sf = sb("sf", [P, SJ, P])
        rel = sb("rel", [P, SJ, P])
        dead = sb("dead", [P, SJ, P])
        inblk = sb("inblk", [P, SJ, P])
        pen = sb("pen", [P, SJ, PW])
        prevf = sb("prevf", [P, SJ])
        nextf = sb("nextf", [P, SJ])
        contl = sb("contl", [P, SJ])
        contr = sb("contr", [P, SJ])
        one = sb("one", [P, SJ])
        both = sb("both", [P, SJ])
        srec = sb("srec", [P, SJ, HK])
        erec = sb("erec", [P, NC_, RK * CH])
        srec_i = sb("srec_i", [P, NC_, CH], I32)
        ps = psum("ps_turn", [P, 4, 512])

        iotas = sem("iotas")
        consts = sem("consts")
        dlast_in = sem("dlast_in")
        fin_ready = sem("fin_ready")
        fin_out = sem("fin_out")
        fbc_in = sem("fbc_in")
        steps_ready = sem("steps_ready")
        steps_out = sem("steps_out")
        near_in = sem("near_in")
        rows_in = sem("rows_in")
        chain_v = sem("chain_v")
        recs_ready = sem("recs_ready")
        turned = sem("turned")
        copied = sem("copied")
        tables_out = sem("tables_out")
        dst_rows = dst.rearrange("(t e) -> t e", e=P)
        src_rows = src.rearrange("(t e) -> t e", e=P)
        wgt_rows = wgt.rearrange("(t e) -> t e", e=P)

        with nc.Block() as block:
            @block.sync
            def _(sp):
                with nc.allow_non_contiguous_dma("small tables"):
                    sp.dma_start(dlast[:, :], dst_rows[:, P - 1:P].rearrange("(j p) o -> p (j o)", p=P),
                                 allow_slow_non_contiguous=True).then_inc(dlast_in, 16)
                    sp.wait_ge(fin_ready, 1)
                    sp.dma_start(t.f_d.rearrange("(j p) -> p j", p=P), fin[:, :],
                                 allow_slow_non_contiguous=True).then_inc(fin_out, 16)
                    sp.wait_ge(fin_out, 16)
                    sp.dma_start(fbc[:, :], t.f_d.partition_broadcast(P)).then_inc(fbc_in, 16)
                    sp.wait_ge(steps_ready, 1)
                    sp.dma_start(t.t_d[1:STEPS + 1].rearrange("(j p) -> p j", p=P), ti[:, :],
                                 allow_slow_non_contiguous=True).then_inc(steps_out, 16)
                    sp.dma_start(t.t_d[0:1].rearrange("(a b) -> a b", a=1), ti[0:1, 0:1]).then_inc(steps_out, 16)
                    sp.dma_start(t.t_d[STEPS + 1:STEPS + 2].rearrange("(a b) -> a b", a=1),
                                 ti[P - 1:P, SJ - 1:SJ]).then_inc(steps_out, 16)
                    sp.dma_start(t.b_d.rearrange("(j a) b -> (a b) j", a=P // CH), bi[:, :],
                                 allow_slow_non_contiguous=True).then_inc(steps_out, 16)
                    sp.wait_ge(steps_out, 64)
                    sp.dma_start(tpi[:, :], t.t_d[0:STEPS].rearrange("(j p) -> p j", p=P),
                                 allow_slow_non_contiguous=True).then_inc(near_in, 16)
                    sp.dma_start(tni[:, :], t.t_d[2:STEPS + 2].rearrange("(j p) -> p j", p=P),
                                 allow_slow_non_contiguous=True).then_inc(near_in, 16)
                    sp.wait_ge(recs_ready, 1)
                    sp.dma_start(t.pen_d.rearrange("(j p) w -> p j w", p=P), pen[:, :, :]).then_inc(tables_out, 16)
                    sp.dma_start(t.step_d.rearrange("(j p) w -> p j w", p=P), srec[:, :, :],
                                 allow_slow_non_contiguous=True).then_inc(tables_out, 16)
                    sp.wait_ge(copied, SJ)
                    sp.dma_start(t.edge_d, erec[:, :, :]).then_inc(tables_out, 16)
                    sp.dma_start(t.src_d, srec_i[:, :, :]).then_inc(tables_out, 16)
                    sp.wait_ge(tables_out, 64)

            @block.gpsimd
            def _(pool):
                pool.iota(t.iota[:, :], [[1, P]], 0, 0, allow_small_or_imprecise_dtypes=True).then_inc(iotas, 1)
                pool.iota(part[:, :], [[0, 1]], 0, 1, allow_small_or_imprecise_dtypes=True).then_inc(iotas, 1)
                pool.iota(sval[:, :], [[P, SJ]], 0, 1, allow_small_or_imprecise_dtypes=True).then_inc(iotas, 1)
                pool.iota(hv[:, :], [[1, HEADS * CH]], 0, -CH, allow_small_or_imprecise_dtypes=True).then_inc(iotas, 1)
                pool.wait_ge(steps_ready, 1)

                def gather(out, table, index, j):
                    pool.indirect_dma_start(out[:, j, :], None, table,
                                            bass.IndirectOffsetOnAxis(ap=index[:, j:j + 1], axis=0)).then_inc(rows_in, 16)

                for j in range(SJ):
                    gather(rows["dst"], dst_rows, ti, j)
                    gather(rows["src"], src_rows, ti, j)
                    gather(wrow, wgt_rows, ti, j)
                pool.wait_ge(near_in, 32)
                for j in range(SJ):
                    gather(rows["prev"], dst_rows, tpi, j)
                    gather(rows["next"], dst_rows, tni, j)

            @block.vector
            def _(dve):
                link = Chain(dve, chain_v).link
                dve.wait_ge(iotas, 4)
                link(dve.tensor_scalar(t.ident[:, :], t.iota[:, :], part[:, 0:1], None, ALU.is_equal))
                link(dve.tensor_scalar(hv1[:, :], hv[:, :], 0.0, None, ALU.is_ge))
                link(dve.scalar_tensor_tensor(t.hselT[:, :], hv[:, :], CH - 1.0, hv1[:, :], ALU.is_le, ALU.mult))
                corner = t.ident[0:HEADS * CH, 0:HEADS * CH]
                dve.tensor_reduce(t.hsel[:, :], corner.rearrange("p (h t) -> p h t", h=HEADS), AX_X, ALU.add)
                dve.tensor_reduce(t.tsel[:, :], corner.rearrange("p (h t) -> p t h", h=HEADS), AX_X, ALU.add)
                dve.wait_ge(dlast_in, 16)
                link(dve.tensor_scalar(blast[:, :], dlast[:, :], 7, None, ALU.arith_shift_right))
                link(dve.tensor_copy(blastf[:, :], blast[:, :]))
                dve.tensor_tensor(fin[:, :], blastf[:, :], sval[:, :], ALU.add).then_inc(fin_ready, 1)
                dve.wait_ge(fbc_in, 16)
                for j in range(SJ):
                    link(dve.tensor_scalar(below[:, :], fbc[:, :], sval[:, j:j + 1], 0.0, ALU.is_lt, ALU.add,
                                           accum_out=tf[:, j:j + 1]))
                link(dve.tensor_tensor(bf[:, :], sval[:, :], tf[:, :], ALU.subtract))
                link(dve.tensor_copy(ti[:, :], tf[:, :]))
                link(dve.tensor_scalar(b128[:, :], bf[:, :], float(P), None, ALU.mult))
                dve.tensor_copy(bi[:, :], bf[:, :]).then_inc(steps_ready, 1)
                dve.wait_ge(rows_in, 16 * 5 * SJ)
                link(dve.tensor_copy(df[:, :, :], rows["dst"][:, :, :]))
                link(dve.tensor_copy(sf[:, :, :], rows["src"][:, :, :]))
                full = [P, SJ, P]
                link(dve.tensor_tensor(rel[:, :, :], df[:, :, :], bc(b128[:, :], 2, full), ALU.subtract))
                link(dve.tensor_scalar(inblk[:, :, :], rel[:, :, :], 0.0, None, ALU.is_ge))
                link(dve.scalar_tensor_tensor(inblk[:, :, :], rel[:, :, :], P - 1.0, inblk[:, :, :],
                                              ALU.is_le, ALU.mult))
                link(dve.tensor_scalar(dead[:, :, :], inblk[:, :, :], -1.0, BIG, ALU.add, ALU.mult))
                link(dve.memset(pen[:, :, :], 0.0))
                link(dve.tensor_tensor(pen[:, :, 1:P], df[:, :, 1:P], df[:, :, 0:P - 1], ALU.is_equal))
                link(dve.tensor_tensor(pen[:, :, P + 1:2 * P + 1], df[:, :, :],
                                       df[:, :, 0:1].to_broadcast(full), ALU.is_equal))
                link(dve.tensor_tensor(pen[:, :, 2 * P + 1:3 * P + 1], df[:, :, :],
                                       df[:, :, P - 1:P].to_broadcast(full), ALU.is_equal))
                link(dve.tensor_scalar(pen[:, :, :], pen[:, :, :], -1.0, BIG, ALU.add, ALU.mult))
                link(dve.tensor_copy(prevf[:, :], rows["prev"][:, :, P - 1]))
                link(dve.tensor_copy(nextf[:, :], rows["next"][:, :, 0]))
                link(dve.tensor_tensor(contl[:, :], prevf[:, :], df[:, :, 0], ALU.is_equal))
                link(dve.tensor_tensor(contr[:, :], nextf[:, :], df[:, :, P - 1], ALU.is_equal))
                link(dve.tensor_tensor(one[:, :], df[:, :, 0], df[:, :, P - 1], ALU.is_equal))
                link(dve.tensor_scalar(srec[:, :, 0], contl[:, :], -1.0, BIG, ALU.add, ALU.mult))
                link(dve.tensor_tensor(both[:, :], contl[:, :], one[:, :], ALU.mult))
                link(dve.tensor_scalar(srec[:, :, 1], both[:, :], -1.0, BIG, ALU.add, ALU.mult))
                link(dve.tensor_scalar(srec[:, :, 2], contr[:, :], -1.0, BIG, ALU.add, ALU.mult))
                link(dve.tensor_tensor(both[:, :], contr[:, :], one[:, :], ALU.mult))
                link(dve.tensor_scalar(srec[:, :, 3], both[:, :], -1.0, BIG, ALU.add, ALU.mult))
                dve.tensor_copy(srec[:, :, 4], rel[:, :, 0]).then_inc(recs_ready, 1)

            @block.tensor
            def _(pe):
                pe.wait_ge(recs_ready, 1)
                for j in range(SJ):
                    if j >= 4:
                        pe.wait_ge(copied, j - 3)
                    for k, rows_f in enumerate((rel, wrow, dead, sf)):
                        last = pe.transpose(ps[:, j % 4, P * k:P * k + P], rows_f[:, j, :], t.ident[:, :])
                    last.then_inc(turned, 1)

            @block.scalar
            def _(act):
                per = P // CH
                for j in range(SJ):
                    act.wait_ge(turned, j + 1)
                    act.activation(
                        erec[:, per * j:per * j + per, :].rearrange("p c (k t) -> p k c t", k=RK),
                        ps[:, j % 4, 0:RK * P].rearrange("p (k c t) -> p k c t", k=RK, c=per), ACT.Copy)
                    act.activation(srec_i[:, per * j:per * j + per, :],
                                   ps[:, j % 4, RK * P:4 * P].rearrange("p (c t) -> p c t", c=per),
                                   ACT.Copy).then_inc(copied, 1)


def block_rows(table):
    return table.rearrange("(a p) f -> p a f", p=P)


def rows_of_turn(table, g):
    return block_rows(table)[:, bass.ds(g * GB, GB), :]


def sums_of_turn(t, g, width):
    return t.acc[:, bass.ds(g * (GB * width), GB * width)].rearrange("p (j w) -> p j w", w=width)


class Norm:

    def __init__(self, sb, sem):
        self.mean, self.var, self.std, self.rstd = (sb(f"ln_{k}", [P, GB]) for k in ("mean", "var", "std", "rstd"))
        self.cent, self.sq = (sb(f"ln_{k}", [P, GB, D]) for k in ("cent", "sq"))
        self.var_ready, self.std_ready = sem("var_ready"), sem("std_ready")

    LINKS = 7

    def vector(self, dve, link, x, y, g):
        full = [P, GB, D]
        link(dve.tensor_reduce(self.mean[:, :], x, AX_X, ALU.add))
        link(dve.tensor_scalar(self.mean[:, :], self.mean[:, :], 1.0 / D, None, ALU.mult))
        link(dve.tensor_tensor(self.cent[:, :, :], x, bc(self.mean[:, :], 2, full), ALU.subtract))
        link(dve.tensor_tensor(self.sq[:, :, :], self.cent[:, :, :], self.cent[:, :, :], ALU.mult))
        link(dve.tensor_reduce(self.var[:, :], self.sq[:, :, :], AX_X, ALU.add))
        dve.tensor_scalar(self.var[:, :], self.var[:, :], 1.0 / D, EPS, ALU.mult, ALU.add).then_inc(self.var_ready, 1)
        dve.wait_ge(self.std_ready, g + 1)
        link(dve.reciprocal(self.rstd[:, :], self.std[:, :]))
        link(dve.tensor_tensor(self.sq[:, :, :], self.cent[:, :, :], bc(self.rstd[:, :], 2, full), ALU.mult))
        return dve.tensor_scalar(y, self.sq[:, :, :], 0.0, None, ALU.max)

    def scalar(self, act, g):
        act.wait_ge(self.var_ready, g + 1)
        act.activation(self.std[:, :], self.var[:, :], ACT.Sqrt).then_inc(self.std_ready, 1)


def norm_phase(nc, t, x):
    with room(nc, "norm") as (sb, psum, sem):
        xb = sb("xb", [P, GB, D])
        hb = sb("hb", [P, GB, D])
        x_in, x_used, h_ready, h_out, chain_v = (sem(k) for k in ("x_in", "x_used", "h_ready", "h_out", "chain_v"))
        norm = Norm(sb, sem)

        with nc.Block() as block:
            @block.sync
            def _(sp):
                with sp.Fori(0, NG) as g:
                    sp.wait_ge(x_used, g + 1)
                    sp.dma_start(xb[:, :, :], rows_of_turn(x, g)).then_inc(x_in, 16)

            @block.vector
            def _(dve):
                chain = Chain(dve, chain_v)
                dve.sem_inc(x_used, 1)
                with chain.turns(NG, Norm.LINKS) as g:
                    dve.wait_ge(x_in, 16 * g + 16)
                    dve.wait_ge(h_out, 16 * g + 16)
                    norm.vector(dve, chain.link, xb[:, :, :], hb[:, :, :], g).then_inc(h_ready, 1)
                    dve.sem_inc(x_used, 1)

            @block.scalar
            def _(act):
                act.sem_inc(h_out, 16)
                with act.Fori(0, NG) as g:
                    norm.scalar(act, g)
                    act.wait_ge(h_ready, g + 1)
                    act.dma_start(rows_of_turn(t.h_d, g), hb[:, :, :]).then_inc(h_out, 16)
                act.wait_ge(h_out, 16 * NG + 16)


def sage_edges(nc, t, table, tag):
    with room(nc, tag) as (sb, psum, sem):
        msg = sb("msg", [P, RING, MW])
        sel = sb("sel", [P, RING, P])
        src = sb("src", [P, 2, CH], I32)
        rec = sb("rec", [P, 2, RK * CH])
        blk = sb("blk", [1, 2, CH], I32)
        ps = psum("ps_sums", [P, 4, 512])
        zeroed, go_v, go_p = sem("zeroed"), sem("go_v"), sem("go_p")
        rec_in = [sem(f"rec_in{h}") for h in range(2)]
        blk_in = [sem(f"blk_in{h}") for h in range(2)]
        src_in = [sem(f"src_in{h}") for h in range(2)]
        gathered = [sem(f"gathered{k}") for k in range(2 * KG)]
        rec_used, ps_used = sem("rec_used"), sem("ps_used")
        sel_ready, sums_ready, chain_v = sem("sel_ready"), sem("sums_ready"), sem("chain_v")

        with nc.Block() as block:
            @block.sync
            def _(sp):
                with sp.Fori(0, PAIRS) as g:
                    for h in range(2):
                        c = g * 2 + h
                        sp.wait_ge(sums_ready, KG * c + KG)
                        sp.dma_start(src[:, h, :], t.src_d[:, bass.ds(c, 1), :]).then_inc(src_in[h], 16)
                        sp.wait_ge(rec_used, c + 1)
                        sp.dma_start(rec[:, h, :], t.edge_d[:, bass.ds(c, 1), :]).then_inc(rec_in[h], 16)
                        sp.dma_start(blk[:, h, :], t.b_d[bass.ds(c, 1), :]).then_inc(blk_in[h], 16)

            @block.gpsimd
            def _(pool):
                pool.wait_ge(zeroed, 2)
                with pool.Fori(0, PAIRS) as g:
                    for h in range(2):
                        c = g * 2 + h
                        pool.wait_ge(src_in[h], 16 * g + 16)
                        for k in range(KG):
                            pool.wait_ge(sums_ready, KG * c + k + 1)

                            pool.sem_inc(go_p, 1)
                            for i in range(GR):
                                slot = h * CH + k * GR + i
                                pool.indirect_dma_start(
                                    msg[:, slot, 0:D], None, table,
                                    bass.IndirectOffsetOnAxis(ap=src[:, h, k * GR + i:k * GR + i + 1], axis=0)).then_inc(gathered[h * KG + k], 16)

            @block.vector
            def _(dve):
                chain = Chain(dve, chain_v)
                dve.memset(t.acc[:, :], 0.0).then_inc(zeroed, 1)
                dve.memset(msg[:, :, D:MW], 1.0).then_inc(zeroed, 1)
                dve.wait_ge(zeroed, 2)
                dve.sem_inc(rec_used, 2)
                dve.sem_inc(ps_used, 2)
                regs = [dve.alloc_register(f"{tag}_block{i}") for i in range(CH)]
                with chain.turns(PAIRS, 2 * CH) as g:
                    for h in range(2):
                        c = g * 2 + h
                        dve.wait_ge(rec_in[h], 16 * g + 16)
                        for k in range(KG):
                            place = rec[:, h, k * GR:k * GR + GR]
                            dve.tensor_tensor(sel[:, h * CH + k * GR:h * CH + k * GR + GR, :],
                                              bc(t.iota[:, :], 1, [P, GR, P]), bc(place, 2, [P, GR, P]),
                                              ALU.is_equal).then_inc(sel_ready, 1)
                        dve.wait_ge(blk_in[h], 16 * g + 16)
                        dve.sem_inc(go_v, 1)
                        dve.load(regs, blk[0:1, h, :])
                        at = [dve.snap(r, min_val=0, max_val=NB - 1) for r in regs]
                        for k in range(KG):
                            dve.wait_ge(sums_ready, KG * c + k + 1 + 2 * KG)
                            for i in range(GR):
                                a = t.acc[:, bass.ds(at[k * GR + i] * MW, MW)]
                                part = ps[:, 2 * (k % 2) + i // 2, (i % 2) * MW:(i % 2) * MW + MW]
                                chain.link(dve.tensor_tensor(a, a, part, ALU.add))
                            dve.sem_inc(ps_used, 1)
                        dve.sem_inc(rec_used, 1)

            @block.tensor
            def _(pe):
                pe.sem_inc(sums_ready, 2 * KG)
                with pe.Fori(0, PAIRS) as g:
                    for h in range(2):
                        for k in range(KG):
                            n = g * (2 * KG) + (h * KG + k + 1)
                            pe.wait_ge(sel_ready, n)
                            pe.wait_ge(gathered[h * KG + k], 16 * GR * g + 16 * GR)
                            pe.wait_ge(ps_used, n)
                            for i in range(GR):
                                slot = h * CH + k * GR + i
                                last = pe.matmul(ps[:, 2 * (k % 2) + i // 2, (i % 2) * MW:(i % 2) * MW + MW],
                                                 sel[:, slot, :], msg[:, slot, :], start=True, stop=True)
                            last.then_inc(sums_ready, 1)


SPLIT = ((0, 512), (512, GN))


def sage_dense(nc, t, w1, b1, w2, b2):
    with room(nc, "sage_dense") as (sb, psum, sem):
        w1s = sb("w1s", [P, 2, HID])
        w2s = sb("w2s", [P, 2, 2, D])
        b1s = sb("b1s", [P, 2])
        b2s = sb("b2s", [P, D])
        hb = sb("hb", [P, GB, D])
        mean = sb("mean", [P, GB, D])
        hT = sb("hT", [P, GN])
        aT = sb("aT", [P, GN])
        hid = sb("hid", [P, 2, GN])
        own = sb("own", [P, GB, D])
        nbr = sb("nbr", [P, GB, D])
        ps = psum("ps_in", [P, 4 * 512])
        psh = psum("ps_hid", [P, 2, 1024])
        w_in, h_in, h_used, mean_ready, turned, copied, hid_ready, hid_copied = (
            sem(k) for k in ("w_in", "h_in", "h_used", "mean_ready", "turned", "copied", "hid_ready", "hid_copied"))
        out_ready, own_ready, nbr_ready, stored, chain_v, go_v = (
            sem(k) for k in ("out_ready", "own_ready", "nbr_ready", "stored", "chain_v", "go_v"))

        with nc.Block() as block:
            @block.sync
            def _(sp):
                sp.dma_start(w1s[:, :, :], w1.rearrange("(s k) h -> k s h", k=P)).then_inc(w_in, 16)
                for part in range(2):
                    sp.dma_start(w2s[:, :, part, :], w2[HID * part:HID * part + HID, :]
                                 .rearrange("(c k) o -> k c o", k=P)).then_inc(w_in, 16)
                sp.dma_start(b1s[:, :], b1.rearrange("(c k) -> k c", k=P), allow_slow_non_contiguous=True).then_inc(w_in, 16)
                sp.dma_start(b2s[:, :], b2.partition_broadcast(P)).then_inc(w_in, 16)
                with sp.Fori(0, NG) as g:
                    sp.wait_ge(h_used, g + 1)
                    sp.dma_start(hb[:, :, :], rows_of_turn(t.h_d, g)).then_inc(h_in, 16)

            @block.vector
            def _(dve):
                chain = Chain(dve, chain_v)
                dve.wait_ge(w_in, 80)
                with chain.turns(NG, 1) as g:
                    a = sums_of_turn(t, g, MW)
                    iv = t.inv[:, bass.ds(g * GB, GB)]
                    chain.link(dve.tensor_scalar(iv, a[:, :, D], 1.0, None, ALU.max))
                    dve.sem_inc(go_v, 1)
                    dve.reciprocal(iv, iv).then_inc(own_ready, 1)
                    dve.wait_ge(own_ready, g * 2 + 1)
                    dve.wait_ge(turned, g + 1)
                    dve.tensor_tensor(mean[:, :, :], a[:, :, 0:D], bc(iv, 2, [P, GB, D]), ALU.mult).then_inc(mean_ready, 1)
                    dve.wait_ge(nbr_ready, g + 2)
                    dve.wait_ge(stored, 32 * g + 32)
                    dve.tensor_tensor(own[:, :, :], ps[:, 0:GB * 2 * D].rearrange("p (j w) -> p j w", j=GB)[:, :, 0:D],
                                      bc(b2s[:, :], 1, [P, GB, D]), ALU.add).then_inc(own_ready, 1)

            @block.tensor
            def _(pe):
                pe.sem_inc(turned, 1)
                pe.sem_inc(h_used, 1)
                pe.wait_ge(w_in, 80)
                with pe.Fori(0, NG) as g:
                    pe.wait_ge(h_in, 16 * g + 16)
                    pe.wait_ge(own_ready, g * 2 + 1)
                    pe.wait_ge(nbr_ready, g + 1)
                    for j in range(GB):
                        pe.transpose(ps[:, P * j:P * j + P], hb[:, j, :], t.ident[:, :])
                    pe.wait_ge(mean_ready, g + 1)
                    for j in range(GB):
                        last = pe.transpose(ps[:, 1024 + P * j:1024 + P * j + P], mean[:, j, :], t.ident[:, :])
                    last.then_inc(turned, 1)
                    pe.wait_ge(copied, g * 2 + 2)
                    pe.sem_inc(h_used, 1)
                    for c in range(2):
                        for lo, hi in SPLIT:
                            for s, rows in ((0, hT), (1, aT)):
                                last = pe.matmul(psh[:, c, lo:hi], w1s[:, s, P * c:P * c + P], rows[:, lo:hi],
                                                 start=(s == 0), stop=(s == 1))
                        last.then_inc(hid_ready, 1)
                    pe.wait_ge(hid_copied, g * 2 + 2)
                    for j in range(GB):
                        for c in range(2):
                            last = pe.matmul(ps[:, 2 * D * j:2 * D * j + 2 * D], hid[:, c, P * j:P * j + P],
                                             w2s[:, c, :, :].rearrange("k s o -> k (s o)"), start=(c == 0), stop=(c == 1))
                    last.then_inc(out_ready, 1)

            @block.scalar
            def _(act):
                act.sem_inc(stored, 32)
                act.sem_inc(nbr_ready, 1)
                act.wait_ge(w_in, 80)
                with act.Fori(0, NG) as g:
                    act.wait_ge(turned, g + 2)
                    act.activation(hT[:, :], ps[:, 0:GN], ACT.Copy).then_inc(copied, 1)
                    act.activation(aT[:, :], ps[:, 1024:1024 + GN], ACT.Copy).then_inc(copied, 1)
                    for c in range(2):
                        act.wait_ge(hid_ready, g * 2 + c + 1)
                        act.activation(hid[:, c, :], psh[:, c, 0:GN], ACT.Relu, bias=b1s[:, c:c + 1]).then_inc(hid_copied, 1)
                    act.wait_ge(out_ready, g + 1)
                    act.wait_ge(stored, 32 * g + 32)
                    act.activation(nbr[:, :, :], ps[:, 0:GB * 2 * D].rearrange("p (j w) -> p j w", j=GB)[:, :, D:2 * D],
                                   ACT.Copy).then_inc(nbr_ready, 1)
                    act.wait_ge(own_ready, g * 2 + 2)
                    act.dma_start(rows_of_turn(t.r_d, g), own[:, :, :]).then_inc(stored, 16)
                    act.wait_ge(nbr_ready, g + 2)
                    act.dma_start(rows_of_turn(t.p_d, g), nbr[:, :, :]).then_inc(stored, 16)
                act.wait_ge(stored, 32 * NG + 32)


def sage_output(nc, t, x, w_in_, b_in_):
    with room(nc, "sage_output") as (sb, psum, sem):
        ws = sb("ws", [P, D])
        bs = sb("bs", [P, 1])
        xb = sb("xb", [P, GB, D])
        rb = sb("rb", [P, GB, D])
        y = sb("y", [P, GB, D])
        z = sb("z", [P, GB, D])
        e = sb("e", [P, GB, D])
        x1 = sb("x1", [P, GB, D])
        hn = sb("hn", [P, GB, D])
        top = sb("top", [P, GB])
        tot = sb("tot", [P, GB])
        lse = sb("lse", [P, GB])
        hT = sb("hT", [P, GN])
        res = sb("res", [P, GN])
        ps = psum("ps_turn", [P, 1024])
        psw = psum("ps_win", [P, 1024])
        w_in, x_in, x_used, z_ready, exp_ready, tot_ready, lse_ready, x1_ready = (
            sem(k) for k in ("w_in", "x_in", "x_used", "z_ready", "exp_ready", "tot_ready", "lse_ready", "x1_ready"))
        hn_ready, turned, copied, prod_ready, res_ready, stored, chain_v = (
            sem(k) for k in ("hn_ready", "turned", "copied", "prod_ready", "res_ready", "stored", "chain_v"))
        norm = Norm(sb, sem)
        full = [P, GB, D]

        with nc.Block() as block:
            @block.sync
            def _(sp):
                sp.dma_start(ws[:, :], w_in_).then_inc(w_in, 16)
                sp.dma_start(bs[:, :], b_in_.rearrange("(k a) -> k a", a=1), allow_slow_non_contiguous=True).then_inc(w_in, 16)
                with sp.Fori(0, NG) as g:
                    sp.wait_ge(x_used, g + 1)
                    sp.dma_start(xb[:, :, :], rows_of_turn(x, g)).then_inc(x_in, 16)
                    sp.dma_start(rb[:, :, :], rows_of_turn(t.r_d, g)).then_inc(x_in, 16)

            @block.vector
            def _(dve):
                chain = Chain(dve, chain_v)
                link = chain.link
                dve.sem_inc(x_used, 1)
                with chain.turns(NG, 4 + Norm.LINKS) as g:
                    iv = t.inv[:, bass.ds(g * GB, GB)]
                    dve.wait_ge(x_in, 32 * g + 32)
                    link(dve.tensor_tensor(y[:, :, :], sums_of_turn(t, g, MW)[:, :, 0:D], bc(iv, 2, full), ALU.mult))
                    link(dve.tensor_tensor(y[:, :, :], y[:, :, :], rb[:, :, :], ALU.add))
                    link(dve.tensor_reduce(top[:, :], y[:, :, :], AX_X, ALU.max))
                    dve.tensor_tensor(z[:, :, :], y[:, :, :], bc(top[:, :], 2, full), ALU.subtract).then_inc(z_ready, 1)
                    dve.wait_ge(exp_ready, g + 1)
                    dve.tensor_reduce(tot[:, :], e[:, :, :], AX_X, ALU.add).then_inc(tot_ready, 1)
                    dve.wait_ge(lse_ready, g + 1)
                    link(dve.tensor_tensor(y[:, :, :], z[:, :, :], bc(lse[:, :], 2, full), ALU.subtract))
                    dve.wait_ge(stored, 32 * g + 32)
                    dve.tensor_tensor(x1[:, :, :], xb[:, :, :], y[:, :, :], ALU.add).then_inc(x1_ready, 1)
                    dve.wait_ge(x1_ready, g + 1)
                    dve.sem_inc(x_used, 1)
                    dve.wait_ge(turned, g + 1)
                    norm.vector(dve, link, x1[:, :, :], hn[:, :, :], g).then_inc(hn_ready, 1)

            @block.tensor
            def _(pe):
                pe.sem_inc(turned, 1)
                pe.wait_ge(w_in, 32)
                with pe.Fori(0, NG) as g:
                    pe.wait_ge(hn_ready, g + 1)
                    pe.wait_ge(copied, g + 1)
                    for j in range(GB):
                        last = pe.transpose(ps[:, P * j:P * j + P], hn[:, j, :], t.ident[:, :])
                    last.then_inc(turned, 1)
                    pe.wait_ge(copied, g + 2)
                    pe.wait_ge(res_ready, g + 1)
                    for lo, hi in SPLIT:
                        last = pe.matmul(psw[:, lo:hi], ws[:, :], hT[:, lo:hi], start=True, stop=True)
                    last.then_inc(prod_ready, 1)

            @block.scalar
            def _(act):
                act.sem_inc(stored, 32)
                act.sem_inc(copied, 1)
                act.sem_inc(res_ready, 1)
                act.wait_ge(w_in, 32)
                with act.Fori(0, NG) as g:
                    act.wait_ge(z_ready, g + 1)
                    act.activation(e[:, :, :], z[:, :, :], ACT.Exp).then_inc(exp_ready, 1)
                    act.wait_ge(tot_ready, g + 1)
                    act.activation(lse[:, :], tot[:, :], ACT.Ln).then_inc(lse_ready, 1)
                    norm.scalar(act, g)
                    act.wait_ge(x1_ready, g + 1)
                    act.dma_start(rows_of_turn(t.x1_d, g), x1[:, :, :]).then_inc(stored, 16)
                    act.wait_ge(turned, g + 2)
                    act.activation(hT[:, :], ps[:, 0:GN], ACT.Copy).then_inc(copied, 1)
                    act.wait_ge(prod_ready, g + 1)
                    act.wait_ge(stored, 32 * g + 48)
                    act.activation(res[:, :], psw[:, 0:GN], ACT.Relu, bias=bs[:, 0:1]).then_inc(res_ready, 1)
                    act.wait_ge(res_ready, g + 2)
                    act.dma_start(t.hT_d[:, bass.ds(g * GN, GN)], res[:, :]).then_inc(stored, 16)
                act.wait_ge(stored, 32 * NG + 32)


SCALE = float(C) ** -0.5


def conv_project(nc, t, layer, a):
    with room(nc, f"project{layer}") as (sb, psum, sem):
        ws = sb("ws", [P, 4, D])
        bs = sb("bs", [P, 4, D])
        web = sb("web", [P, D])
        hT = sb("hT", [P, GN])
        kv = sb("kv", [P, GB, 2 * D])
        xr = sb("xr", [P, GB, D])
        qe = sb("qe", [P, GB, D])
        ps = psum("ps_proj", [P, GB, 512])
        w_in, h_in, proj_ready, q_ready, qe_ready, kv_ready, xr_ready, stored, chain_v, go_v = (
            sem(k) for k in ("w_in", "h_in", "proj_ready", "q_ready", "qe_ready", "kv_ready", "xr_ready", "stored", "chain_v", "go_v"))

        with nc.Block() as block:
            @block.sync
            def _(sp):
                for k, name in enumerate(("q", "k", "v", "skip")):
                    sp.dma_start(ws[:, k, :], a[f"L1_gnn_W{name}"][layer]).then_inc(w_in, 16)
                    sp.dma_start(bs[:, k, :], a[f"L1_gnn_b{name}"][layer].partition_broadcast(P)).then_inc(w_in, 16)
                sp.dma_start(web[:, :], a["L1_gnn_We"][layer].rearrange("a d -> (a d)").partition_broadcast(P)).then_inc(w_in, 16)
                with sp.Fori(0, NG) as g:
                    sp.wait_ge(proj_ready, g + 1)
                    sp.dma_start(hT[:, :], t.hT_d[:, bass.ds(g * GN, GN)]).then_inc(h_in, 16)

            @block.tensor
            def _(pe):
                pe.wait_ge(w_in, 16 * 9)
                pe.sem_inc(proj_ready, 1)
                with pe.Fori(0, NG) as g:
                    pe.wait_ge(h_in, 16 * g + 16)
                    pe.wait_ge(q_ready, g + 1)
                    pe.wait_ge(kv_ready, g + 1)
                    pe.wait_ge(xr_ready, g + 1)
                    for j in range(GB):
                        last = pe.matmul(ps[:, j, :], hT[:, P * j:P * j + P], ws[:, :, :].rearrange("k s o -> k (s o)"),
                                         start=True, stop=True)
                    last.then_inc(proj_ready, 1)

            @block.vector
            def _(dve):
                chain = Chain(dve, chain_v)
                for s in (q_ready, kv_ready, xr_ready):
                    dve.sem_inc(s, 1)
                dve.wait_ge(w_in, 16 * 9)
                chain.link(dve.tensor_scalar(bs[:, 0, :], bs[:, 0, :], SCALE, None, ALU.mult))
                with chain.turns(NG, 1) as g:
                    rows = t.qreg[:, bass.ds(g * (GB * QW), GB * QW)].rearrange("p (j w) -> p j w", w=QW)
                    dve.wait_ge(proj_ready, g + 2)
                    dve.wait_ge(stored, 32 * g + 32)
                    dve.tensor_tensor(kv[:, :, :], ps[:, :, D:3 * D],
                                      bc(bs[:, 1:3, :].rearrange("p k d -> p (k d)"), 1, [P, GB, 2 * D]), ALU.add).then_inc(kv_ready, 1)
                    dve.tensor_tensor(xr[:, :, :], ps[:, :, 3 * D:4 * D], bc(bs[:, 3, :], 1, [P, GB, D]), ALU.add).then_inc(xr_ready, 1)
                    dve.scalar_tensor_tensor(rows[:, :, 0:D], ps[:, :, 0:D], SCALE, bc(bs[:, 0, :], 1, [P, GB, D]),
                                             ALU.mult, ALU.add).then_inc(q_ready, 1)
                    dve.wait_ge(q_ready, g + 2)
                    chain.link(dve.tensor_tensor(qe[:, :, :], rows[:, :, 0:D], bc(web[:, :], 1, [P, GB, D]), ALU.mult))
                    dve.sem_inc(go_v, 1)
                    dve.tensor_reduce(rows[:, :, D:QW], qe[:, :, :].rearrange("p j (h c) -> p j h c", h=HEADS),
                                      AX_X, ALU.add).then_inc(qe_ready, 1)

            @block.scalar
            def _(act):
                act.sem_inc(stored, 32)
                with act.Fori(0, NG) as g:
                    act.wait_ge(kv_ready, g + 2)
                    act.dma_start(rows_of_turn(t.kv_d, g), kv[:, :, :]).then_inc(stored, 16)
                    act.wait_ge(xr_ready, g + 2)
                    act.dma_start(rows_of_turn(t.xr_d, g), xr[:, :, :]).then_inc(stored, 16)
                act.wait_ge(stored, 32 * NG + 32)


def chunk(g, half):
    return g * 2 + half, half, g


def conv_edges(nc, t, tag):
    with room(nc, tag) as (sb, psum, sem):
        HR = HEADS * CH
        kv = sb("kv", [P, RING, 2 * D])
        sel = sb("sel", [P, RING, P])
        selT = sb("selT", [P, 2, GR * P])
        src = sb("src", [P, 2, CH], I32)
        rec = sb("rec", [P, 2, RK * CH])
        blk = sb("blk", [1, 2, CH], I32)
        pen = sb("pen", [HR, 2, PW])
        stp = sb("stp", [HEADS, 2, CH, HK])
        prod = sb("prod", [P, 2, GR, D])
        score = sb("score", [P, HEADS, CH])
        qwe = sb("qwe", [P, HEADS, CH])
        fwd = sb("fwd", [HR, P])
        run = sb("run", [HR, P])
        top = sb("top", [HR, P])
        below = sb("below", [HR, P])
        expo = sb("expo", [HR, P])
        ends = sb("ends", [HR, 2, HEADS])
        fromleft = sb("fromleft", [HEADS, CH + 1])
        fromright = sb("fromright", [HEADS, CH + 1])
        sides = sb("sides", [HEADS, 2, CH])
        picked = sb("picked", [HR, 2, CH])
        side = sb("side", [HR, 2])
        newtop = sb("newtop", [HEADS, 1])
        drop = sb("drop", [HEADS, 1])
        fac = sb("fac", [HEADS, 1])
        facm = sb("facm", [HEADS, HEADS])
        node = sb("node", [HEADS, P])
        rescale = sb("rescale", [P, HEADS])
        pv = sb("pv", [P, CH, HEADS, C + 2])
        psT = psum("ps_selT", [P, GR * P])
        psQ = psum("ps_query", [P, 4, 512])
        psC = psum("ps_sums", [P, 2, 512])
        psM = psum("ps_small", [P, 512])
        rows = psM[0:HR, 0:P]
        psEnds = psM[0:HEADS, P:P + 2 * CH]
        psSides = psM[0:HR, 160:160 + 2 * CH]
        psFac = psM[:, 192:192 + HEADS]
        psExp = psM[:, 196:196 + HR]

        rec_in, blk_in, src_in = ([sem(f"{k}{h}") for h in range(2)] for k in ("rec_in", "blk_in", "src_in"))
        gathered = [sem(f"gathered{k}") for k in range(2 * KG)]
        ready, go_v, go_p, go_t, chain_v = (sem(k) for k in ("ready", "go_v", "go_p", "go_t", "chain_v"))
        scored, rec_used, blk_used = (sem(k) for k in ("scored", "rec_used", "blk_used"))
        sel_ready, selT_ready, selT_copied, q_ready, q_used = (
            sem(k) for k in ("sel_ready", "selT_ready", "selT_copied", "q_ready", "q_used"))
        rows_ready, ends_ready, ends_summed, sides_ready, sides_spread, drop_ready, fac_exp, fac_ready, fac_spread = (
            sem(k) for k in ("rows_ready", "ends_ready", "ends_summed", "sides_ready", "sides_spread", "drop_ready",
                             "fac_exp", "fac_ready", "fac_spread"))
        below_ready, expo_ready, expo_turned, pv_ready, sums_ready, ps_used = (
            sem(k) for k in ("below_ready", "expo_ready", "expo_turned", "pv_ready", "sums_ready", "ps_used"))

        def pipeline(eng, stages, chain=None, per=0):
            stages(chunk(0, 0), None)
            loop = chain.turns(PAIRS - 1, per) if chain else eng.Fori(0, PAIRS - 1)
            with loop as g:
                stages(chunk(g, 1), chunk(g, 0))
                stages(chunk(g + 1, 0), chunk(g, 1))
            stages(chunk(PAIRS - 1, 1), chunk(PAIRS - 1, 0))
            stages(None, chunk(PAIRS - 1, 1))

        with nc.Block() as block:
            @block.sync
            def _(sp):
                with sp.Fori(0, PAIRS) as g:
                    for h in range(2):
                        c = g * 2 + h
                        sp.wait_ge(scored, c + 1)
                        sp.dma_start(src[:, h, :], t.src_d[:, bass.ds(c, 1), :]).then_inc(src_in[h], 16)
                        sp.wait_ge(rec_used, c + 1)
                        sp.dma_start(rec[:, h, :], t.edge_d[:, bass.ds(c, 1), :]).then_inc(rec_in[h], 16)
                        for k in range(HEADS):
                            sp.dma_start(pen[CH * k:CH * k + CH, h, :], t.pen_d[bass.ds(c * CH, CH), :]).then_inc(rec_in[h], 16)
                        sp.dma_start(stp[:, h, :, :], t.step_d[bass.ds(c * CH, CH), :].partition_broadcast(HEADS)).then_inc(rec_in[h], 16)
                        sp.wait_ge(blk_used, c + 1)
                        sp.dma_start(blk[:, h, :], t.b_d[bass.ds(c, 1), :]).then_inc(blk_in[h], 16)

            @block.gpsimd
            def _(pool):
                with pool.Fori(0, PAIRS) as g:
                    for h in range(2):
                        c = g * 2 + h
                        pool.wait_ge(src_in[h], 16 * g + 16)
                        for k in range(KG):
                            pool.wait_ge(pv_ready, KG * c + k + 1)
                            pool.sem_inc(go_p, 1)
                            for i in range(GR):
                                j = k * GR + i
                                pool.indirect_dma_start(
                                    kv[:, h * CH + j, :], None, t.kv_d,
                                    bass.IndirectOffsetOnAxis(ap=src[:, h, j:j + 1], axis=0)).then_inc(gathered[h * KG + k], 16)

            @block.vector
            def _(dve):
                chain = Chain(dve, chain_v)
                link = chain.link
                regs = [dve.alloc_register(f"{tag}_sumblock{i}") for i in range(CH)]
                link(dve.memset(t.acc[:, :], 0.0))
                link(dve.memset(fromleft[:, :], -BIG))
                link(dve.memset(fromright[:, :], -BIG))
                for s, n in ((scored, 2), (rec_used, 2), (blk_used, 2), (pv_ready, 2 * KG), (q_used, 2), (ps_used, 1)):
                    dve.sem_inc(s, n)

                def select(a, k):
                    c, h, g = a
                    if k == 0:
                        dve.wait_ge(rec_in[h], 96 * g + 96)
                    dve.tensor_tensor(sel[:, h * CH + k * GR:h * CH + k * GR + GR, :],
                                      bc(t.iota[:, :], 1, [P, GR, P]),
                                      bc(rec[:, h, k * GR:k * GR + GR], 2, [P, GR, P]),
                                      ALU.is_equal).then_inc(sel_ready, 1)

                def scores(a, k):
                    c, h, g = a
                    lo = h * CH + k * GR
                    q = psQ[:, 2 * (k % 2):2 * (k % 2) + 2, 0:2 * QW].rearrange("p b (s w) -> p b s w", s=2)
                    dve.wait_ge(q_ready, KG * c + k + 1 + 2)
                    dve.wait_ge(gathered[h * KG + k], 16 * GR * g + 16 * GR)
                    link(dve.tensor_tensor(prod[:, k % 2, :, :].rearrange("p (b s) d -> p b s d", s=2), q[:, :, :, 0:D],
                                           kv[:, lo:lo + GR, 0:D].rearrange("p (b s) d -> p b s d", s=2), ALU.mult))
                    dve.tensor_reduce(score[:, :, k * GR:k * GR + GR].rearrange("p h i -> p i h"),
                                      prod[:, k % 2, :, :].rearrange("p i (h c) -> p i h c", h=HEADS), AX_X, ALU.add)
                    w = rec[:, h, CH + k * GR:CH + k * GR + GR].rearrange("p (b s) -> p b s", s=2)
                    dve.tensor_tensor(qwe[:, :, k * GR:k * GR + GR].rearrange("p h (b s) -> p b s h", s=2),
                                      q[:, :, :, D:QW], bc(w, 3, [P, 2, 2, HEADS]), ALU.mult).then_inc(q_used, 1)

                def maxima(a):
                    c, h, g = a
                    step = [stp[:, h, :, n] for n in range(HK)]
                    dve.wait_ge(q_used, KG * c + KG + 2)
                    link(dve.tensor_tensor(score[:, :, :], score[:, :, :], qwe[:, :, :], ALU.add))
                    dve.tensor_tensor(score[:, :, :], score[:, :, :],
                                      bc(rec[:, h, 2 * CH:3 * CH], 1, [P, HEADS, CH]), ALU.add).then_inc(scored, 1)
                    dve.wait_ge(rows_ready, c + 1)
                    link(dve.tensor_tensor_scan(fwd[:, :], pen[:, h, 0:P], rows, -BIG, ALU.add, ALU.max))
                    link(dve.tensor_tensor_scan(run[:, ::-1], pen[:, h, P:0:-1], fwd[:, ::-1], -BIG, ALU.add, ALU.max))
                    dve.tensor_scalar(ends[:, 0, :], t.hsel[:, :], run[:, P - 1:P], None, ALU.mult)
                    dve.tensor_scalar(ends[:, 1, :], t.hsel[:, :], run[:, 0:1], None, ALU.mult).then_inc(ends_ready, 1)
                    dve.wait_ge(ends_summed, c + 1)
                    link(dve.tensor_tensor_scan(fromleft[:, 1:CH + 1], step[1], psEnds[:, 0:CH], fromleft[:, 0:1],
                                                ALU.add, ALU.max))
                    link(dve.tensor_tensor_scan(fromright[:, CH - 1::-1], step[3][:, ::-1], psEnds[:, 2 * CH - 1:CH - 1:-1],
                                                -BIG, ALU.add, ALU.max))
                    dve.tensor_tensor(sides[:, 0, :], fromleft[:, 0:CH], step[0], ALU.add)
                    link(dve.tensor_tensor(sides[:, 1, :], fromright[:, 1:CH + 1], step[2], ALU.add))
                    dve.sem_inc(sides_ready, 1)
                    link(dve.tensor_tensor(newtop[:, :], fromright[:, 0:1], sides[:, 0, 0:1], ALU.max))
                    link(dve.tensor_tensor(drop[:, :], fromleft[:, 0:1], newtop[:, :], ALU.subtract))
                    dve.tensor_scalar(drop[:, :], drop[:, :], 0.0, None, ALU.min).then_inc(drop_ready, 1)
                    dve.tensor_copy(fromleft[:, 0:1], fromleft[:, CH:CH + 1])
                    dve.tensor_scalar(node[:, :], t.iota[0:HEADS, :], step[4][:, 0:1], None, ALU.is_equal)
                    dve.wait_ge(sides_spread, c + 1)
                    link(dve.tensor_tensor(picked[:, :, :], psSides.rearrange("p (s t) -> p s t", s=2),
                                           bc(t.tsel[:, :], 1, [HR, 2, CH]), ALU.mult))
                    link(dve.tensor_reduce(side[:, :], picked[:, :, :], AX_X, ALU.add))
                    link(dve.scalar_tensor_tensor(top[:, :], pen[:, h, P + 1:2 * P + 1], side[:, 0:1], run[:, :],
                                                  ALU.add, ALU.max))
                    link(dve.scalar_tensor_tensor(top[:, :], pen[:, h, 2 * P + 1:3 * P + 1], side[:, 1:2], top[:, :],
                                                  ALU.add, ALU.max))
                    dve.tensor_tensor(below[:, :], rows, top[:, :], ALU.subtract).then_inc(below_ready, 1)
                    dve.wait_ge(fac_exp, c + 1)
                    link(dve.tensor_scalar(fac[:, :], fac[:, :], -1.0, None, ALU.add))
                    dve.tensor_scalar(facm[:, :], t.ident[0:HEADS, 0:HEADS], fac[:, 0:1], None, ALU.mult).then_inc(fac_ready, 1)
                    dve.wait_ge(expo_turned, c + 1)
                    p = psExp.rearrange("p (h i) -> p i h", h=HEADS)
                    dve.tensor_copy(pv[:, :, :, C], p)
                    dve.tensor_tensor(pv[:, :, :, C + 1], p, bc(rec[:, h, CH:2 * CH], 2, [P, CH, HEADS]), ALU.mult)
                    dve.wait_ge(fac_spread, c + 1)
                    link(dve.tensor_scalar(rescale[:, :], psFac, 1.0, None, ALU.add))
                    dve.sem_inc(rec_used, 1)

                def weigh(b, k):
                    c, h, g = b
                    lo, j = h * CH + k * GR, k * GR
                    full = [P, GR, HEADS, C]
                    dve.tensor_tensor(pv[:, j:j + GR, :, 0:C],
                                      kv[:, lo:lo + GR, D:2 * D].rearrange("p i (h c) -> p i h c", h=HEADS),
                                      pv[:, j:j + GR, :, C:C + 1].to_broadcast(full), ALU.mult).then_inc(pv_ready, 1)

                def add(b, k, at):
                    c, h, g = b
                    if k == 0:
                        a = t.acc[:, bass.ds(at[0] * AW, AW)].rearrange("p (h w) -> p h w", h=HEADS)
                        link(dve.tensor_tensor(a, a, bc(rescale[:, :], 2, [P, HEADS, C + 2]), ALU.mult))
                    dve.wait_ge(sums_ready, KG * c + k + 1)
                    for i in range(GR):
                        a = t.acc[:, bass.ds(at[k * GR + i] * AW, AW)]
                        link(dve.tensor_tensor(a, a, psC[:, i // 2, (i % 2) * AW:(i % 2) * AW + AW], ALU.add))
                    dve.sem_inc(ps_used, 1)

                def stages(a, b):
                    if b is not None:
                        dve.wait_ge(blk_in[b[1]], 16 * b[2] + 16)
                        dve.sem_inc(go_v, 1)
                        dve.load(regs, blk[0:1, b[1], :])
                        at = [dve.snap(r, min_val=0, max_val=NB - 1) for r in regs]
                        dve.sem_inc(blk_used, 1)
                    for k in range(KG + 1):
                        if k < KG:
                            if a is not None:
                                select(a, k)
                            if b is not None:
                                weigh(b, k)
                        if k > 0:
                            if b is not None:
                                add(b, k - 1, at)
                            if a is not None:
                                scores(a, k - 1)
                    if a is not None:
                        maxima(a)

                pipeline(dve, stages, chain, 2 * (KG + 1 + CH + 14))

            @block.tensor
            def _(pe):
                pe.sem_inc(q_ready, 2)
                regs = [pe.alloc_register(f"{tag}_queryblock{i}") for i in range(CH)]

                def stages(a, b):
                    if a is not None:
                        c, h, g = a
                        pe.wait_ge(blk_in[h], 16 * g + 16)
                        pe.sem_inc(go_t, 1)
                        pe.load(regs, blk[0:1, h, :])
                        at = [pe.snap(r, min_val=0, max_val=NB - 1) for r in regs]
                    for k in range(KG):
                        if a is not None:
                            pe.wait_ge(sel_ready, KG * c + k + 1)
                            if k > 0 or b is not None:
                                pe.wait_ge(selT_copied, KG * c + k)
                            for i in range(GR):
                                last = pe.transpose(psT[:, P * i:P * i + P], sel[:, h * CH + k * GR + i, :], t.ident[:, :])
                            last.then_inc(selT_ready, 1)
                        if b is not None:
                            cb, hb, gb = b
                            pe.wait_ge(pv_ready, KG * cb + k + 1 + 2 * KG)
                            pe.wait_ge(ps_used, KG * cb + k + 1)
                            for i in range(GR):
                                j = k * GR + i
                                last = pe.matmul(psC[:, i // 2, (i % 2) * AW:(i % 2) * AW + AW], sel[:, hb * CH + j, :],
                                                 pv[:, j, :, :].rearrange("p h w -> p (h w)"), start=True, stop=True)
                            last.then_inc(sums_ready, 1)
                        if a is not None:
                            pe.wait_ge(selT_copied, KG * c + k + 1)
                            pe.wait_ge(q_used, KG * c + k + 1)
                            for i in range(GR):
                                last = pe.matmul(psQ[:, 2 * (k % 2) + i // 2, (i % 2) * QW:(i % 2) * QW + QW],
                                                 selT[:, k % 2, P * i:P * i + P],
                                                 t.qreg[:, bass.ds(at[k * GR + i] * QW, QW)], start=True, stop=True)
                            last.then_inc(q_ready, 1)
                    if a is None:
                        return
                    pe.wait_ge(scored, c + 1 + 2)
                    pe.sem_inc(go_t, 1)
                    pe.transpose(rows, score[:, :, :].rearrange("p h t -> p (h t)"), t.ident[:, :]).then_inc(rows_ready, 1)
                    pe.wait_ge(ends_ready, c + 1)
                    pe.sem_inc(go_t, 1)
                    pe.matmul(psEnds[:, 0:CH], ends[:, 0, :], t.tsel[:, :], start=True, stop=True)
                    pe.matmul(psEnds[:, CH:2 * CH], ends[:, 1, :], t.tsel[:, :], start=True, stop=True).then_inc(ends_summed, 1)
                    pe.wait_ge(sides_ready, c + 1)
                    pe.sem_inc(go_t, 1)
                    pe.matmul(psSides, t.hselT[:, :], sides[:, :, :].rearrange("p s t -> p (s t)"),
                              start=True, stop=True).then_inc(sides_spread, 1)
                    pe.wait_ge(fac_ready, c + 1)
                    pe.sem_inc(go_t, 1)
                    pe.matmul(psFac, node[:, :], facm[:, :], start=True, stop=True).then_inc(fac_spread, 1)
                    pe.wait_ge(expo_ready, c + 1)
                    pe.sem_inc(go_t, 1)
                    pe.transpose(psExp, expo[:, :], t.ident[0:HR, 0:HR]).then_inc(expo_turned, 1)

                pipeline(pe, stages)

            @block.scalar
            def _(act):
                def stages(a, b):
                    if a is None:
                        return
                    c, h, g = a
                    for k in range(KG):
                        act.wait_ge(selT_ready, KG * c + k + 1)
                        act.wait_ge(q_ready, KG * c + k + 1)
                        act.activation(selT[:, k % 2, :], psT[:, :], ACT.Copy).then_inc(selT_copied, 1)
                    act.wait_ge(drop_ready, c + 1)
                    act.activation(fac[:, :], drop[:, :], ACT.Exp).then_inc(fac_exp, 1)
                    act.wait_ge(below_ready, c + 1)
                    act.activation(expo[:, :], below[:, :], ACT.Exp).then_inc(expo_ready, 1)

                pipeline(act, stages)


def conv_combine(nc, t, layer, a):
    with room(nc, f"combine{layer}") as (sb, psum, sem):
        web = sb("web", [P, D])
        wbeta = sb("wbeta", [P, 3, D])
        xr = sb("xr", [P, GB, D])
        rden = sb("rden", [P, GB, HEADS])
        out = sb("out", [P, GB, HEADS, C])
        dif = sb("dif", [P, GB, D])
        part = sb("part", [P, GB, D])
        part2 = sb("part2", [P, GB, D])
        logit = sb("logit", [P, GB])
        gate = sb("gate", [P, GB])
        mix = sb("mix", [P, GB, D])
        ps = psum("ps_turn", [P, 1024])
        w_in, x_in, x_used, logit_ready, gate_ready, mix_ready, turned, copied, chain_v, go_v = (
            sem(k) for k in ("w_in", "x_in", "x_used", "logit_ready", "gate_ready", "mix_ready", "turned", "copied", "chain_v", "go_v"))
        full = [P, GB, D]
        full4 = [P, GB, HEADS, C]

        with nc.Block() as block:
            @block.sync
            def _(sp):
                sp.dma_start(web[:, :], a["L1_gnn_We"][layer].rearrange("a d -> (a d)").partition_broadcast(P)).then_inc(w_in, 16)
                sp.dma_start(wbeta[:, :, :].rearrange("p k d -> p (k d)"),
                             a["L1_gnn_Wbeta"][layer].rearrange("d a -> (d a)").partition_broadcast(P)).then_inc(w_in, 16)
                with sp.Fori(0, NG) as g:
                    sp.wait_ge(x_used, g + 1)
                    sp.dma_start(xr[:, :, :], rows_of_turn(t.xr_d, g)).then_inc(x_in, 16)

            @block.vector
            def _(dve):
                chain = Chain(dve, chain_v)
                link = chain.link
                dve.wait_ge(w_in, 32)
                dve.sem_inc(x_used, 1)
                with chain.turns(NG, 13) as g:
                    s = sums_of_turn(t, g, AW).rearrange("p j (h w) -> p j h w", h=HEADS)
                    flat = out[:, :, :, :].rearrange("p j h c -> p j (h c)")
                    link(dve.tensor_scalar(rden[:, :, :], s[:, :, :, C], 1e-20, None, ALU.max))
                    link(dve.reciprocal(rden[:, :, :], rden[:, :, :]))
                    link(dve.tensor_tensor(out[:, :, :, :], s[:, :, :, C + 1:C + 2].to_broadcast(full4),
                                           bc(web[:, :].rearrange("p (h c) -> p h c", h=HEADS), 1, full4), ALU.mult))
                    link(dve.tensor_tensor(out[:, :, :, :], out[:, :, :, :], s[:, :, :, 0:C], ALU.add))
                    link(dve.tensor_tensor(out[:, :, :, :], out[:, :, :, :], bc(rden[:, :, :], 3, full4), ALU.mult))
                    dve.wait_ge(x_in, 16 * g + 16)
                    link(dve.tensor_tensor(dif[:, :, :], flat, xr[:, :, :], ALU.subtract))
                    link(dve.tensor_tensor(part[:, :, :], flat, bc(wbeta[:, 0, :], 1, full), ALU.mult))
                    link(dve.tensor_tensor(part2[:, :, :], xr[:, :, :], bc(wbeta[:, 1, :], 1, full), ALU.mult))
                    dve.sem_inc(x_used, 1)
                    link(dve.tensor_tensor(part[:, :, :], part[:, :, :], part2[:, :, :], ALU.add))
                    link(dve.tensor_tensor(part2[:, :, :], dif[:, :, :], bc(wbeta[:, 2, :], 1, full), ALU.mult))
                    link(dve.tensor_tensor(part[:, :, :], part[:, :, :], part2[:, :, :], ALU.add))
                    dve.tensor_reduce(logit[:, :], part[:, :, :], AX_X, ALU.add).then_inc(logit_ready, 1)
                    dve.wait_ge(gate_ready, g + 1)
                    link(dve.tensor_tensor(part2[:, :, :], dif[:, :, :], bc(gate[:, :], 2, full), ALU.mult))
                    dve.wait_ge(turned, g + 1)
                    link(dve.tensor_tensor(mix[:, :, :], flat, part2[:, :, :], ALU.subtract))
                    dve.sem_inc(mix_ready, 1)

            @block.tensor
            def _(pe):
                pe.sem_inc(turned, 1)
                with pe.Fori(0, NG) as g:
                    pe.wait_ge(mix_ready, g + 1)
                    pe.wait_ge(copied, g + 1)
                    for j in range(GB):
                        last = pe.transpose(ps[:, P * j:P * j + P], mix[:, j, :], t.ident[:, :])
                    last.then_inc(turned, 1)

            @block.scalar
            def _(act):
                act.sem_inc(copied, 1)
                with act.Fori(0, NG) as g:
                    act.wait_ge(logit_ready, g + 1)
                    act.activation(gate[:, :], logit[:, :], ACT.Sigmoid).then_inc(gate_ready, 1)
                    act.wait_ge(turned, g + 2)
                    act.activation(t.qreg[:, bass.ds(g * GN, GN)], ps[:, 0:GN], ACT.Copy).then_inc(copied, 1)


STAT = 500
assert N % STAT == 0


def conv_norm(nc, t, layer, a, out):
    final = layer == LAYERS - 1
    with room(nc, f"batch_norm{layer}") as (sb, psum, sem):
        gamma = sb("gamma", [P, 1])
        beta = sb("beta", [P, 1])
        stats = sb("stats", [P, N // STAT, 6])
        mv = sb("mv", [P, 2])
        var = sb("var", [P, 1])
        std = sb("std", [P, 1])
        mul = sb("mul", [P, 1])
        hT = sb("hT", [P, GN])
        x1 = sb("x1", [P, GB, D])
        cen = sb("cen", [P, GN])
        rel = sb("rel", [P, GN])
        new = sb("new", [P, GN])
        res = sb("res", [P, GB, D])
        ps = psum("ps_turn", [P, 1024])
        w_in, x_in, x_used, var_ready, std_ready, cen_ready, rel_ready, new_ready, turned, res_ready, stored, chain_v = (
            sem(k) for k in ("w_in", "x_in", "x_used", "var_ready", "std_ready", "cen_ready", "rel_ready", "new_ready",
                             "turned", "res_ready", "stored", "chain_v"))

        with nc.Block() as block:
            @block.sync
            def _(sp):
                sp.dma_start(gamma[:, :], a["L1_gnn_bn_gamma"][layer].rearrange("(d a) -> d a", a=1)).then_inc(w_in, 16)
                sp.dma_start(beta[:, :], a["L1_gnn_bn_beta"][layer].rearrange("(d a) -> d a", a=1)).then_inc(w_in, 16)
                with sp.Fori(0, NG) as g:
                    sp.wait_ge(x_used, g + 1)
                    sp.dma_start(hT[:, :], t.hT_d[:, bass.ds(g * GN, GN)]).then_inc(x_in, 16)
                    if final:
                        sp.dma_start(x1[:, :, :], rows_of_turn(t.x1_d, g)).then_inc(x_in, 16)

            @block.vector
            def _(dve):
                chain = Chain(dve, chain_v)
                link = chain.link
                dve.sem_inc(x_used, 1)
                dve.sem_inc(new_ready, 1)
                for j in range(N // STAT):
                    last = dve.bn_stats(stats[:, j, :], t.qreg[:, STAT * j:STAT * j + STAT])
                link(last)
                link(dve.bn_aggr(mv[:, :], stats[:, :, :].rearrange("p a b -> p (a b)")))
                dve.tensor_scalar(var[:, :], mv[:, 1:2], EPS, None, ALU.add).then_inc(var_ready, 1)
                dve.wait_ge(std_ready, 1)
                dve.wait_ge(w_in, 32)
                link(dve.reciprocal(mul[:, :], std[:, :]))
                link(dve.tensor_tensor(mul[:, :], mul[:, :], gamma[:, :], ALU.mult))
                with dve.Fori(0, NG) as g:
                    dve.wait_ge(rel_ready, g + 1)
                    dve.tensor_scalar(cen[:, :], t.qreg[:, bass.ds(g * GN, GN)], mv[:, 0:1], mul[:, 0:1],
                                      ALU.subtract, ALU.mult).then_inc(cen_ready, 1)
                    dve.wait_ge(rel_ready, g + 2)
                    dve.wait_ge(x_in, (32 if final else 16) * g + (32 if final else 16))
                    if final:
                        dve.wait_ge(turned, g + 1)
                    else:
                        dve.wait_ge(stored, 16 * g + 16)
                    dve.tensor_tensor(new[:, :], rel[:, :], hT[:, :], ALU.add).then_inc(new_ready, 1)
                    if final:
                        dve.wait_ge(turned, g + 2)
                        dve.wait_ge(stored, 16 * g + 16)
                        dve.tensor_tensor(res[:, :, :], x1[:, :, :], ps[:, 0:GN].rearrange("p (j d) -> p j d", j=GB),
                                          ALU.add).then_inc(res_ready, 1)
                        dve.wait_ge(res_ready, g + 1)
                    else:
                        dve.wait_ge(new_ready, g + 2)
                    dve.sem_inc(x_used, 1)

            @block.tensor
            def _(pe):
                if final:
                    pe.sem_inc(turned, 1)
                    with pe.Fori(0, NG) as g:
                        pe.wait_ge(new_ready, g + 2)
                        pe.wait_ge(x_used, g + 1)
                        for j in range(GB):
                            last = pe.transpose(ps[:, P * j:P * j + P], new[:, P * j:P * j + P], t.ident[:, :])
                        last.then_inc(turned, 1)

            @block.scalar
            def _(act):
                act.sem_inc(stored, 16)
                act.sem_inc(rel_ready, 1)
                act.wait_ge(var_ready, 1)
                act.activation(std[:, :], var[:, :], ACT.Sqrt).then_inc(std_ready, 1)
                act.wait_ge(w_in, 32)
                with act.Fori(0, NG) as g:
                    act.wait_ge(cen_ready, g + 1)
                    act.wait_ge(new_ready, g + 1)
                    act.activation(rel[:, :], cen[:, :], ACT.Relu, bias=beta[:, 0:1]).then_inc(rel_ready, 1)
                    if final:
                        act.wait_ge(res_ready, g + 1)
                        act.dma_start(rows_of_turn(out, g), res[:, :, :]).then_inc(stored, 16)
                    else:
                        act.wait_ge(new_ready, g + 2)
                        act.dma_start(t.hT_d[:, bass.ds(g * GN, GN)], new[:, :]).then_inc(stored, 16)
                act.wait_ge(stored, 16 * NG + 16)


_IN = ["x", "src", "dst", "edge_weight1", "L0_gnn_W1", "L0_gnn_b1", "L0_gnn_W2", "L0_gnn_b2", "L1_gnn_W_in",
       "L1_gnn_b_in", "L1_gnn_Wq", "L1_gnn_bq", "L1_gnn_Wk", "L1_gnn_bk", "L1_gnn_Wv", "L1_gnn_bv", "L1_gnn_We",
       "L1_gnn_Wskip", "L1_gnn_bskip", "L1_gnn_Wbeta", "L1_gnn_bn_gamma", "L1_gnn_bn_beta"]


def lay_out(inputs):
    import numpy as np

    a = {name: np.ascontiguousarray(np.asarray(inputs[name])) for name in _IN}
    x = np.zeros((NP, D), a["x"].dtype)
    x[:N] = a["x"]
    src = np.zeros((STEPS * P,), a["src"].dtype)
    src[:E] = a["src"]
    dst = np.full((STEPS * P,), NP - 1, a["dst"].dtype)
    dst[:E] = a["dst"]
    wgt = np.zeros((STEPS * P,), a["edge_weight1"].dtype)
    wgt[:E] = a["edge_weight1"].reshape(-1)
    a.update(x=x, src=src, dst=dst, edge_weight1=wgt)
    return a


def program(nc, a, out):
    t = Tables()
    with ExitStack() as ctx:
        declare(nc, t, ctx)
        setup_phase(nc, t, a["src"], a["dst"], a["edge_weight1"])
        declare_sums(nc, t, ctx)
        norm_phase(nc, t, a["x"])
        sage_edges(nc, t, t.h_d, "first")
        sage_dense(nc, t, a["L0_gnn_W1"], a["L0_gnn_b1"], a["L0_gnn_W2"], a["L0_gnn_b2"])
        sage_edges(nc, t, t.p_d, "second")
        sage_output(nc, t, a["x"], a["L1_gnn_W_in"], a["L1_gnn_b_in"])
        for layer in range(LAYERS):
            conv_project(nc, t, layer, a)
            conv_edges(nc, t, f"conv{layer}")
            conv_combine(nc, t, layer, a)
            conv_norm(nc, t, layer, a, out)


def kernel(**inputs):
    import numpy as np
    import concourse.bacc as bacc
    from concourse.bass_utils import run_bass_kernel_spmd

    a = lay_out(inputs)
    nc = bacc.Bacc("TRN2", target_bir_lowering=False, num_devices=1)
    aps = {name: nc.dram_tensor(f"in_{name}", v.shape, mybir.dt.from_np(v.dtype), kind="ExternalInput").ap()
           for name, v in a.items()}
    out = nc.dram_tensor("out", [NP, D], F32, kind="ExternalOutput").ap()
    program(nc, aps, out)
    r = run_bass_kernel_spmd(nc, [{f"in_{name}": v for name, v in a.items()}], core_ids=[0])
    return np.asarray(r.results[0]["out"])[:N]
```

```python
from contextlib import ExitStack, contextmanager

import concourse.bass as bass
from concourse import mybir

ALU = mybir.AluOpType
ACT = mybir.ActivationFunctionType
AX_X = mybir.AxisListType.X
F32 = mybir.dt.float32
I32 = mybir.dt.int32

P = 128
N = 12500
E = 200000
D = 128
HID = 256
HEADS = 4
C = D // HEADS
LAYERS = 2
EPS = 1e-5
BIG = 1e30

NB = -(-N // P)
NP = NB * P
CH = 16
GR = 4
KG = CH // GR
STEPS = -(-(-(-E // P) + NB - 1) // (P)) * P
STEPS = STEPS if STEPS % (2 * CH) == 0 else STEPS + CH
NC_ = STEPS // CH
PAIRS = NC_ // 2
SJ = STEPS // P
GB = 7
NG = NB // GB
GN = GB * P
QW = D + HEADS
AW = HEADS * (C + 2)
MW = D + 1
RING = 2 * CH
PW = 3 * P + 4
RK = 3
HK = 5
assert NB % GB == 0 and NC_ % 2 == 0 and SJ * P == STEPS


class Chain:

    def __init__(self, eng, sem):
        self.eng, self.sem, self.base, self.n = eng, sem, 0, 0

    def link(self, ins):
        self.n += 1
        ins.then_inc(self.sem, 1)
        self.eng.wait_ge(self.sem, self.base + self.n)

    def mark(self, ins):
        self.n += 1
        ins.then_inc(self.sem, 1)
        return self.n

    def need(self, mark):
        self.eng.wait_ge(self.sem, self.base + mark)

    @contextmanager
    def turns(self, count, per):
        start = self.base + self.n
        with self.eng.Fori(0, count) as i:
            self.base, self.n = start + i * per, 0
            yield i
            assert self.n == per, (self.n, per)
        self.base, self.n = start + count * per, 0


@contextmanager
def room(nc, phase):
    with ExitStack() as ctx:
        def sb(name, shape, dt=F32):
            return ctx.enter_context(nc.sbuf_tensor(f"{phase}_{name}", shape, dt))

        def psum(name, shape):
            return ctx.enter_context(nc.psum_tensor(f"{phase}_{name}", shape, F32))

        sems = []

        def sem(name):
            sems.append(nc.alloc_semaphore(f"{phase}_{name}"))
            return sems[-1]

        yield sb, psum, sem
    nc.clear_and_free_semaphores(sems)
    nc.all_engine_barrier()


class Tables:
    pass


def bc(ap, dim, shape):
    return ap.unsqueeze(dim).to_broadcast(shape)


def declare(nc, t, ctx):
    def dram(name, shape, dt=F32):
        return nc.dram_tensor(name, shape, dt, kind="Internal").ap()

    def sb(name, shape, dt=F32):
        return ctx.enter_context(nc.sbuf_tensor(name, shape, dt))

    t.f_d = dram("finish_steps", [STEPS])
    t.t_d = dram("tile_of_step", [STEPS + 2], I32)
    t.b_d = dram("block_of_step", [NC_, CH], I32)
    t.edge_d = dram("edge_records", [P, NC_, RK * CH])
    t.src_d = dram("source_records", [P, NC_, CH], I32)
    t.step_d = dram("step_records", [STEPS, HK])
    t.place_d = dram("place_rows", [NC_, CH * P])
    t.pen_d = dram("run_penalties", [STEPS, PW])
    t.h_d = dram("sage_in", [NP, D])
    t.p_d = dram("sage_hidden_projected", [NP, D])
    t.r_d = dram("sage_own_part", [NP, D])
    t.x1_d = dram("x_after_sage", [NP, D])
    t.hT_d = dram("conv_in_transposed", [P, NP])
    t.kv_d = dram("key_value", [NP, 2 * D])
    t.xr_d = dram("conv_skip", [NP, D])
    t.inv = sb("inverse_degree", [P, NB])
    t.iota = sb("iota_row", [P, P])
    t.ident = sb("identity", [P, P])
    t.minus = sb("minus_partition", [P, 1])
    t.hselT = sb("head_rows", [HEADS, HEADS * CH])
    t.hsel = sb("head_of_row", [HEADS * CH, HEADS])
    t.tsel = sb("step_of_row", [HEADS * CH, CH])


def declare_sums(nc, t, ctx):
    t.acc = ctx.enter_context(nc.sbuf_tensor("sums", [P, NB * AW], F32))
    t.qreg = ctx.enter_context(nc.sbuf_tensor("query_table", [P, NB * QW], F32))


def setup_phase(nc, t, src, dst, wgt):
    with room(nc, "setup") as (sb, psum, sem):
        dlast = sb("dlast", [P, SJ], I32)
        blast = sb("blast", [P, SJ], I32)
        blastf = sb("blastf", [P, SJ])
        fin = sb("fin", [P, SJ])
        sval = sb("sval", [P, SJ])
        part = sb("part", [P, 1])
        hv = sb("hv", [HEADS, HEADS * CH])
        hv1 = sb("hv1", [HEADS, HEADS * CH])
        fbc = sb("fbc", [P, STEPS])
        below = sb("below", [P, STEPS])
        tf = sb("tf", [P, SJ])
        ti = sb("ti", [P, SJ], I32)
        tpi = sb("tpi", [P, SJ], I32)
        tni = sb("tni", [P, SJ], I32)
        bf = sb("bf", [P, SJ])
        bi = sb("bi", [P, SJ], I32)
        b128 = sb("b128", [P, SJ])
        rows = {k: sb(f"rows_{k}", [P, SJ, P], I32) for k in ("dst", "prev", "next", "src")}
        wrow = sb("wrow", [P, SJ, P])
        df = sb("df", [P, SJ, P])
        sf = sb("sf", [P, SJ, P])
        rel = sb("rel", [P, SJ, P])
        dead = sb("dead", [P, SJ, P])
        inblk = sb("inblk", [P, SJ, P])
        pen = sb("pen", [P, SJ, PW])
        prevf = sb("prevf", [P, SJ])
        nextf = sb("nextf", [P, SJ])
        contl = sb("contl", [P, SJ])
        contr = sb("contr", [P, SJ])
        one = sb("one", [P, SJ])
        both = sb("both", [P, SJ])
        srec = sb("srec", [P, SJ, HK])
        erec = sb("erec", [P, NC_, RK * CH])
        srec_i = sb("srec_i", [P, NC_, CH], I32)
        ps = psum("ps_turn", [P, 4, 512])

        iotas = sem("iotas")
        consts = sem("consts")
        dlast_in = sem("dlast_in")
        fin_ready = sem("fin_ready")
        fin_out = sem("fin_out")
        fbc_in = sem("fbc_in")
        steps_ready = sem("steps_ready")
        steps_out = sem("steps_out")
        near_in = sem("near_in")
        rows_in = sem("rows_in")
        chain_v = sem("chain_v")
        recs_ready = sem("recs_ready")
        turned = sem("turned")
        copied = sem("copied")
        tables_out = sem("tables_out")
        dst_rows = dst.rearrange("(t e) -> t e", e=P)
        src_rows = src.rearrange("(t e) -> t e", e=P)
        wgt_rows = wgt.rearrange("(t e) -> t e", e=P)

        with nc.Block() as block:
            @block.sync
            def _(sp):
                with nc.allow_non_contiguous_dma("small tables"):
                    sp.dma_start(dlast[:, :], dst_rows[:, P - 1:P].rearrange("(j p) o -> p (j o)", p=P),
                                 allow_slow_non_contiguous=True).then_inc(dlast_in, 16)
                    sp.wait_ge(fin_ready, 1)
                    sp.dma_start(t.f_d.rearrange("(j p) -> p j", p=P), fin[:, :],
                                 allow_slow_non_contiguous=True).then_inc(fin_out, 16)
                    sp.wait_ge(fin_out, 16)
                    sp.dma_start(fbc[:, :], t.f_d.partition_broadcast(P)).then_inc(fbc_in, 16)
                    sp.wait_ge(steps_ready, 1)
                    sp.dma_start(t.t_d[1:STEPS + 1].rearrange("(j p) -> p j", p=P), ti[:, :],
                                 allow_slow_non_contiguous=True).then_inc(steps_out, 16)
                    sp.dma_start(t.t_d[0:1].rearrange("(a b) -> a b", a=1), ti[0:1, 0:1]).then_inc(steps_out, 16)
                    sp.dma_start(t.t_d[STEPS + 1:STEPS + 2].rearrange("(a b) -> a b", a=1),
                                 ti[P - 1:P, SJ - 1:SJ]).then_inc(steps_out, 16)
                    sp.dma_start(t.b_d.rearrange("(j a) b -> (a b) j", a=P // CH), bi[:, :],
                                 allow_slow_non_contiguous=True).then_inc(steps_out, 16)
                    sp.wait_ge(steps_out, 64)
                    sp.dma_start(tpi[:, :], t.t_d[0:STEPS].rearrange("(j p) -> p j", p=P),
                                 allow_slow_non_contiguous=True).then_inc(near_in, 16)
                    sp.dma_start(tni[:, :], t.t_d[2:STEPS + 2].rearrange("(j p) -> p j", p=P),
                                 allow_slow_non_contiguous=True).then_inc(near_in, 16)
                    sp.wait_ge(recs_ready, 1)
                    sp.dma_start(t.pen_d.rearrange("(j p) w -> p j w", p=P), pen[:, :, :]).then_inc(tables_out, 16)
                    sp.dma_start(t.step_d.rearrange("(j p) w -> p j w", p=P), srec[:, :, :],
                                 allow_slow_non_contiguous=True).then_inc(tables_out, 16)
                    sp.dma_start(t.place_d.rearrange("(j a) (b e) -> (a b) j e", a=P // CH, e=P), rel[:, :, :]).then_inc(tables_out, 16)
                    sp.wait_ge(copied, SJ)
                    sp.dma_start(t.edge_d, erec[:, :, :]).then_inc(tables_out, 16)
                    sp.dma_start(t.src_d, srec_i[:, :, :]).then_inc(tables_out, 16)
                    sp.wait_ge(tables_out, 80)

            @block.gpsimd
            def _(pool):
                pool.iota(t.iota[:, :], [[1, P]], 0, 0, allow_small_or_imprecise_dtypes=True).then_inc(iotas, 1)
                pool.iota(part[:, :], [[0, 1]], 0, 1, allow_small_or_imprecise_dtypes=True).then_inc(iotas, 1)
                pool.iota(sval[:, :], [[P, SJ]], 0, 1, allow_small_or_imprecise_dtypes=True).then_inc(iotas, 1)
                pool.iota(hv[:, :], [[1, HEADS * CH]], 0, -CH, allow_small_or_imprecise_dtypes=True).then_inc(iotas, 1)
                pool.wait_ge(steps_ready, 1)

                def gather(out, table, index, j):
                    pool.indirect_dma_start(out[:, j, :], None, table,
                                            bass.IndirectOffsetOnAxis(ap=index[:, j:j + 1], axis=0)).then_inc(rows_in, 16)

                for j in range(SJ):
                    gather(rows["dst"], dst_rows, ti, j)
                    gather(rows["src"], src_rows, ti, j)
                    gather(wrow, wgt_rows, ti, j)
                pool.wait_ge(near_in, 32)
                for j in range(SJ):
                    gather(rows["prev"], dst_rows, tpi, j)
                    gather(rows["next"], dst_rows, tni, j)

            @block.vector
            def _(dve):
                link = Chain(dve, chain_v).link
                dve.wait_ge(iotas, 4)
                link(dve.tensor_scalar(t.ident[:, :], t.iota[:, :], part[:, 0:1], None, ALU.is_equal))
                link(dve.tensor_scalar(t.minus[:, :], part[:, 0:1], -1.0, None, ALU.mult))
                link(dve.tensor_scalar(hv1[:, :], hv[:, :], 0.0, None, ALU.is_ge))
                link(dve.scalar_tensor_tensor(t.hselT[:, :], hv[:, :], CH - 1.0, hv1[:, :], ALU.is_le, ALU.mult))
                corner = t.ident[0:HEADS * CH, 0:HEADS * CH]
                dve.tensor_reduce(t.hsel[:, :], corner.rearrange("p (h t) -> p h t", h=HEADS), AX_X, ALU.add)
                dve.tensor_reduce(t.tsel[:, :], corner.rearrange("p (h t) -> p t h", h=HEADS), AX_X, ALU.add)
                dve.wait_ge(dlast_in, 16)
                link(dve.tensor_scalar(blast[:, :], dlast[:, :], 7, None, ALU.arith_shift_right))
                link(dve.tensor_copy(blastf[:, :], blast[:, :]))
                dve.tensor_tensor(fin[:, :], blastf[:, :], sval[:, :], ALU.add).then_inc(fin_ready, 1)
                dve.wait_ge(fbc_in, 16)
                for j in range(SJ):
                    link(dve.tensor_scalar(below[:, :], fbc[:, :], sval[:, j:j + 1], 0.0, ALU.is_lt, ALU.add,
                                           accum_out=tf[:, j:j + 1]))
                link(dve.tensor_tensor(bf[:, :], sval[:, :], tf[:, :], ALU.subtract))
                link(dve.tensor_copy(ti[:, :], tf[:, :]))
                link(dve.tensor_scalar(b128[:, :], bf[:, :], float(P), None, ALU.mult))
                dve.tensor_copy(bi[:, :], bf[:, :]).then_inc(steps_ready, 1)
                dve.wait_ge(rows_in, 16 * 5 * SJ)
                link(dve.tensor_copy(df[:, :, :], rows["dst"][:, :, :]))
                link(dve.tensor_copy(sf[:, :, :], rows["src"][:, :, :]))
                full = [P, SJ, P]
                link(dve.tensor_tensor(rel[:, :, :], df[:, :, :], bc(b128[:, :], 2, full), ALU.subtract))
                link(dve.tensor_scalar(inblk[:, :, :], rel[:, :, :], 0.0, None, ALU.is_ge))
                link(dve.scalar_tensor_tensor(inblk[:, :, :], rel[:, :, :], P - 1.0, inblk[:, :, :],
                                              ALU.is_le, ALU.mult))
                link(dve.tensor_scalar(dead[:, :, :], inblk[:, :, :], -1.0, BIG, ALU.add, ALU.mult))
                link(dve.memset(pen[:, :, :], 0.0))
                link(dve.tensor_tensor(pen[:, :, 1:P], df[:, :, 1:P], df[:, :, 0:P - 1], ALU.is_equal))
                link(dve.tensor_tensor(pen[:, :, P + 1:2 * P + 1], df[:, :, :],
                                       df[:, :, 0:1].to_broadcast(full), ALU.is_equal))
                link(dve.tensor_tensor(pen[:, :, 2 * P + 1:3 * P + 1], df[:, :, :],
                                       df[:, :, P - 1:P].to_broadcast(full), ALU.is_equal))
                link(dve.tensor_scalar(pen[:, :, :], pen[:, :, :], -1.0, BIG, ALU.add, ALU.mult))
                link(dve.tensor_copy(prevf[:, :], rows["prev"][:, :, P - 1]))
                link(dve.tensor_copy(nextf[:, :], rows["next"][:, :, 0]))
                link(dve.tensor_tensor(contl[:, :], prevf[:, :], df[:, :, 0], ALU.is_equal))
                link(dve.tensor_tensor(contr[:, :], nextf[:, :], df[:, :, P - 1], ALU.is_equal))
                link(dve.tensor_tensor(one[:, :], df[:, :, 0], df[:, :, P - 1], ALU.is_equal))
                link(dve.tensor_scalar(srec[:, :, 0], contl[:, :], -1.0, BIG, ALU.add, ALU.mult))
                link(dve.tensor_tensor(both[:, :], contl[:, :], one[:, :], ALU.mult))
                link(dve.tensor_scalar(srec[:, :, 1], both[:, :], -1.0, BIG, ALU.add, ALU.mult))
                link(dve.tensor_scalar(srec[:, :, 2], contr[:, :], -1.0, BIG, ALU.add, ALU.mult))
                link(dve.tensor_tensor(both[:, :], contr[:, :], one[:, :], ALU.mult))
                link(dve.tensor_scalar(srec[:, :, 3], both[:, :], -1.0, BIG, ALU.add, ALU.mult))
                dve.tensor_copy(srec[:, :, 4], rel[:, :, 0]).then_inc(recs_ready, 1)

            @block.tensor
            def _(pe):
                pe.wait_ge(recs_ready, 1)
                for j in range(SJ):
                    if j >= 4:
                        pe.wait_ge(copied, j - 3)
                    for k, rows_f in enumerate((rel, wrow, dead, sf)):
                        last = pe.transpose(ps[:, j % 4, P * k:P * k + P], rows_f[:, j, :], t.ident[:, :])
                    last.then_inc(turned, 1)

            @block.scalar
            def _(act):
                per = P // CH
                for j in range(SJ):
                    act.wait_ge(turned, j + 1)
                    act.activation(
                        erec[:, per * j:per * j + per, :].rearrange("p c (k t) -> p k c t", k=RK),
                        ps[:, j % 4, 0:RK * P].rearrange("p (k c t) -> p k c t", k=RK, c=per), ACT.Copy)
                    act.activation(srec_i[:, per * j:per * j + per, :],
                                   ps[:, j % 4, RK * P:4 * P].rearrange("p (c t) -> p c t", c=per),
                                   ACT.Copy).then_inc(copied, 1)


def block_rows(table):
    return table.rearrange("(a p) f -> p a f", p=P)


def rows_of_turn(table, g):
    return block_rows(table)[:, bass.ds(g * GB, GB), :]


def sums_of_turn(t, g, width):
    return t.acc[:, bass.ds(g * (GB * width), GB * width)].rearrange("p (j w) -> p j w", w=width)


class Norm:

    def __init__(self, sb, sem):
        self.mean, self.var, self.std, self.rstd = (sb(f"ln_{k}", [P, GB]) for k in ("mean", "var", "std", "rstd"))
        self.cent, self.sq = (sb(f"ln_{k}", [P, GB, D]) for k in ("cent", "sq"))
        self.var_ready, self.std_ready = sem("var_ready"), sem("std_ready")

    LINKS = 7

    def vector(self, dve, link, x, y, g):
        full = [P, GB, D]
        link(dve.tensor_reduce(self.mean[:, :], x, AX_X, ALU.add))
        link(dve.tensor_scalar(self.mean[:, :], self.mean[:, :], 1.0 / D, None, ALU.mult))
        link(dve.tensor_tensor(self.cent[:, :, :], x, bc(self.mean[:, :], 2, full), ALU.subtract))
        link(dve.tensor_tensor(self.sq[:, :, :], self.cent[:, :, :], self.cent[:, :, :], ALU.mult))
        link(dve.tensor_reduce(self.var[:, :], self.sq[:, :, :], AX_X, ALU.add))
        dve.tensor_scalar(self.var[:, :], self.var[:, :], 1.0 / D, EPS, ALU.mult, ALU.add).then_inc(self.var_ready, 1)
        dve.wait_ge(self.std_ready, g + 1)
        link(dve.reciprocal(self.rstd[:, :], self.std[:, :]))
        link(dve.tensor_tensor(self.sq[:, :, :], self.cent[:, :, :], bc(self.rstd[:, :], 2, full), ALU.mult))
        return dve.tensor_scalar(y, self.sq[:, :, :], 0.0, None, ALU.max)

    def scalar(self, act, g):
        act.wait_ge(self.var_ready, g + 1)
        act.activation(self.std[:, :], self.var[:, :], ACT.Sqrt).then_inc(self.std_ready, 1)


def norm_phase(nc, t, x):
    with room(nc, "norm") as (sb, psum, sem):
        xb = sb("xb", [P, GB, D])
        hb = sb("hb", [P, GB, D])
        x_in, x_used, h_ready, h_out, chain_v = (sem(k) for k in ("x_in", "x_used", "h_ready", "h_out", "chain_v"))
        norm = Norm(sb, sem)

        with nc.Block() as block:
            @block.sync
            def _(sp):
                with sp.Fori(0, NG) as g:
                    sp.wait_ge(x_used, g + 1)
                    sp.dma_start(xb[:, :, :], rows_of_turn(x, g)).then_inc(x_in, 16)

            @block.vector
            def _(dve):
                chain = Chain(dve, chain_v)
                dve.sem_inc(x_used, 1)
                with chain.turns(NG, Norm.LINKS) as g:
                    dve.wait_ge(x_in, 16 * g + 16)
                    dve.wait_ge(h_out, 16 * g + 16)
                    norm.vector(dve, chain.link, xb[:, :, :], hb[:, :, :], g).then_inc(h_ready, 1)
                    dve.sem_inc(x_used, 1)

            @block.scalar
            def _(act):
                act.sem_inc(h_out, 16)
                with act.Fori(0, NG) as g:
                    norm.scalar(act, g)
                    act.wait_ge(h_ready, g + 1)
                    act.dma_start(rows_of_turn(t.h_d, g), hb[:, :, :]).then_inc(h_out, 16)
                act.wait_ge(h_out, 16 * NG + 16)


def sage_edges(nc, t, table, tag):
    with room(nc, tag) as (sb, psum, sem):
        msg = sb("msg", [P, RING, MW])
        sel = sb("sel", [P, RING, P])
        src = sb("src", [P, 2, CH], I32)
        rec = sb("rec", [P, 2, RK * CH])
        blk = sb("blk", [1, 2, CH], I32)
        ps = psum("ps_sums", [P, 4, 512])
        zeroed, go_v, go_p = sem("zeroed"), sem("go_v"), sem("go_p")
        rec_in = [sem(f"rec_in{h}") for h in range(2)]
        blk_in = [sem(f"blk_in{h}") for h in range(2)]
        src_in = [sem(f"src_in{h}") for h in range(2)]
        gathered = [sem(f"gathered{k}") for k in range(2 * KG)]
        rec_used, ps_used = sem("rec_used"), sem("ps_used")
        sel_ready, sums_ready, chain_v = sem("sel_ready"), sem("sums_ready"), sem("chain_v")

        with nc.Block() as block:
            @block.sync
            def _(sp):
                with sp.Fori(0, PAIRS) as g:
                    for h in range(2):
                        c = g * 2 + h
                        sp.wait_ge(sums_ready, KG * c + KG)
                        sp.dma_start(src[:, h, :], t.src_d[:, bass.ds(c, 1), :]).then_inc(src_in[h], 16)
                        sp.wait_ge(rec_used, c + 1)
                        sp.dma_start(rec[:, h, :], t.edge_d[:, bass.ds(c, 1), :]).then_inc(rec_in[h], 16)
                        sp.dma_start(blk[:, h, :], t.b_d[bass.ds(c, 1), :]).then_inc(blk_in[h], 16)

            @block.gpsimd
            def _(pool):
                pool.wait_ge(zeroed, 2)
                with pool.Fori(0, PAIRS) as g:
                    for h in range(2):
                        c = g * 2 + h
                        pool.wait_ge(src_in[h], 16 * g + 16)
                        for k in range(KG):
                            pool.wait_ge(sums_ready, KG * c + k + 1)

                            pool.sem_inc(go_p, 1)
                            for i in range(GR):
                                slot = h * CH + k * GR + i
                                pool.indirect_dma_start(
                                    msg[:, slot, 0:D], None, table,
                                    bass.IndirectOffsetOnAxis(ap=src[:, h, k * GR + i:k * GR + i + 1], axis=0)).then_inc(gathered[h * KG + k], 16)

            @block.vector
            def _(dve):
                chain = Chain(dve, chain_v)
                dve.memset(t.acc[:, :], 0.0).then_inc(zeroed, 1)
                dve.memset(msg[:, :, D:MW], 1.0).then_inc(zeroed, 1)
                dve.wait_ge(zeroed, 2)
                dve.sem_inc(rec_used, 2)
                dve.sem_inc(ps_used, 2)
                regs = [dve.alloc_register(f"{tag}_block{i}") for i in range(CH)]
                with chain.turns(PAIRS, 2 * CH) as g:
                    for h in range(2):
                        c = g * 2 + h
                        dve.wait_ge(rec_in[h], 16 * g + 16)
                        for k in range(KG):
                            place = rec[:, h, k * GR:k * GR + GR]
                            dve.tensor_tensor(sel[:, h * CH + k * GR:h * CH + k * GR + GR, :],
                                              bc(t.iota[:, :], 1, [P, GR, P]), bc(place, 2, [P, GR, P]),
                                              ALU.is_equal).then_inc(sel_ready, 1)
                        dve.wait_ge(blk_in[h], 16 * g + 16)
                        dve.sem_inc(go_v, 1)
                        dve.load(regs, blk[0:1, h, :])
                        at = [dve.snap(r, min_val=0, max_val=NB - 1) for r in regs]
                        for k in range(KG):
                            dve.wait_ge(sums_ready, KG * c + k + 1 + 2 * KG)
                            for i in range(GR):
                                a = t.acc[:, bass.ds(at[k * GR + i] * MW, MW)]
                                part = ps[:, 2 * (k % 2) + i // 2, (i % 2) * MW:(i % 2) * MW + MW]
                                chain.link(dve.tensor_tensor(a, a, part, ALU.add))
                            dve.sem_inc(ps_used, 1)
                        dve.sem_inc(rec_used, 1)

            @block.tensor
            def _(pe):
                pe.sem_inc(sums_ready, 2 * KG)
                with pe.Fori(0, PAIRS) as g:
                    for h in range(2):
                        for k in range(KG):
                            n = g * (2 * KG) + (h * KG + k + 1)
                            pe.wait_ge(sel_ready, n)
                            pe.wait_ge(gathered[h * KG + k], 16 * GR * g + 16 * GR)
                            pe.wait_ge(ps_used, n)
                            for i in range(GR):
                                slot = h * CH + k * GR + i
                                last = pe.matmul(ps[:, 2 * (k % 2) + i // 2, (i % 2) * MW:(i % 2) * MW + MW],
                                                 sel[:, slot, :], msg[:, slot, :], start=True, stop=True)
                            last.then_inc(sums_ready, 1)


SPLIT = ((0, 512), (512, GN))


def sage_dense(nc, t, w1, b1, w2, b2):
    with room(nc, "sage_dense") as (sb, psum, sem):
        w1s = sb("w1s", [P, 2, HID])
        w2s = sb("w2s", [P, 2, 2, D])
        b1s = sb("b1s", [P, 2])
        b2s = sb("b2s", [P, D])
        hb = sb("hb", [P, GB, D])
        mean = sb("mean", [P, GB, D])
        hT = sb("hT", [P, GN])
        aT = sb("aT", [P, GN])
        hid = sb("hid", [P, 2, GN])
        own = sb("own", [P, GB, D])
        nbr = sb("nbr", [P, GB, D])
        ps = psum("ps_in", [P, 4 * 512])
        psh = psum("ps_hid", [P, 2, 1024])
        w_in, h_in, h_used, mean_ready, turned, copied, hid_ready, hid_copied = (
            sem(k) for k in ("w_in", "h_in", "h_used", "mean_ready", "turned", "copied", "hid_ready", "hid_copied"))
        out_ready, own_ready, nbr_ready, stored, chain_v, go_v = (
            sem(k) for k in ("out_ready", "own_ready", "nbr_ready", "stored", "chain_v", "go_v"))

        with nc.Block() as block:
            @block.sync
            def _(sp):
                sp.dma_start(w1s[:, :, :], w1.rearrange("(s k) h -> k s h", k=P)).then_inc(w_in, 16)
                for part in range(2):
                    sp.dma_start(w2s[:, :, part, :], w2[HID * part:HID * part + HID, :]
                                 .rearrange("(c k) o -> k c o", k=P)).then_inc(w_in, 16)
                sp.dma_start(b1s[:, :], b1.rearrange("(c k) -> k c", k=P), allow_slow_non_contiguous=True).then_inc(w_in, 16)
                sp.dma_start(b2s[:, :], b2.partition_broadcast(P)).then_inc(w_in, 16)
                with sp.Fori(0, NG) as g:
                    sp.wait_ge(h_used, g + 1)
                    sp.dma_start(hb[:, :, :], rows_of_turn(t.h_d, g)).then_inc(h_in, 16)

            @block.vector
            def _(dve):
                chain = Chain(dve, chain_v)
                dve.wait_ge(w_in, 80)
                with chain.turns(NG, 1) as g:
                    a = sums_of_turn(t, g, MW)
                    iv = t.inv[:, bass.ds(g * GB, GB)]
                    chain.link(dve.tensor_scalar(iv, a[:, :, D], 1.0, None, ALU.max))
                    dve.sem_inc(go_v, 1)
                    dve.reciprocal(iv, iv).then_inc(own_ready, 1)
                    dve.wait_ge(own_ready, g * 2 + 1)
                    dve.wait_ge(turned, g + 1)
                    dve.tensor_tensor(mean[:, :, :], a[:, :, 0:D], bc(iv, 2, [P, GB, D]), ALU.mult).then_inc(mean_ready, 1)
                    dve.wait_ge(nbr_ready, g + 2)
                    dve.wait_ge(stored, 32 * g + 32)
                    dve.tensor_tensor(own[:, :, :], ps[:, 0:GB * 2 * D].rearrange("p (j w) -> p j w", j=GB)[:, :, 0:D],
                                      bc(b2s[:, :], 1, [P, GB, D]), ALU.add).then_inc(own_ready, 1)

            @block.tensor
            def _(pe):
                pe.sem_inc(turned, 1)
                pe.sem_inc(h_used, 1)
                pe.wait_ge(w_in, 80)
                with pe.Fori(0, NG) as g:
                    pe.wait_ge(h_in, 16 * g + 16)
                    pe.wait_ge(own_ready, g * 2 + 1)
                    pe.wait_ge(nbr_ready, g + 1)
                    for j in range(GB):
                        pe.transpose(ps[:, P * j:P * j + P], hb[:, j, :], t.ident[:, :])
                    pe.wait_ge(mean_ready, g + 1)
                    for j in range(GB):
                        last = pe.transpose(ps[:, 1024 + P * j:1024 + P * j + P], mean[:, j, :], t.ident[:, :])
                    last.then_inc(turned, 1)
                    pe.wait_ge(copied, g * 2 + 2)
                    pe.sem_inc(h_used, 1)
                    for c in range(2):
                        for lo, hi in SPLIT:
                            for s, rows in ((0, hT), (1, aT)):
                                last = pe.matmul(psh[:, c, lo:hi], w1s[:, s, P * c:P * c + P], rows[:, lo:hi],
                                                 start=(s == 0), stop=(s == 1))
                        last.then_inc(hid_ready, 1)
                    pe.wait_ge(hid_copied, g * 2 + 2)
                    for j in range(GB):
                        for c in range(2):
                            last = pe.matmul(ps[:, 2 * D * j:2 * D * j + 2 * D], hid[:, c, P * j:P * j + P],
                                             w2s[:, c, :, :].rearrange("k s o -> k (s o)"), start=(c == 0), stop=(c == 1))
                    last.then_inc(out_ready, 1)

            @block.scalar
            def _(act):
                act.sem_inc(stored, 32)
                act.sem_inc(nbr_ready, 1)
                act.wait_ge(w_in, 80)
                with act.Fori(0, NG) as g:
                    act.wait_ge(turned, g + 2)
                    act.activation(hT[:, :], ps[:, 0:GN], ACT.Copy).then_inc(copied, 1)
                    act.activation(aT[:, :], ps[:, 1024:1024 + GN], ACT.Copy).then_inc(copied, 1)
                    for c in range(2):
                        act.wait_ge(hid_ready, g * 2 + c + 1)
                        act.activation(hid[:, c, :], psh[:, c, 0:GN], ACT.Relu, bias=b1s[:, c:c + 1]).then_inc(hid_copied, 1)
                    act.wait_ge(out_ready, g + 1)
                    act.wait_ge(stored, 32 * g + 32)
                    act.activation(nbr[:, :, :], ps[:, 0:GB * 2 * D].rearrange("p (j w) -> p j w", j=GB)[:, :, D:2 * D],
                                   ACT.Copy).then_inc(nbr_ready, 1)
                    act.wait_ge(own_ready, g * 2 + 2)
                    act.dma_start(rows_of_turn(t.r_d, g), own[:, :, :]).then_inc(stored, 16)
                    act.wait_ge(nbr_ready, g + 2)
                    act.dma_start(rows_of_turn(t.p_d, g), nbr[:, :, :]).then_inc(stored, 16)
                act.wait_ge(stored, 32 * NG + 32)


def sage_output(nc, t, x, w_in_, b_in_):
    with room(nc, "sage_output") as (sb, psum, sem):
        ws = sb("ws", [P, D])
        bs = sb("bs", [P, 1])
        xb = sb("xb", [P, GB, D])
        rb = sb("rb", [P, GB, D])
        y = sb("y", [P, GB, D])
        z = sb("z", [P, GB, D])
        e = sb("e", [P, GB, D])
        x1 = sb("x1", [P, GB, D])
        hn = sb("hn", [P, GB, D])
        top = sb("top", [P, GB])
        tot = sb("tot", [P, GB])
        lse = sb("lse", [P, GB])
        hT = sb("hT", [P, GN])
        res = sb("res", [P, GN])
        ps = psum("ps_turn", [P, 1024])
        psw = psum("ps_win", [P, 1024])
        w_in, x_in, x_used, z_ready, exp_ready, tot_ready, lse_ready, x1_ready = (
            sem(k) for k in ("w_in", "x_in", "x_used", "z_ready", "exp_ready", "tot_ready", "lse_ready", "x1_ready"))
        hn_ready, turned, copied, prod_ready, res_ready, stored, chain_v = (
            sem(k) for k in ("hn_ready", "turned", "copied", "prod_ready", "res_ready", "stored", "chain_v"))
        norm = Norm(sb, sem)
        full = [P, GB, D]

        with nc.Block() as block:
            @block.sync
            def _(sp):
                sp.dma_start(ws[:, :], w_in_).then_inc(w_in, 16)
                sp.dma_start(bs[:, :], b_in_.rearrange("(k a) -> k a", a=1), allow_slow_non_contiguous=True).then_inc(w_in, 16)
                with sp.Fori(0, NG) as g:
                    sp.wait_ge(x_used, g + 1)
                    sp.dma_start(xb[:, :, :], rows_of_turn(x, g)).then_inc(x_in, 16)
                    sp.dma_start(rb[:, :, :], rows_of_turn(t.r_d, g)).then_inc(x_in, 16)

            @block.vector
            def _(dve):
                chain = Chain(dve, chain_v)
                link = chain.link
                dve.sem_inc(x_used, 1)
                with chain.turns(NG, 4 + Norm.LINKS) as g:
                    iv = t.inv[:, bass.ds(g * GB, GB)]
                    dve.wait_ge(x_in, 32 * g + 32)
                    link(dve.tensor_tensor(y[:, :, :], sums_of_turn(t, g, MW)[:, :, 0:D], bc(iv, 2, full), ALU.mult))
                    link(dve.tensor_tensor(y[:, :, :], y[:, :, :], rb[:, :, :], ALU.add))
                    link(dve.tensor_reduce(top[:, :], y[:, :, :], AX_X, ALU.max))
                    dve.tensor_tensor(z[:, :, :], y[:, :, :], bc(top[:, :], 2, full), ALU.subtract).then_inc(z_ready, 1)
                    dve.wait_ge(exp_ready, g + 1)
                    dve.tensor_reduce(tot[:, :], e[:, :, :], AX_X, ALU.add).then_inc(tot_ready, 1)
                    dve.wait_ge(lse_ready, g + 1)
                    link(dve.tensor_tensor(y[:, :, :], z[:, :, :], bc(lse[:, :], 2, full), ALU.subtract))
                    dve.wait_ge(stored, 32 * g + 32)
                    dve.tensor_tensor(x1[:, :, :], xb[:, :, :], y[:, :, :], ALU.add).then_inc(x1_ready, 1)
                    dve.wait_ge(x1_ready, g + 1)
                    dve.sem_inc(x_used, 1)
                    dve.wait_ge(turned, g + 1)
                    norm.vector(dve, link, x1[:, :, :], hn[:, :, :], g).then_inc(hn_ready, 1)

            @block.tensor
            def _(pe):
                pe.sem_inc(turned, 1)
                pe.wait_ge(w_in, 32)
                with pe.Fori(0, NG) as g:
                    pe.wait_ge(hn_ready, g + 1)
                    pe.wait_ge(copied, g + 1)
                    for j in range(GB):
                        last = pe.transpose(ps[:, P * j:P * j + P], hn[:, j, :], t.ident[:, :])
                    last.then_inc(turned, 1)
                    pe.wait_ge(copied, g + 2)
                    pe.wait_ge(res_ready, g + 1)
                    for lo, hi in SPLIT:
                        last = pe.matmul(psw[:, lo:hi], ws[:, :], hT[:, lo:hi], start=True, stop=True)
                    last.then_inc(prod_ready, 1)

            @block.scalar
            def _(act):
                act.sem_inc(stored, 32)
                act.sem_inc(copied, 1)
                act.sem_inc(res_ready, 1)
                act.wait_ge(w_in, 32)
                with act.Fori(0, NG) as g:
                    act.wait_ge(z_ready, g + 1)
                    act.activation(e[:, :, :], z[:, :, :], ACT.Exp).then_inc(exp_ready, 1)
                    act.wait_ge(tot_ready, g + 1)
                    act.activation(lse[:, :], tot[:, :], ACT.Ln).then_inc(lse_ready, 1)
                    norm.scalar(act, g)
                    act.wait_ge(x1_ready, g + 1)
                    act.dma_start(rows_of_turn(t.x1_d, g), x1[:, :, :]).then_inc(stored, 16)
                    act.wait_ge(turned, g + 2)
                    act.activation(hT[:, :], ps[:, 0:GN], ACT.Copy).then_inc(copied, 1)
                    act.wait_ge(prod_ready, g + 1)
                    act.wait_ge(stored, 32 * g + 48)
                    act.activation(res[:, :], psw[:, 0:GN], ACT.Relu, bias=bs[:, 0:1]).then_inc(res_ready, 1)
                    act.wait_ge(res_ready, g + 2)
                    act.dma_start(t.hT_d[:, bass.ds(g * GN, GN)], res[:, :]).then_inc(stored, 16)
                act.wait_ge(stored, 32 * NG + 32)


SCALE = float(C) ** -0.5


def conv_project(nc, t, layer, a):
    with room(nc, f"project{layer}") as (sb, psum, sem):
        ws = sb("ws", [P, 4, D])
        bs = sb("bs", [P, 4, D])
        web = sb("web", [P, D])
        hT = sb("hT", [P, GN])
        kv = sb("kv", [P, GB, 2 * D])
        xr = sb("xr", [P, GB, D])
        qe = sb("qe", [P, GB, D])
        ps = psum("ps_proj", [P, GB, 512])
        w_in, h_in, proj_ready, q_ready, qe_ready, kv_ready, xr_ready, stored, chain_v, go_v = (
            sem(k) for k in ("w_in", "h_in", "proj_ready", "q_ready", "qe_ready", "kv_ready", "xr_ready", "stored", "chain_v", "go_v"))

        with nc.Block() as block:
            @block.sync
            def _(sp):
                for k, name in enumerate(("q", "k", "v", "skip")):
                    sp.dma_start(ws[:, k, :], a[f"L1_gnn_W{name}"][layer]).then_inc(w_in, 16)
                    sp.dma_start(bs[:, k, :], a[f"L1_gnn_b{name}"][layer].partition_broadcast(P)).then_inc(w_in, 16)
                sp.dma_start(web[:, :], a["L1_gnn_We"][layer].rearrange("a d -> (a d)").partition_broadcast(P)).then_inc(w_in, 16)
                with sp.Fori(0, NG) as g:
                    sp.wait_ge(proj_ready, g + 1)
                    sp.dma_start(hT[:, :], t.hT_d[:, bass.ds(g * GN, GN)]).then_inc(h_in, 16)

            @block.tensor
            def _(pe):
                pe.wait_ge(w_in, 16 * 9)
                pe.sem_inc(proj_ready, 1)
                with pe.Fori(0, NG) as g:
                    pe.wait_ge(h_in, 16 * g + 16)
                    pe.wait_ge(q_ready, g + 1)
                    pe.wait_ge(kv_ready, g + 1)
                    pe.wait_ge(xr_ready, g + 1)
                    for j in range(GB):
                        last = pe.matmul(ps[:, j, :], hT[:, P * j:P * j + P], ws[:, :, :].rearrange("k s o -> k (s o)"),
                                         start=True, stop=True)
                    last.then_inc(proj_ready, 1)

            @block.vector
            def _(dve):
                chain = Chain(dve, chain_v)
                for s in (q_ready, kv_ready, xr_ready):
                    dve.sem_inc(s, 1)
                dve.wait_ge(w_in, 16 * 9)
                chain.link(dve.tensor_scalar(bs[:, 0, :], bs[:, 0, :], SCALE, None, ALU.mult))
                with chain.turns(NG, 1) as g:
                    rows = t.qreg[:, bass.ds(g * (GB * QW), GB * QW)].rearrange("p (j w) -> p j w", w=QW)
                    dve.wait_ge(proj_ready, g + 2)
                    dve.wait_ge(stored, 32 * g + 32)
                    dve.tensor_tensor(kv[:, :, :], ps[:, :, D:3 * D],
                                      bc(bs[:, 1:3, :].rearrange("p k d -> p (k d)"), 1, [P, GB, 2 * D]), ALU.add).then_inc(kv_ready, 1)
                    dve.tensor_tensor(xr[:, :, :], ps[:, :, 3 * D:4 * D], bc(bs[:, 3, :], 1, [P, GB, D]), ALU.add).then_inc(xr_ready, 1)
                    dve.scalar_tensor_tensor(rows[:, :, 0:D], ps[:, :, 0:D], SCALE, bc(bs[:, 0, :], 1, [P, GB, D]),
                                             ALU.mult, ALU.add).then_inc(q_ready, 1)
                    dve.wait_ge(q_ready, g + 2)
                    chain.link(dve.tensor_tensor(qe[:, :, :], rows[:, :, 0:D], bc(web[:, :], 1, [P, GB, D]), ALU.mult))
                    dve.sem_inc(go_v, 1)
                    dve.tensor_reduce(rows[:, :, D:QW], qe[:, :, :].rearrange("p j (h c) -> p j h c", h=HEADS),
                                      AX_X, ALU.add).then_inc(qe_ready, 1)

            @block.scalar
            def _(act):
                act.sem_inc(stored, 32)
                with act.Fori(0, NG) as g:
                    act.wait_ge(kv_ready, g + 2)
                    act.dma_start(rows_of_turn(t.kv_d, g), kv[:, :, :]).then_inc(stored, 16)
                    act.wait_ge(xr_ready, g + 2)
                    act.dma_start(rows_of_turn(t.xr_d, g), xr[:, :, :]).then_inc(stored, 16)
                act.wait_ge(stored, 32 * NG + 32)


def chunk(g, half):
    return g * 2 + half, half, g


def conv_edges(nc, t, tag):
    with room(nc, tag) as (sb, psum, sem):
        HR = HEADS * CH
        kv = sb("kv", [P, RING, 2 * D])
        sel = sb("sel", [P, RING, P])
        selT = sb("selT", [P, KG, GR * P])
        src = sb("src", [P, 2, CH], I32)
        rec = sb("rec", [P, 2, RK * CH])
        blk = sb("blk", [1, 2, CH], I32)
        pen = sb("pen", [HR, 2, PW])
        stp = sb("stp", [HEADS, 2, CH, HK])
        prod = sb("prod", [P, 2, GR, D])
        score = sb("score", [P, HEADS, CH])
        qwe = sb("qwe", [P, HEADS, CH])
        fwd = sb("fwd", [HR, P])
        run = sb("run", [HR, P])
        top = sb("top", [HR, P])
        below = sb("below", [HR, P])
        expo = sb("expo", [HR, P])
        ends = sb("ends", [HR, 2, HEADS])
        fromleft = sb("fromleft", [HEADS, CH + 1])
        fromright = sb("fromright", [HEADS, CH + 1])
        sides = sb("sides", [HEADS, 2, CH])
        picked = sb("picked", [HR, 2, CH])
        side = sb("side", [HR, 2])
        newtop = sb("newtop", [HEADS, 1])
        drop = sb("drop", [HEADS, 1])
        fac = sb("fac", [HEADS, 1])
        facm = sb("facm", [HEADS, HEADS])
        node = sb("node", [HEADS, P])
        rescale = sb("rescale", [P, HEADS])
        pv = sb("pv", [P, CH, HEADS, C + 2])
        away = sb("away", [P, 2, GR, P])
        place = sb("place", [P, 2, CH * P])
        awayT = sb("awayT", [P, 2, GR * P])
        psQ = psum("ps_query", [P, 4, 512])
        psC = psum("ps_sums", [P, 2, 512])
        psM = psum("ps_small", [P, 512])
        rows = psM[0:HR, 0:P]
        psEnds = psM[0:HEADS, P:P + 2 * CH]
        psSides = psM[0:HR, 160:160 + 2 * CH]
        psFac = psM[:, 192:192 + HEADS]
        psExp = psM[:, 196:196 + HR]

        rec_in, blk_in, src_in, place_in = (
            [sem(f"{k}{h}") for h in range(2)] for k in ("rec_in", "blk_in", "src_in", "place_in"))
        gathered = [sem(f"gathered{k}") for k in range(2 * KG)]
        ready, go_v, go_p, go_t, chain_v = (sem(k) for k in ("ready", "go_v", "go_p", "go_t", "chain_v"))
        scored, rec_used, blk_used, away_ready = (sem(k) for k in ("scored", "rec_used", "blk_used", "away_ready"))
        sel_ready, selT_ready, awayT_ready, place_used, q_ready, q_used = (
            sem(k) for k in ("sel_ready", "selT_ready", "awayT_ready", "place_used", "q_ready", "q_used"))
        rows_ready, ends_ready, ends_summed, sides_ready, sides_spread, drop_ready, fac_exp, fac_ready, fac_spread = (
            sem(k) for k in ("rows_ready", "ends_ready", "ends_summed", "sides_ready", "sides_spread", "drop_ready",
                             "fac_exp", "fac_ready", "fac_spread"))
        below_ready, expo_ready, expo_turned, pv_ready, sums_ready, ps_used = (
            sem(k) for k in ("below_ready", "expo_ready", "expo_turned", "pv_ready", "sums_ready", "ps_used"))

        def pipeline(eng, stages, chain=None, per=0):
            stages(chunk(0, 0), None)
            loop = chain.turns(PAIRS - 1, per) if chain else eng.Fori(0, PAIRS - 1)
            with loop as g:
                stages(chunk(g, 1), chunk(g, 0))
                stages(chunk(g + 1, 0), chunk(g, 1))
            stages(chunk(PAIRS - 1, 1), chunk(PAIRS - 1, 0))
            stages(None, chunk(PAIRS - 1, 1))

        with nc.Block() as block:
            @block.sync
            def _(sp):
                with sp.Fori(0, PAIRS) as g:
                    for h in range(2):
                        c = g * 2 + h
                        sp.wait_ge(scored, c + 1)
                        sp.dma_start(src[:, h, :], t.src_d[:, bass.ds(c, 1), :]).then_inc(src_in[h], 16)
                        sp.wait_ge(rec_used, c + 1)
                        sp.dma_start(rec[:, h, :], t.edge_d[:, bass.ds(c, 1), :]).then_inc(rec_in[h], 16)
                        for k in range(HEADS):
                            sp.dma_start(pen[CH * k:CH * k + CH, h, :], t.pen_d[bass.ds(c * CH, CH), :]).then_inc(rec_in[h], 16)
                        sp.dma_start(stp[:, h, :, :], t.step_d[bass.ds(c * CH, CH), :].partition_broadcast(HEADS)).then_inc(rec_in[h], 16)
                        sp.wait_ge(place_used, c + 1)
                        sp.dma_start(place[:, h, :], t.place_d[bass.ds(c, 1), :].rearrange("a n -> (a n)")
                                     .partition_broadcast(P)).then_inc(place_in[h], 16)
                        sp.wait_ge(blk_used, c + 1)
                        sp.dma_start(blk[:, h, :], t.b_d[bass.ds(c, 1), :]).then_inc(blk_in[h], 16)

            @block.gpsimd
            def _(pool):
                with pool.Fori(0, PAIRS) as g:
                    for h in range(2):
                        c = g * 2 + h
                        pool.wait_ge(src_in[h], 16 * g + 16)
                        for k in range(KG):
                            pool.wait_ge(pv_ready, KG * c + k + 1)
                            pool.sem_inc(go_p, 1)
                            for i in range(GR):
                                j = k * GR + i
                                pool.indirect_dma_start(
                                    kv[:, h * CH + j, :], None, t.kv_d,
                                    bass.IndirectOffsetOnAxis(ap=src[:, h, j:j + 1], axis=0)).then_inc(gathered[h * KG + k], 16)

            @block.vector
            def _(dve):
                chain = Chain(dve, chain_v)
                link, mark, need = chain.link, chain.mark, chain.need
                regs = [dve.alloc_register(f"{tag}_sumblock{i}") for i in range(CH)]
                link(dve.memset(t.acc[:, :], 0.0))
                link(dve.memset(fromleft[:, :], -BIG))
                link(dve.memset(fromright[:, :], -BIG))
                for s, n in ((scored, 2), (rec_used, 2), (blk_used, 2), (pv_ready, 2 * KG), (q_used, 2), (ps_used, 1)):
                    dve.sem_inc(s, n)

                def query(a, k):
                    return psQ[:, 2 * (k % 2):2 * (k % 2) + 2, 0:2 * QW].rearrange("p b (s w) -> p b s w", s=2)

                def multiply(a, k):
                    c, h, g = a
                    lo = h * CH + k * GR
                    if k == 0:
                        dve.wait_ge(rec_in[h], 96 * g + 96)
                    dve.wait_ge(q_ready, KG * c + k + 1 + KG)
                    dve.wait_ge(gathered[h * KG + k], 16 * GR * g + 16 * GR)
                    return mark(dve.tensor_tensor(
                        prod[:, k % 2, :, :].rearrange("p (b s) d -> p b s d", s=2), query(a, k)[:, :, :, 0:D],
                        kv[:, lo:lo + GR, 0:D].rearrange("p (b s) d -> p b s d", s=2), ALU.mult))

                def score_sum(a, k, multiplied):
                    need(multiplied)
                    return mark(dve.tensor_reduce(score[:, :, k * GR:k * GR + GR].rearrange("p h i -> p i h"),
                                                  prod[:, k % 2, :, :].rearrange("p i (h c) -> p i h c", h=HEADS),
                                                  AX_X, ALU.add))

                def edge_term(a, k):
                    c, h, g = a
                    w = rec[:, h, CH + k * GR:CH + k * GR + GR].rearrange("p (b s) -> p b s", s=2)
                    dve.tensor_tensor(qwe[:, :, k * GR:k * GR + GR].rearrange("p h (b s) -> p b s h", s=2),
                                      query(a, k)[:, :, :, D:QW], bc(w, 3, [P, 2, 2, HEADS]), ALU.mult).then_inc(q_used, 1)

                def weigh(b, k):
                    c, h, g = b
                    lo, j = h * CH + k * GR, k * GR
                    dve.tensor_tensor(pv[:, j:j + GR, :, 0:C],
                                      kv[:, lo:lo + GR, D:2 * D].rearrange("p i (h c) -> p i h c", h=HEADS),
                                      pv[:, j:j + GR, :, C:C + 1].to_broadcast([P, GR, HEADS, C]),
                                      ALU.mult).then_inc(pv_ready, 1)

                def rescaled(b, at):
                    a = t.acc[:, bass.ds(at[0] * AW, AW)].rearrange("p (h w) -> p h w", h=HEADS)
                    return mark(dve.tensor_tensor(a, a, bc(rescale[:, :], 2, [P, HEADS, C + 2]), ALU.mult))

                def add(b, k, i, at, before):
                    c, h, g = b
                    if i == 0:
                        dve.wait_ge(sums_ready, KG * c + k + 1 + 2 * KG)
                    if before is not None:
                        need(before)
                    a = t.acc[:, bass.ds(at[k * GR + i] * AW, AW)]
                    done = mark(dve.tensor_tensor(a, a, psC[:, i // 2, (i % 2) * AW:(i % 2) * AW + AW], ALU.add))
                    if i == GR - 1:
                        need(done)
                        dve.sem_inc(ps_used, 1)
                    return done

                def stages(a, b):
                    done = None
                    if b is not None:
                        weigh(b, 0)
                    if a is not None:
                        c, h, g = a
                        m = multiply(a, 0)
                        score_sum(a, 0, m)
                        edge_term(a, 0)
                    if b is not None:
                        weigh(b, 1)
                        dve.wait_ge(blk_in[b[1]], 16 * b[2] + 16)
                        dve.sem_inc(go_v, 1)
                        dve.load(regs, blk[0:1, b[1], :])
                        at = [dve.snap(r, min_val=0, max_val=NB - 1) for r in regs]
                        dve.sem_inc(blk_used, 1)
                        done = rescaled(b, at)
                    for k in (1, 2):
                        if a is not None:
                            m = multiply(a, k)
                        if b is not None and k == 2:
                            weigh(b, 2)
                        if b is not None:
                            done = add(b, k - 1, 0, at, done)
                        if a is not None:
                            r = score_sum(a, k, m)
                        if b is not None:
                            done = add(b, k - 1, 1, at, done)
                        if a is not None:
                            edge_term(a, k)
                        if b is not None:
                            done = add(b, k - 1, 2, at, done)
                            done = add(b, k - 1, 3, at, done)
                    if a is None:
                        weigh(b, 3)
                        for k in (2, 3):
                            for i in range(GR):
                                done = add(b, k, i, at, done)
                        return

                    step = [stp[:, h, :, n] for n in range(HK)]
                    m = multiply(a, 3)
                    edge_term(a, 3)
                    r = score_sum(a, 3, m)
                    dve.wait_ge(q_used, KG * c + KG + 2)
                    need(r)
                    m = mark(dve.tensor_tensor(score[:, :, :], score[:, :, :], qwe[:, :, :], ALU.add))
                    need(m)
                    dve.tensor_tensor(score[:, :, :], score[:, :, :],
                                      bc(rec[:, h, 2 * CH:3 * CH], 1, [P, HEADS, CH]), ALU.add).then_inc(scored, 1)
                    if b is not None:
                        weigh(b, 3)
                    dve.wait_ge(rows_ready, c + 1)
                    m = mark(dve.tensor_tensor_scan(fwd[:, :], pen[:, h, 0:P], rows, -BIG, ALU.add, ALU.max))
                    if b is not None:
                        done = add(b, 2, 0, at, done)
                    need(m)
                    m = mark(dve.tensor_tensor_scan(run[:, ::-1], pen[:, h, P:0:-1], fwd[:, ::-1], -BIG, ALU.add, ALU.max))
                    if b is not None:
                        done = add(b, 2, 1, at, done)
                    need(m)
                    dve.tensor_scalar(ends[:, 0, :], t.hsel[:, :], run[:, P - 1:P], None, ALU.mult)
                    dve.tensor_scalar(ends[:, 1, :], t.hsel[:, :], run[:, 0:1], None, ALU.mult).then_inc(ends_ready, 1)
                    if b is not None:
                        done = add(b, 2, 2, at, done)
                        done = add(b, 2, 3, at, done)
                    dve.tensor_scalar(node[:, :], t.iota[0:HEADS, :], step[4][:, 0:1], None, ALU.is_equal)
                    dve.wait_ge(ends_summed, c + 1)
                    m1 = mark(dve.tensor_tensor_scan(fromleft[:, 1:CH + 1], step[1], psEnds[:, 0:CH], fromleft[:, 0:1],
                                                     ALU.add, ALU.max))
                    m2 = mark(dve.tensor_tensor_scan(fromright[:, CH - 1::-1], step[3][:, ::-1],
                                                     psEnds[:, 2 * CH - 1:CH - 1:-1], -BIG, ALU.add, ALU.max))
                    need(m1)
                    m1 = mark(dve.tensor_tensor(sides[:, 0, :], fromleft[:, 0:CH], step[0], ALU.add))
                    need(m2)
                    dve.tensor_tensor(sides[:, 1, :], fromright[:, 1:CH + 1], step[2], ALU.add).then_inc(sides_ready, 1)
                    need(m1)
                    m = mark(dve.tensor_tensor(newtop[:, :], fromright[:, 0:1], sides[:, 0, 0:1], ALU.max))
                    need(m)
                    m = mark(dve.tensor_tensor(drop[:, :], fromleft[:, 0:1], newtop[:, :], ALU.subtract))
                    if b is not None:
                        done = add(b, 3, 0, at, done)
                    need(m)
                    dve.tensor_scalar(drop[:, :], drop[:, :], 0.0, None, ALU.min).then_inc(drop_ready, 1)
                    dve.tensor_copy(fromleft[:, 0:1], fromleft[:, CH:CH + 1])
                    dve.wait_ge(sides_spread, c + 1)
                    m = mark(dve.tensor_tensor(picked[:, :, :], psSides.rearrange("p (s t) -> p s t", s=2),
                                               bc(t.tsel[:, :], 1, [HR, 2, CH]), ALU.mult))
                    if b is not None:
                        done = add(b, 3, 1, at, done)
                    need(m)
                    m = mark(dve.tensor_reduce(side[:, :], picked[:, :, :], AX_X, ALU.add))
                    need(m)
                    m = mark(dve.scalar_tensor_tensor(top[:, :], pen[:, h, P + 1:2 * P + 1], side[:, 0:1], run[:, :],
                                                      ALU.add, ALU.max))
                    need(m)
                    m = mark(dve.scalar_tensor_tensor(top[:, :], pen[:, h, 2 * P + 1:3 * P + 1], side[:, 1:2], top[:, :],
                                                      ALU.add, ALU.max))
                    need(m)
                    dve.tensor_tensor(below[:, :], rows, top[:, :], ALU.subtract).then_inc(below_ready, 1)
                    if b is not None:
                        done = add(b, 3, 2, at, done)
                    dve.wait_ge(fac_exp, c + 1)
                    m = mark(dve.tensor_scalar(fac[:, :], fac[:, :], -1.0, None, ALU.add))
                    need(m)
                    dve.tensor_scalar(facm[:, :], t.ident[0:HEADS, 0:HEADS], fac[:, 0:1], None, ALU.mult).then_inc(fac_ready, 1)
                    if b is not None:
                        done = add(b, 3, 3, at, done)
                    dve.wait_ge(expo_turned, c + 1)
                    p = psExp.rearrange("p (h i) -> p i h", h=HEADS)
                    dve.tensor_copy(pv[:, :, :, C], p)
                    dve.tensor_tensor(pv[:, :, :, C + 1], p, bc(rec[:, h, CH:2 * CH], 2, [P, CH, HEADS]), ALU.mult)
                    dve.wait_ge(fac_spread, c + 1)
                    m = mark(dve.tensor_scalar(rescale[:, :], psFac, 1.0, None, ALU.add))
                    need(m)
                    dve.sem_inc(rec_used, 1)

                pipeline(dve, stages, chain, 2 * (2 * KG + 1 + CH + 14))

            @block.tensor
            def _(pe):
                pe.sem_inc(q_ready, KG)
                pe.sem_inc(sums_ready, 2 * KG)
                regs = [pe.alloc_register(f"{tag}_queryblock{i}") for i in range(CH)]

                def blocks_of(a):
                    c, h, g = a
                    pe.wait_ge(blk_in[h], 16 * g + 16)
                    pe.sem_inc(go_t, 1)
                    pe.load(regs, blk[0:1, h, :])
                    return loaded()

                def loaded():
                    return [pe.snap(r, min_val=0, max_val=NB - 1) for r in regs]

                def queries(a, k, at):
                    c, h, g = a
                    pe.wait_ge(selT_ready, KG * c + k + 1)
                    pe.wait_ge(q_used, KG * c + k + 1)
                    for i in range(GR):
                        last = pe.matmul(psQ[:, 2 * (k % 2) + i // 2, (i % 2) * QW:(i % 2) * QW + QW],
                                         selT[:, k, P * i:P * i + P],
                                         t.qreg[:, bass.ds(at[k * GR + i] * QW, QW)], start=True, stop=True)
                    last.then_inc(q_ready, 1)

                def sums(b, k):
                    if b is None:
                        return
                    c, h, g = b
                    pe.wait_ge(pv_ready, KG * c + k + 1 + 2 * KG)
                    pe.wait_ge(sel_ready, KG * c + k + 1)
                    pe.wait_ge(ps_used, KG * c + k + 1)
                    for i in range(GR):
                        j = k * GR + i
                        last = pe.matmul(psC[:, i // 2, (i % 2) * AW:(i % 2) * AW + AW], sel[:, h * CH + j, :],
                                         pv[:, j, :, :].rearrange("p h w -> p (h w)"), start=True, stop=True)
                    last.then_inc(sums_ready, 1)

                def stages(a, b, at, following):
                    c = a[0]
                    sums(b, 0)
                    queries(a, 2, at)
                    sums(b, 1)
                    queries(a, 3, at)
                    sums(b, 2)
                    pe.wait_ge(scored, c + 1 + 2)
                    pe.sem_inc(go_t, 1)
                    pe.transpose(rows, score[:, :, :].rearrange("p h t -> p (h t)"), t.ident[:, :]).then_inc(rows_ready, 1)
                    pe.wait_ge(ends_ready, c + 1)
                    pe.sem_inc(go_t, 1)
                    pe.matmul(psEnds[:, 0:CH], ends[:, 0, :], t.tsel[:, :], start=True, stop=True)
                    pe.matmul(psEnds[:, CH:2 * CH], ends[:, 1, :], t.tsel[:, :], start=True, stop=True).then_inc(ends_summed, 1)
                    sums(b, 3)
                    pe.wait_ge(sides_ready, c + 1)
                    pe.sem_inc(go_t, 1)
                    pe.matmul(psSides, t.hselT[:, :], sides[:, :, :].rearrange("p s t -> p (s t)"),
                              start=True, stop=True).then_inc(sides_spread, 1)
                    if following is not None:
                        at = blocks_of(following)
                        queries(following, 0, at)
                    pe.wait_ge(fac_ready, c + 1)
                    pe.sem_inc(go_t, 1)
                    pe.matmul(psFac, node[:, :], facm[:, :], start=True, stop=True).then_inc(fac_spread, 1)
                    pe.wait_ge(expo_ready, c + 1)
                    pe.sem_inc(go_t, 1)
                    pe.transpose(psExp, expo[:, :], t.ident[0:HR, 0:HR]).then_inc(expo_turned, 1)
                    if following is not None:
                        queries(following, 1, at)
                    return at

                at = blocks_of(chunk(0, 0))
                queries(chunk(0, 0), 0, at)
                queries(chunk(0, 0), 1, at)
                at = stages(chunk(0, 0), None, at, chunk(0, 1))
                with pe.Fori(0, PAIRS - 1) as g:
                    at = stages(chunk(g, 1), chunk(g, 0), loaded(), chunk(g + 1, 0))
                    at = stages(chunk(g + 1, 0), chunk(g, 1), at, chunk(g + 1, 1))
                stages(chunk(PAIRS - 1, 1), chunk(PAIRS - 1, 0), loaded(), None)
                for k in range(KG):
                    sums(chunk(PAIRS - 1, 1), k)

            @block.scalar
            def _(act):
                act.sem_inc(place_used, 2)

                def select(a, k):
                    c, h, g = a
                    if k == 0:
                        act.wait_ge(rec_in[h], 96 * g + 96)
                    act.wait_ge(sums_ready, KG * c + k + 1)
                    lo = h * CH + k * GR
                    for i in range(GR):
                        j = k * GR + i
                        act.activation(away[:, k % 2, i, :], t.iota[:, :], ACT.Abs, bias=rec[:, h, j:j + 1],
                                       scale=-1.0).then_inc(away_ready, 1)
                    act.wait_ge(away_ready, CH * c + GR * k + GR)
                    act.activation(sel[:, lo:lo + GR, :], away[:, k % 2, :, :], ACT.Relu, bias=1.0,
                                   scale=-1.0).then_inc(sel_ready, 1)

                def select_turned(a, k):
                    c, h, g = a
                    if k == 0:
                        act.wait_ge(place_in[h], 16 * g + 16)
                    act.activation(awayT[:, k % 2, :], place[:, h, k * GR * P:k * GR * P + GR * P], ACT.Abs,
                                   bias=t.minus[:, 0:1]).then_inc(awayT_ready, 1)
                    act.wait_ge(awayT_ready, KG * c + k + 1)
                    act.wait_ge(q_ready, KG * c + k + 1)
                    act.activation(selT[:, k, :], awayT[:, k % 2, :], ACT.Relu, bias=1.0,
                                   scale=-1.0).then_inc(selT_ready, 1)
                    if k == KG - 1:
                        act.sem_inc(place_used, 1)

                def stages(a, following):
                    c, h, g = a
                    for k in range(KG):
                        select(a, k)
                    if following is not None:
                        for k in range(KG):
                            select_turned(following, k)
                    act.wait_ge(drop_ready, c + 1)
                    act.activation(fac[:, :], drop[:, :], ACT.Exp).then_inc(fac_exp, 1)
                    act.wait_ge(below_ready, c + 1)
                    act.activation(expo[:, :], below[:, :], ACT.Exp).then_inc(expo_ready, 1)

                for k in range(KG):
                    select_turned(chunk(0, 0), k)
                stages(chunk(0, 0), chunk(0, 1))
                with act.Fori(0, PAIRS - 1) as g:
                    stages(chunk(g, 1), chunk(g + 1, 0))
                    stages(chunk(g + 1, 0), chunk(g + 1, 1))
                stages(chunk(PAIRS - 1, 1), None)


def conv_combine(nc, t, layer, a):
    with room(nc, f"combine{layer}") as (sb, psum, sem):
        web = sb("web", [P, D])
        wbeta = sb("wbeta", [P, 3, D])
        xr = sb("xr", [P, GB, D])
        rden = sb("rden", [P, GB, HEADS])
        out = sb("out", [P, GB, HEADS, C])
        dif = sb("dif", [P, GB, D])
        part = sb("part", [P, GB, D])
        part2 = sb("part2", [P, GB, D])
        logit = sb("logit", [P, GB])
        gate = sb("gate", [P, GB])
        mix = sb("mix", [P, GB, D])
        ps = psum("ps_turn", [P, 1024])
        w_in, x_in, x_used, logit_ready, gate_ready, mix_ready, turned, copied, chain_v, go_v = (
            sem(k) for k in ("w_in", "x_in", "x_used", "logit_ready", "gate_ready", "mix_ready", "turned", "copied", "chain_v", "go_v"))
        full = [P, GB, D]
        full4 = [P, GB, HEADS, C]

        with nc.Block() as block:
            @block.sync
            def _(sp):
                sp.dma_start(web[:, :], a["L1_gnn_We"][layer].rearrange("a d -> (a d)").partition_broadcast(P)).then_inc(w_in, 16)
                sp.dma_start(wbeta[:, :, :].rearrange("p k d -> p (k d)"),
                             a["L1_gnn_Wbeta"][layer].rearrange("d a -> (d a)").partition_broadcast(P)).then_inc(w_in, 16)
                with sp.Fori(0, NG) as g:
                    sp.wait_ge(x_used, g + 1)
                    sp.dma_start(xr[:, :, :], rows_of_turn(t.xr_d, g)).then_inc(x_in, 16)

            @block.vector
            def _(dve):
                chain = Chain(dve, chain_v)
                link = chain.link
                dve.wait_ge(w_in, 32)
                dve.sem_inc(x_used, 1)
                with chain.turns(NG, 13) as g:
                    s = sums_of_turn(t, g, AW).rearrange("p j (h w) -> p j h w", h=HEADS)
                    flat = out[:, :, :, :].rearrange("p j h c -> p j (h c)")
                    link(dve.tensor_scalar(rden[:, :, :], s[:, :, :, C], 1e-20, None, ALU.max))
                    link(dve.reciprocal(rden[:, :, :], rden[:, :, :]))
                    link(dve.tensor_tensor(out[:, :, :, :], s[:, :, :, C + 1:C + 2].to_broadcast(full4),
                                           bc(web[:, :].rearrange("p (h c) -> p h c", h=HEADS), 1, full4), ALU.mult))
                    link(dve.tensor_tensor(out[:, :, :, :], out[:, :, :, :], s[:, :, :, 0:C], ALU.add))
                    link(dve.tensor_tensor(out[:, :, :, :], out[:, :, :, :], bc(rden[:, :, :], 3, full4), ALU.mult))
                    dve.wait_ge(x_in, 16 * g + 16)
                    link(dve.tensor_tensor(dif[:, :, :], flat, xr[:, :, :], ALU.subtract))
                    link(dve.tensor_tensor(part[:, :, :], flat, bc(wbeta[:, 0, :], 1, full), ALU.mult))
                    link(dve.tensor_tensor(part2[:, :, :], xr[:, :, :], bc(wbeta[:, 1, :], 1, full), ALU.mult))
                    dve.sem_inc(x_used, 1)
                    link(dve.tensor_tensor(part[:, :, :], part[:, :, :], part2[:, :, :], ALU.add))
                    link(dve.tensor_tensor(part2[:, :, :], dif[:, :, :], bc(wbeta[:, 2, :], 1, full), ALU.mult))
                    link(dve.tensor_tensor(part[:, :, :], part[:, :, :], part2[:, :, :], ALU.add))
                    dve.tensor_reduce(logit[:, :], part[:, :, :], AX_X, ALU.add).then_inc(logit_ready, 1)
                    dve.wait_ge(gate_ready, g + 1)
                    link(dve.tensor_tensor(part2[:, :, :], dif[:, :, :], bc(gate[:, :], 2, full), ALU.mult))
                    dve.wait_ge(turned, g + 1)
                    link(dve.tensor_tensor(mix[:, :, :], flat, part2[:, :, :], ALU.subtract))
                    dve.sem_inc(mix_ready, 1)

            @block.tensor
            def _(pe):
                pe.sem_inc(turned, 1)
                with pe.Fori(0, NG) as g:
                    pe.wait_ge(mix_ready, g + 1)
                    pe.wait_ge(copied, g + 1)
                    for j in range(GB):
                        last = pe.transpose(ps[:, P * j:P * j + P], mix[:, j, :], t.ident[:, :])
                    last.then_inc(turned, 1)

            @block.scalar
            def _(act):
                act.sem_inc(copied, 1)
                with act.Fori(0, NG) as g:
                    act.wait_ge(logit_ready, g + 1)
                    act.activation(gate[:, :], logit[:, :], ACT.Sigmoid).then_inc(gate_ready, 1)
                    act.wait_ge(turned, g + 2)
                    act.activation(t.qreg[:, bass.ds(g * GN, GN)], ps[:, 0:GN], ACT.Copy).then_inc(copied, 1)


STAT = 500
assert N % STAT == 0


def conv_norm(nc, t, layer, a, out):
    final = layer == LAYERS - 1
    with room(nc, f"batch_norm{layer}") as (sb, psum, sem):
        gamma = sb("gamma", [P, 1])
        beta = sb("beta", [P, 1])
        stats = sb("stats", [P, N // STAT, 6])
        mv = sb("mv", [P, 2])
        var = sb("var", [P, 1])
        std = sb("std", [P, 1])
        mul = sb("mul", [P, 1])
        hT = sb("hT", [P, GN])
        x1 = sb("x1", [P, GB, D])
        cen = sb("cen", [P, GN])
        rel = sb("rel", [P, GN])
        new = sb("new", [P, GN])
        res = sb("res", [P, GB, D])
        ps = psum("ps_turn", [P, 1024])
        w_in, x_in, x_used, var_ready, std_ready, cen_ready, rel_ready, new_ready, turned, res_ready, stored, chain_v = (
            sem(k) for k in ("w_in", "x_in", "x_used", "var_ready", "std_ready", "cen_ready", "rel_ready", "new_ready",
                             "turned", "res_ready", "stored", "chain_v"))

        with nc.Block() as block:
            @block.sync
            def _(sp):
                sp.dma_start(gamma[:, :], a["L1_gnn_bn_gamma"][layer].rearrange("(d a) -> d a", a=1)).then_inc(w_in, 16)
                sp.dma_start(beta[:, :], a["L1_gnn_bn_beta"][layer].rearrange("(d a) -> d a", a=1)).then_inc(w_in, 16)
                with sp.Fori(0, NG) as g:
                    sp.wait_ge(x_used, g + 1)
                    sp.dma_start(hT[:, :], t.hT_d[:, bass.ds(g * GN, GN)]).then_inc(x_in, 16)
                    if final:
                        sp.dma_start(x1[:, :, :], rows_of_turn(t.x1_d, g)).then_inc(x_in, 16)

            @block.vector
            def _(dve):
                chain = Chain(dve, chain_v)
                link = chain.link
                dve.sem_inc(x_used, 1)
                dve.sem_inc(new_ready, 1)
                for j in range(N // STAT):
                    last = dve.bn_stats(stats[:, j, :], t.qreg[:, STAT * j:STAT * j + STAT])
                link(last)
                link(dve.bn_aggr(mv[:, :], stats[:, :, :].rearrange("p a b -> p (a b)")))
                dve.tensor_scalar(var[:, :], mv[:, 1:2], EPS, None, ALU.add).then_inc(var_ready, 1)
                dve.wait_ge(std_ready, 1)
                dve.wait_ge(w_in, 32)
                link(dve.reciprocal(mul[:, :], std[:, :]))
                link(dve.tensor_tensor(mul[:, :], mul[:, :], gamma[:, :], ALU.mult))
                with dve.Fori(0, NG) as g:
                    dve.wait_ge(rel_ready, g + 1)
                    dve.tensor_scalar(cen[:, :], t.qreg[:, bass.ds(g * GN, GN)], mv[:, 0:1], mul[:, 0:1],
                                      ALU.subtract, ALU.mult).then_inc(cen_ready, 1)
                    dve.wait_ge(rel_ready, g + 2)
                    dve.wait_ge(x_in, (32 if final else 16) * g + (32 if final else 16))
                    if final:
                        dve.wait_ge(turned, g + 1)
                    else:
                        dve.wait_ge(stored, 16 * g + 16)
                    dve.tensor_tensor(new[:, :], rel[:, :], hT[:, :], ALU.add).then_inc(new_ready, 1)
                    if final:
                        dve.wait_ge(turned, g + 2)
                        dve.wait_ge(stored, 16 * g + 16)
                        dve.tensor_tensor(res[:, :, :], x1[:, :, :], ps[:, 0:GN].rearrange("p (j d) -> p j d", j=GB),
                                          ALU.add).then_inc(res_ready, 1)
                        dve.wait_ge(res_ready, g + 1)
                    else:
                        dve.wait_ge(new_ready, g + 2)
                    dve.sem_inc(x_used, 1)

            @block.tensor
            def _(pe):
                if final:
                    pe.sem_inc(turned, 1)
                    with pe.Fori(0, NG) as g:
                        pe.wait_ge(new_ready, g + 2)
                        pe.wait_ge(x_used, g + 1)
                        for j in range(GB):
                            last = pe.transpose(ps[:, P * j:P * j + P], new[:, P * j:P * j + P], t.ident[:, :])
                        last.then_inc(turned, 1)

            @block.scalar
            def _(act):
                act.sem_inc(stored, 16)
                act.sem_inc(rel_ready, 1)
                act.wait_ge(var_ready, 1)
                act.activation(std[:, :], var[:, :], ACT.Sqrt).then_inc(std_ready, 1)
                act.wait_ge(w_in, 32)
                with act.Fori(0, NG) as g:
                    act.wait_ge(cen_ready, g + 1)
                    act.wait_ge(new_ready, g + 1)
                    act.activation(rel[:, :], cen[:, :], ACT.Relu, bias=beta[:, 0:1]).then_inc(rel_ready, 1)
                    if final:
                        act.wait_ge(res_ready, g + 1)
                        act.dma_start(rows_of_turn(out, g), res[:, :, :]).then_inc(stored, 16)
                    else:
                        act.wait_ge(new_ready, g + 2)
                        act.dma_start(t.hT_d[:, bass.ds(g * GN, GN)], new[:, :]).then_inc(stored, 16)
                act.wait_ge(stored, 16 * NG + 16)


_IN = ["x", "src", "dst", "edge_weight1", "L0_gnn_W1", "L0_gnn_b1", "L0_gnn_W2", "L0_gnn_b2", "L1_gnn_W_in",
       "L1_gnn_b_in", "L1_gnn_Wq", "L1_gnn_bq", "L1_gnn_Wk", "L1_gnn_bk", "L1_gnn_Wv", "L1_gnn_bv", "L1_gnn_We",
       "L1_gnn_Wskip", "L1_gnn_bskip", "L1_gnn_Wbeta", "L1_gnn_bn_gamma", "L1_gnn_bn_beta"]


def lay_out(inputs):
    import numpy as np

    a = {name: np.ascontiguousarray(np.asarray(inputs[name])) for name in _IN}
    x = np.zeros((NP, D), a["x"].dtype)
    x[:N] = a["x"]
    src = np.zeros((STEPS * P,), a["src"].dtype)
    src[:E] = a["src"]
    dst = np.full((STEPS * P,), NP - 1, a["dst"].dtype)
    dst[:E] = a["dst"]
    wgt = np.zeros((STEPS * P,), a["edge_weight1"].dtype)
    wgt[:E] = a["edge_weight1"].reshape(-1)
    a.update(x=x, src=src, dst=dst, edge_weight1=wgt)
    return a


def program(nc, a, out):
    t = Tables()
    with ExitStack() as ctx:
        declare(nc, t, ctx)
        setup_phase(nc, t, a["src"], a["dst"], a["edge_weight1"])
        declare_sums(nc, t, ctx)
        norm_phase(nc, t, a["x"])
        sage_edges(nc, t, t.h_d, "first")
        sage_dense(nc, t, a["L0_gnn_W1"], a["L0_gnn_b1"], a["L0_gnn_W2"], a["L0_gnn_b2"])
        sage_edges(nc, t, t.p_d, "second")
        sage_output(nc, t, a["x"], a["L1_gnn_W_in"], a["L1_gnn_b_in"])
        for layer in range(LAYERS):
            conv_project(nc, t, layer, a)
            conv_edges(nc, t, f"conv{layer}")
            conv_combine(nc, t, layer, a)
            conv_norm(nc, t, layer, a, out)


def kernel(**inputs):
    import numpy as np
    import concourse.bacc as bacc
    from concourse.bass_utils import run_bass_kernel_spmd

    a = lay_out(inputs)
    nc = bacc.Bacc("TRN2", target_bir_lowering=False, num_devices=1)
    aps = {name: nc.dram_tensor(f"in_{name}", v.shape, mybir.dt.from_np(v.dtype), kind="ExternalInput").ap()
           for name, v in a.items()}
    out = nc.dram_tensor("out", [NP, D], F32, kind="ExternalOutput").ap()
    program(nc, aps, out)
    r = run_bass_kernel_spmd(nc, [{f"in_{name}": v for name, v in a.items()}], core_ids=[0])
    return np.asarray(r.results[0]["out"])[:N]
```

```python
from contextlib import ExitStack, contextmanager

import concourse.bass as bass
from concourse import mybir

ALU = mybir.AluOpType
ACT = mybir.ActivationFunctionType
AX_X = mybir.AxisListType.X
F32 = mybir.dt.float32
I32 = mybir.dt.int32

P = 128
N = 12500
E = 200000
D = 128
HID = 256
HEADS = 4
C = D // HEADS
LAYERS = 2
EPS = 1e-5
BIG = 1e30

NB = -(-N // P)
NP = NB * P
CH = 16
GR = 4
KG = CH // GR
STEPS = -(-(-(-E // P) + NB - 1) // (P)) * P
STEPS = STEPS if STEPS % (2 * CH) == 0 else STEPS + CH
NC_ = STEPS // CH
PAIRS = NC_ // 2
SJ = STEPS // P
GB = 7
NG = NB // GB
GN = GB * P
QW = D + HEADS
AW = HEADS * (C + 2)
MW = D + 1
RING = 2 * CH
PW = 3 * P + 4
RK = 3
HK = 5
assert NB % GB == 0 and NC_ % 2 == 0 and SJ * P == STEPS


class Chain:

    def __init__(self, eng, sem):
        self.eng, self.sem, self.base, self.n = eng, sem, 0, 0

    def link(self, ins):
        self.n += 1
        ins.then_inc(self.sem, 1)
        self.eng.wait_ge(self.sem, self.base + self.n)

    def mark(self, ins):
        self.n += 1
        ins.then_inc(self.sem, 1)
        return self.n

    def need(self, mark):
        self.eng.wait_ge(self.sem, self.base + mark)

    @contextmanager
    def turns(self, count, per):
        start = self.base + self.n
        with self.eng.Fori(0, count) as i:
            self.base, self.n = start + i * per, 0
            yield i
            assert self.n == per, (self.n, per)
        self.base, self.n = start + count * per, 0


@contextmanager
def room(nc, phase):
    with ExitStack() as ctx:
        def sb(name, shape, dt=F32):
            return ctx.enter_context(nc.sbuf_tensor(f"{phase}_{name}", shape, dt))

        def psum(name, shape):
            return ctx.enter_context(nc.psum_tensor(f"{phase}_{name}", shape, F32))

        sems = []

        def sem(name):
            sems.append(nc.alloc_semaphore(f"{phase}_{name}"))
            return sems[-1]

        yield sb, psum, sem
    nc.clear_and_free_semaphores(sems)
    nc.all_engine_barrier()


class Tables:
    pass


def bc(ap, dim, shape):
    return ap.unsqueeze(dim).to_broadcast(shape)


def declare(nc, t, ctx):
    def dram(name, shape, dt=F32):
        return nc.dram_tensor(name, shape, dt, kind="Internal").ap()

    def sb(name, shape, dt=F32):
        return ctx.enter_context(nc.sbuf_tensor(name, shape, dt))

    t.f_d = dram("finish_steps", [STEPS])
    t.t_d = dram("tile_of_step", [STEPS + 2], I32)
    t.b_d = dram("block_of_step", [NC_, CH], I32)
    t.edge_d = dram("edge_records", [P, NC_, RK * CH])
    t.src_d = dram("source_records", [P, NC_, CH], I32)
    t.step_d = dram("step_records", [STEPS, HK])
    t.place_d = dram("place_rows", [NC_, CH * P])
    t.pen_d = dram("run_penalties", [STEPS, PW])
    t.h_d = dram("sage_in", [NP, D])
    t.p_d = dram("sage_hidden_projected", [NP, D])
    t.r_d = dram("sage_own_part", [NP, D])
    t.x1_d = dram("x_after_sage", [NP, D])
    t.hT_d = dram("conv_in_transposed", [P, NP])
    t.kv_d = dram("key_value", [NP, 2 * D])
    t.qreg = sb("query_table", [P, NB * QW])
    t.inv = sb("inverse_degree", [P, NB])
    t.iota = sb("iota_row", [P, P])
    t.ident = sb("identity", [P, P])
    t.minus = sb("minus_partition", [P, 1])
    t.hselT = sb("head_rows", [HEADS, HEADS * CH])
    t.hsel = sb("head_of_row", [HEADS * CH, HEADS])
    t.tsel = sb("step_of_row", [HEADS * CH, CH])


def declare_sums(nc, t, ctx):
    t.acc = ctx.enter_context(nc.sbuf_tensor("sums", [P, NB * AW], F32))


def setup_phase(nc, t, x, src, dst, wgt):
    with room(nc, "setup") as (sb, psum, sem):
        norm = InputNorm(t, x, sb, sem)
        dlast = sb("dlast", [P, SJ], I32)
        blast = sb("blast", [P, SJ], I32)
        blastf = sb("blastf", [P, SJ])
        fin = sb("fin", [P, SJ])
        sval = sb("sval", [P, SJ])
        part = sb("part", [P, 1])
        hv = sb("hv", [HEADS, HEADS * CH])
        hv1 = sb("hv1", [HEADS, HEADS * CH])
        fbc = sb("fbc", [P, STEPS])
        below = sb("below", [P, STEPS])
        tf = sb("tf", [P, SJ])
        ti = sb("ti", [P, SJ], I32)
        tpi = sb("tpi", [P, SJ], I32)
        tni = sb("tni", [P, SJ], I32)
        bf = sb("bf", [P, SJ])
        bi = sb("bi", [P, SJ], I32)
        b128 = sb("b128", [P, SJ])
        rows = {k: sb(f"rows_{k}", [P, SJ, P], I32) for k in ("dst", "prev", "next", "src")}
        wrow = sb("wrow", [P, SJ, P])
        df = sb("df", [P, SJ, P])
        sf = sb("sf", [P, SJ, P])
        rel = sb("rel", [P, SJ, P])
        dead = sb("dead", [P, SJ, P])
        inblk = sb("inblk", [P, SJ, P])
        pen = sb("pen", [P, SJ, PW])
        prevf = sb("prevf", [P, SJ])
        nextf = sb("nextf", [P, SJ])
        contl = sb("contl", [P, SJ])
        contr = sb("contr", [P, SJ])
        one = sb("one", [P, SJ])
        both = sb("both", [P, SJ])
        srec = sb("srec", [P, SJ, HK])
        erec = sb("erec", [P, NC_, RK * CH])
        srec_i = sb("srec_i", [P, NC_, CH], I32)
        ps = psum("ps_turn", [P, 4, 512])

        iotas = sem("iotas")
        dlast_in = sem("dlast_in")
        fin_ready = sem("fin_ready")
        fin_out = sem("fin_out")
        fbc_in = sem("fbc_in")
        steps_ready = sem("steps_ready")
        steps_out = sem("steps_out")
        near_in = sem("near_in")
        rows_in = sem("rows_in")
        chain_v = sem("chain_v")
        recs_ready = sem("recs_ready")
        turned = sem("turned")
        copied = sem("copied")
        tables_out = sem("tables_out")
        dst_rows = dst.rearrange("(t e) -> t e", e=P)
        src_rows = src.rearrange("(t e) -> t e", e=P)
        wgt_rows = wgt.rearrange("(t e) -> t e", e=P)

        with nc.Block() as block:
            @block.sync
            def _(sp):
                with nc.allow_non_contiguous_dma("small tables"):
                    sp.dma_start(dlast[:, :], dst_rows[:, P - 1:P].rearrange("(j p) o -> p (j o)", p=P),
                                 allow_slow_non_contiguous=True).then_inc(dlast_in, 16)
                    sp.wait_ge(fin_ready, 1)
                    sp.dma_start(t.f_d.rearrange("(j p) -> p j", p=P), fin[:, :],
                                 allow_slow_non_contiguous=True).then_inc(fin_out, 16)
                    sp.wait_ge(fin_out, 16)
                    sp.dma_start(fbc[:, :], t.f_d.partition_broadcast(P)).then_inc(fbc_in, 16)
                    sp.wait_ge(steps_ready, 1)
                    sp.dma_start(t.t_d[1:STEPS + 1].rearrange("(j p) -> p j", p=P), ti[:, :],
                                 allow_slow_non_contiguous=True).then_inc(steps_out, 16)
                    sp.dma_start(t.t_d[0:1].rearrange("(a b) -> a b", a=1), ti[0:1, 0:1]).then_inc(steps_out, 16)
                    sp.dma_start(t.t_d[STEPS + 1:STEPS + 2].rearrange("(a b) -> a b", a=1),
                                 ti[P - 1:P, SJ - 1:SJ]).then_inc(steps_out, 16)
                    sp.dma_start(t.b_d.rearrange("(j a) b -> (a b) j", a=P // CH), bi[:, :],
                                 allow_slow_non_contiguous=True).then_inc(steps_out, 16)
                    sp.wait_ge(steps_out, 64)
                    sp.dma_start(tpi[:, :], t.t_d[0:STEPS].rearrange("(j p) -> p j", p=P),
                                 allow_slow_non_contiguous=True).then_inc(near_in, 16)
                    sp.dma_start(tni[:, :], t.t_d[2:STEPS + 2].rearrange("(j p) -> p j", p=P),
                                 allow_slow_non_contiguous=True).then_inc(near_in, 16)
                    sp.wait_ge(recs_ready, 1)
                    sp.dma_start(t.pen_d.rearrange("(j p) w -> p j w", p=P), pen[:, :, :]).then_inc(tables_out, 16)
                    sp.dma_start(t.step_d.rearrange("(j p) w -> p j w", p=P), srec[:, :, :],
                                 allow_slow_non_contiguous=True).then_inc(tables_out, 16)
                    sp.dma_start(t.place_d.rearrange("(j a) (b e) -> (a b) j e", a=P // CH, e=P), rel[:, :, :]).then_inc(tables_out, 16)
                    sp.wait_ge(copied, SJ)
                    sp.dma_start(t.edge_d, erec[:, :, :]).then_inc(tables_out, 16)
                    sp.dma_start(t.src_d, srec_i[:, :, :]).then_inc(tables_out, 16)
                    sp.wait_ge(tables_out, 80)

            @block.gpsimd
            def _(pool):
                pool.iota(t.iota[:, :], [[1, P]], 0, 0, allow_small_or_imprecise_dtypes=True).then_inc(iotas, 1)
                pool.iota(part[:, :], [[0, 1]], 0, 1, allow_small_or_imprecise_dtypes=True).then_inc(iotas, 1)
                pool.iota(sval[:, :], [[P, SJ]], 0, 1, allow_small_or_imprecise_dtypes=True).then_inc(iotas, 1)
                pool.iota(hv[:, :], [[1, HEADS * CH]], 0, -CH, allow_small_or_imprecise_dtypes=True).then_inc(iotas, 1)
                pool.wait_ge(steps_ready, 1)

                def gather(out, table, index, j):
                    pool.indirect_dma_start(out[:, j, :], None, table,
                                            bass.IndirectOffsetOnAxis(ap=index[:, j:j + 1], axis=0)).then_inc(rows_in, 16)

                for j in range(SJ):
                    gather(rows["dst"], dst_rows, ti, j)
                    gather(rows["src"], src_rows, ti, j)
                    gather(wrow, wgt_rows, ti, j)
                pool.wait_ge(near_in, 32)
                for j in range(SJ):
                    gather(rows["prev"], dst_rows, tpi, j)
                    gather(rows["next"], dst_rows, tni, j)

            @block.vector
            def _(dve):
                link = Chain(dve, chain_v).link
                dve.wait_ge(iotas, 4)
                link(dve.tensor_scalar(t.ident[:, :], t.iota[:, :], part[:, 0:1], None, ALU.is_equal))
                link(dve.tensor_scalar(t.minus[:, :], part[:, 0:1], -1.0, None, ALU.mult))
                link(dve.tensor_scalar(hv1[:, :], hv[:, :], 0.0, None, ALU.is_ge))
                link(dve.scalar_tensor_tensor(t.hselT[:, :], hv[:, :], CH - 1.0, hv1[:, :], ALU.is_le, ALU.mult))
                corner = t.ident[0:HEADS * CH, 0:HEADS * CH]
                dve.tensor_reduce(t.hsel[:, :], corner.rearrange("p (h t) -> p h t", h=HEADS), AX_X, ALU.add)
                dve.tensor_reduce(t.tsel[:, :], corner.rearrange("p (h t) -> p t h", h=HEADS), AX_X, ALU.add)
                dve.wait_ge(dlast_in, 16)
                link(dve.tensor_scalar(blast[:, :], dlast[:, :], 7, None, ALU.arith_shift_right))
                link(dve.tensor_copy(blastf[:, :], blast[:, :]))
                dve.tensor_tensor(fin[:, :], blastf[:, :], sval[:, :], ALU.add).then_inc(fin_ready, 1)
                dve.wait_ge(fbc_in, 16)
                for j in range(SJ):
                    link(dve.tensor_scalar(below[:, :], fbc[:, :], sval[:, j:j + 1], 0.0, ALU.is_lt, ALU.add,
                                           accum_out=tf[:, j:j + 1]))
                link(dve.tensor_tensor(bf[:, :], sval[:, :], tf[:, :], ALU.subtract))
                link(dve.tensor_copy(ti[:, :], tf[:, :]))
                link(dve.tensor_scalar(b128[:, :], bf[:, :], float(P), None, ALU.mult))
                dve.tensor_copy(bi[:, :], bf[:, :]).then_inc(steps_ready, 1)
                norm.vector(dve)
                dve.wait_ge(rows_in, 16 * 5 * SJ)
                link(dve.tensor_copy(df[:, :, :], rows["dst"][:, :, :]))
                link(dve.tensor_copy(sf[:, :, :], rows["src"][:, :, :]))
                full = [P, SJ, P]
                link(dve.tensor_tensor(rel[:, :, :], df[:, :, :], bc(b128[:, :], 2, full), ALU.subtract))
                link(dve.tensor_scalar(inblk[:, :, :], rel[:, :, :], 0.0, None, ALU.is_ge))
                link(dve.scalar_tensor_tensor(inblk[:, :, :], rel[:, :, :], P - 1.0, inblk[:, :, :],
                                              ALU.is_le, ALU.mult))
                link(dve.tensor_scalar(dead[:, :, :], inblk[:, :, :], -1.0, BIG, ALU.add, ALU.mult))
                link(dve.memset(pen[:, :, :], 0.0))
                link(dve.tensor_tensor(pen[:, :, 1:P], df[:, :, 1:P], df[:, :, 0:P - 1], ALU.is_equal))
                link(dve.tensor_tensor(pen[:, :, P + 1:2 * P + 1], df[:, :, :],
                                       df[:, :, 0:1].to_broadcast(full), ALU.is_equal))
                link(dve.tensor_tensor(pen[:, :, 2 * P + 1:3 * P + 1], df[:, :, :],
                                       df[:, :, P - 1:P].to_broadcast(full), ALU.is_equal))
                link(dve.tensor_scalar(pen[:, :, :], pen[:, :, :], -1.0, BIG, ALU.add, ALU.mult))
                link(dve.tensor_copy(prevf[:, :], rows["prev"][:, :, P - 1]))
                link(dve.tensor_copy(nextf[:, :], rows["next"][:, :, 0]))
                link(dve.tensor_tensor(contl[:, :], prevf[:, :], df[:, :, 0], ALU.is_equal))
                link(dve.tensor_tensor(contr[:, :], nextf[:, :], df[:, :, P - 1], ALU.is_equal))
                link(dve.tensor_tensor(one[:, :], df[:, :, 0], df[:, :, P - 1], ALU.is_equal))
                link(dve.tensor_scalar(srec[:, :, 0], contl[:, :], -1.0, BIG, ALU.add, ALU.mult))
                link(dve.tensor_tensor(both[:, :], contl[:, :], one[:, :], ALU.mult))
                link(dve.tensor_scalar(srec[:, :, 1], both[:, :], -1.0, BIG, ALU.add, ALU.mult))
                link(dve.tensor_scalar(srec[:, :, 2], contr[:, :], -1.0, BIG, ALU.add, ALU.mult))
                link(dve.tensor_tensor(both[:, :], contr[:, :], one[:, :], ALU.mult))
                link(dve.tensor_scalar(srec[:, :, 3], both[:, :], -1.0, BIG, ALU.add, ALU.mult))
                dve.tensor_copy(srec[:, :, 4], rel[:, :, 0]).then_inc(recs_ready, 1)

            @block.tensor
            def _(pe):
                pe.wait_ge(recs_ready, 1)
                for j in range(SJ):
                    if j >= 4:
                        pe.wait_ge(copied, j - 3)
                    for k, rows_f in enumerate((rel, wrow, dead, sf)):
                        last = pe.transpose(ps[:, j % 4, P * k:P * k + P], rows_f[:, j, :], t.ident[:, :])
                    last.then_inc(turned, 1)

            @block.scalar
            def _(act):
                norm.scalar(act)
                per = P // CH
                for j in range(SJ):
                    act.wait_ge(turned, j + 1)
                    act.activation(
                        erec[:, per * j:per * j + per, :].rearrange("p c (k t) -> p k c t", k=RK),
                        ps[:, j % 4, 0:RK * P].rearrange("p (k c t) -> p k c t", k=RK, c=per), ACT.Copy)
                    act.activation(srec_i[:, per * j:per * j + per, :],
                                   ps[:, j % 4, RK * P:4 * P].rearrange("p (c t) -> p c t", c=per),
                                   ACT.Copy).then_inc(copied, 1)


def block_rows(table):
    return table.rearrange("(a p) f -> p a f", p=P)


def rows_of_turn(table, g):
    return block_rows(table)[:, bass.ds(g * GB, GB), :]


def sums_of_turn(t, g, width):
    return t.acc[:, bass.ds(g * (GB * width), GB * width)].rearrange("p (j w) -> p j w", w=width)


def staggered(eng, front, back, chain=None, per=0):
    def turn(g, h):
        return g * 2 + h, h, g

    front(turn(0, 0))
    with (chain.turns(NG // 2 - 1, per) if chain else eng.Fori(0, NG // 2 - 1)) as g:
        front(turn(g, 1))
        back(turn(g, 0))
        front(turn(g + 1, 0))
        back(turn(g, 1))
    last = NG // 2 - 1
    front(turn(last, 1))
    back(turn(last, 0))
    back(turn(last, 1))


def in_order(eng, body):
    with eng.Fori(0, NG // 2) as g:
        body((g * 2, 0, g))
        body((g * 2 + 1, 1, g))


class Norm:

    def __init__(self, sb, sem):
        self.stats = sb("ln_stats", [P, GB, 6])
        self.mv = sb("ln_mean_var", [P, 2, GB, 2])
        self.var, self.std, self.rstd, self.shift = (sb(f"ln_{k}", [P, 2, GB]) for k in ("var", "std", "rstd", "shift"))
        self.var_ready, self.std_ready, self.ln_ready = sem("var_ready"), sem("std_ready"), sem("ln_ready")
        self.go_aggr = sem("go_aggr")

    LINKS = 4

    def moments(self, dve, chain, x, h):
        for j in range(GB):
            last = dve.bn_stats(self.stats[:, j, :], x[:, j, :])
        chain.link(last)
        dve.sem_inc(self.go_aggr, 1)
        for j in range(GB):
            last = dve.bn_aggr(self.mv[:, h, j, :], self.stats[:, j, :])
        chain.link(last)
        dve.tensor_scalar(self.var[:, h, :], self.mv[:, h, :, 1], EPS, None, ALU.add).then_inc(self.var_ready, 1)

    def coefficients(self, dve, chain, n, h):
        dve.wait_ge(self.std_ready, n + 1)
        chain.link(dve.reciprocal(self.rstd[:, h, :], self.std[:, h, :]))
        chain.link(dve.scalar_tensor_tensor(self.shift[:, h, :], self.mv[:, h, :, 0], -1.0, self.rstd[:, h, :], ALU.mult, ALU.mult))
        dve.sem_inc(self.ln_ready, 1)

    def root(self, act, n, h):
        act.wait_ge(self.var_ready, n + 1)
        act.activation(self.std[:, h, :], self.var[:, h, :], ACT.Sqrt).then_inc(self.std_ready, 1)

    def apply(self, act, n, h, y, x):
        act.wait_ge(self.ln_ready, n + 1)
        for j in range(GB):
            last = act.activation(y[:, j, :], x[:, j, :], ACT.Relu, bias=self.shift[:, h, j:j + 1],
                                  scale=self.rstd[:, h, j:j + 1])
        return last


def x_of_turn(t, n):
    return t.qreg[:, bass.ds(n * GN, GN)].rearrange("p (j d) -> p j d", d=D)


class InputNorm:

    def __init__(self, t, x, sb, sem):
        self.t, self.x = t, x
        self.hb = sb("norm_hb", [P, 2, GB, D])
        self.h_ready, self.chain_v = sem("norm_h_ready"), sem("norm_chain_v")
        self.x_in = [sem(f"norm_x_in{h}") for h in range(2)]
        self.stored = [sem(f"norm_stored{h}") for h in range(2)]
        self.norm = Norm(sb, sem)

    def vector(self, dve):
        chain = Chain(dve, self.chain_v)

        def front(turn):
            n, h, g = turn
            dve.wait_ge(self.x_in[h], 16 * g + 32)
            self.norm.moments(dve, chain, x_of_turn(self.t, n), h)

        def back(turn):
            n, h, g = turn
            dve.wait_ge(self.h_ready, n + 1)
            self.norm.coefficients(dve, chain, n, h)

        staggered(dve, front, back, chain, 2 * Norm.LINKS)

    def scalar(self, act):
        for h in range(2):
            act.sem_inc(self.x_in[h], 16)

        def load(turn):
            n, h, g = turn
            act.wait_ge(self.x_in[h], 16 * g + 16)
            act.dma_start(x_of_turn(self.t, n), rows_of_turn(self.x, n)).then_inc(self.x_in[h], 16)

        in_order(act, load)
        act.sem_inc(self.h_ready, 2)
        for h in range(2):
            act.sem_inc(self.stored[h], 16)

        def front(turn):
            self.norm.root(act, turn[0], turn[1])

        def back(turn):
            n, h, g = turn
            act.wait_ge(self.stored[h], 16 * g + 16)
            self.norm.apply(act, n, h, self.hb[:, h, :, :], x_of_turn(self.t, n)).then_inc(self.h_ready, 1)
            act.wait_ge(self.h_ready, n + 3)
            act.dma_start(rows_of_turn(self.t.h_d, n), self.hb[:, h, :, :]).then_inc(self.stored[h], 16)

        staggered(act, front, back)
        for h in range(2):
            act.wait_ge(self.stored[h], 16 * (NG // 2) + 16)


def sage_edges(nc, t, table, tag):
    with room(nc, tag) as (sb, psum, sem):
        msg = sb("msg", [P, RING, MW])
        sel = sb("sel", [P, RING, P])
        src = sb("src", [P, 2, CH], I32)
        rec = sb("rec", [P, 2, RK * CH])
        blk = sb("blk", [1, 2, CH], I32)
        ps = psum("ps_sums", [P, 4, 512])
        zeroed, go_v, go_p = sem("zeroed"), sem("go_v"), sem("go_p")
        rec_in = [sem(f"rec_in{h}") for h in range(2)]
        blk_in = [sem(f"blk_in{h}") for h in range(2)]
        src_in = [sem(f"src_in{h}") for h in range(2)]
        gathered = [sem(f"gathered{k}") for k in range(2 * KG)]
        rec_used, ps_used = sem("rec_used"), sem("ps_used")
        sel_ready, sums_ready, chain_v = sem("sel_ready"), sem("sums_ready"), sem("chain_v")

        with nc.Block() as block:
            @block.sync
            def _(sp):
                with sp.Fori(0, PAIRS) as g:
                    for h in range(2):
                        c = g * 2 + h
                        sp.wait_ge(sums_ready, KG * c + KG)
                        sp.dma_start(src[:, h, :], t.src_d[:, bass.ds(c, 1), :]).then_inc(src_in[h], 16)
                        sp.wait_ge(rec_used, c + 1)
                        sp.dma_start(rec[:, h, :], t.edge_d[:, bass.ds(c, 1), :]).then_inc(rec_in[h], 16)
                        sp.dma_start(blk[:, h, :], t.b_d[bass.ds(c, 1), :]).then_inc(blk_in[h], 16)

            @block.gpsimd
            def _(pool):
                pool.wait_ge(zeroed, 2)
                with pool.Fori(0, PAIRS) as g:
                    for h in range(2):
                        c = g * 2 + h
                        pool.wait_ge(src_in[h], 16 * g + 16)
                        for k in range(KG):
                            pool.wait_ge(sums_ready, KG * c + k + 1)
                            pool.sem_inc(go_p, 1)
                            for i in range(GR):
                                slot = h * CH + k * GR + i
                                pool.indirect_dma_start(
                                    msg[:, slot, 0:D], None, table,
                                    bass.IndirectOffsetOnAxis(ap=src[:, h, k * GR + i:k * GR + i + 1], axis=0)).then_inc(gathered[h * KG + k], 16)

            @block.vector
            def _(dve):
                chain = Chain(dve, chain_v)
                dve.memset(t.acc[:, :], 0.0).then_inc(zeroed, 1)
                dve.memset(msg[:, :, D:MW], 1.0).then_inc(zeroed, 1)
                dve.wait_ge(zeroed, 2)
                dve.sem_inc(rec_used, 2)
                dve.sem_inc(ps_used, 2)
                regs = [dve.alloc_register(f"{tag}_block{i}") for i in range(CH)]
                with chain.turns(PAIRS, 2 * CH) as g:
                    for h in range(2):
                        c = g * 2 + h
                        dve.wait_ge(rec_in[h], 16 * g + 16)
                        for k in range(KG):
                            place = rec[:, h, k * GR:k * GR + GR]
                            dve.tensor_tensor(sel[:, h * CH + k * GR:h * CH + k * GR + GR, :],
                                              bc(t.iota[:, :], 1, [P, GR, P]), bc(place, 2, [P, GR, P]),
                                              ALU.is_equal).then_inc(sel_ready, 1)
                        dve.wait_ge(blk_in[h], 16 * g + 16)
                        dve.sem_inc(go_v, 1)
                        dve.load(regs, blk[0:1, h, :])
                        at = [dve.snap(r, min_val=0, max_val=NB - 1) for r in regs]
                        for k in range(KG):
                            dve.wait_ge(sums_ready, KG * c + k + 1 + 2 * KG)
                            for i in range(GR):
                                a = t.acc[:, bass.ds(at[k * GR + i] * MW, MW)]
                                part = ps[:, 2 * (k % 2) + i // 2, (i % 2) * MW:(i % 2) * MW + MW]
                                chain.link(dve.tensor_tensor(a, a, part, ALU.add))
                            dve.sem_inc(ps_used, 1)
                        dve.sem_inc(rec_used, 1)

            @block.tensor
            def _(pe):
                pe.sem_inc(sums_ready, 2 * KG)
                with pe.Fori(0, PAIRS) as g:
                    for h in range(2):
                        for k in range(KG):
                            n = g * (2 * KG) + (h * KG + k + 1)
                            pe.wait_ge(sel_ready, n)
                            pe.wait_ge(gathered[h * KG + k], 16 * GR * g + 16 * GR)
                            pe.wait_ge(ps_used, n)
                            for i in range(GR):
                                slot = h * CH + k * GR + i
                                last = pe.matmul(ps[:, 2 * (k % 2) + i // 2, (i % 2) * MW:(i % 2) * MW + MW],
                                                 sel[:, slot, :], msg[:, slot, :], start=True, stop=True)
                            last.then_inc(sums_ready, 1)


SPLIT = ((0, 512), (512, GN))


def sage_dense(nc, t, w1, b1, w2, b2):
    with room(nc, "sage_dense") as (sb, psum, sem):
        w1s = sb("w1s", [P, 2, HID])
        w2s = sb("w2s", [P, 2, 2, D])
        b1s = sb("b1s", [P, 2])
        b2s = sb("b2s", [P, D])
        hb = sb("hb", [P, GB, D])
        mean = sb("mean", [P, GB, D])
        hT = sb("hT", [P, GN])
        aT = sb("aT", [P, GN])
        hid = sb("hid", [P, 2, GN])
        own = sb("own", [P, GB, D])
        nbr = sb("nbr", [P, GB, D])
        ps = psum("ps_in", [P, 4 * 512])
        psh = psum("ps_hid", [P, 2, 1024])
        w_in, h_in, mean_ready, turned, copied, hid_ready, hid_copied = (
            sem(k) for k in ("w_in", "h_in", "mean_ready", "turned", "copied", "hid_ready", "hid_copied"))
        out_ready, inv_ready, own_ready, nbr_ready, stored, chain_v, go_v = (
            sem(k) for k in ("out_ready", "inv_ready", "own_ready", "nbr_ready", "stored", "chain_v", "go_v"))

        with nc.Block() as block:
            @block.sync
            def _(sp):
                sp.dma_start(w1s[:, :, :], w1.rearrange("(s k) h -> k s h", k=P)).then_inc(w_in, 16)
                for part in range(2):
                    sp.dma_start(w2s[:, :, part, :], w2[HID * part:HID * part + HID, :]
                                 .rearrange("(c k) o -> k c o", k=P)).then_inc(w_in, 16)
                sp.dma_start(b1s[:, :], b1.rearrange("(c k) -> k c", k=P), allow_slow_non_contiguous=True).then_inc(w_in, 16)
                sp.dma_start(b2s[:, :], b2.partition_broadcast(P)).then_inc(w_in, 16)
                with sp.Fori(0, NG) as g:
                    sp.wait_ge(turned, g + 1)
                    sp.dma_start(hb[:, :, :], rows_of_turn(t.h_d, g)).then_inc(h_in, 16)

            @block.vector
            def _(dve):
                chain = Chain(dve, chain_v)
                dve.wait_ge(w_in, 80)

                def average(n):
                    a = sums_of_turn(t, n, MW)
                    iv = t.inv[:, bass.ds(n * GB, GB)]
                    chain.link(dve.tensor_scalar(iv, a[:, :, D], 1.0, None, ALU.max))
                    dve.sem_inc(go_v, 1)
                    dve.reciprocal(iv, iv).then_inc(inv_ready, 1)
                    dve.wait_ge(inv_ready, n + 1)
                    dve.wait_ge(turned, n + 1)
                    dve.tensor_tensor(mean[:, :, :], a[:, :, 0:D], bc(iv, 2, [P, GB, D]), ALU.mult).then_inc(mean_ready, 1)

                def take_own(n):
                    dve.wait_ge(nbr_ready, n + 2)
                    dve.wait_ge(stored, 32 * n + 32)
                    dve.tensor_tensor(own[:, :, :], ps[:, 0:GB * 2 * D].rearrange("p (j w) -> p j w", j=GB)[:, :, 0:D],
                                      bc(b2s[:, :], 1, [P, GB, D]), ALU.add).then_inc(own_ready, 1)

                dve.sem_inc(own_ready, 1)
                average(0)
                with chain.turns(NG - 1, 1) as g:
                    average(g + 1)
                    take_own(g)
                take_own(NG - 1)

            @block.tensor
            def _(pe):
                def turn_rows(n):
                    pe.wait_ge(h_in, 16 * n + 16)
                    pe.wait_ge(mean_ready, n + 1)
                    for j in range(GB):
                        pe.transpose(psh[:, 0, P * j:P * j + P], hb[:, j, :], t.ident[:, :])
                    for j in range(GB):
                        last = pe.transpose(psh[:, 1, P * j:P * j + P], mean[:, j, :], t.ident[:, :])
                    last.then_inc(turned, 1)

                def hidden(n):
                    pe.wait_ge(copied, n * 2 + 2)
                    for c in range(2):
                        for lo, hi in SPLIT:
                            for s, rows in ((0, hT), (1, aT)):
                                last = pe.matmul(psh[:, c, lo:hi], w1s[:, s, P * c:P * c + P], rows[:, lo:hi],
                                                 start=(s == 0), stop=(s == 1))
                        last.then_inc(hid_ready, 1)
                    pe.wait_ge(hid_copied, n * 2 + 2)

                def project(n):
                    pe.wait_ge(own_ready, n + 1)
                    for j in range(GB):
                        for c in range(2):
                            last = pe.matmul(ps[:, 2 * D * j:2 * D * j + 2 * D], hid[:, c, P * j:P * j + P],
                                             w2s[:, c, :, :].rearrange("k s o -> k (s o)"), start=(c == 0), stop=(c == 1))
                    last.then_inc(out_ready, 1)

                pe.sem_inc(turned, 1)
                pe.wait_ge(w_in, 80)
                turn_rows(0)
                with pe.Fori(0, NG - 1) as g:
                    hidden(g)
                    turn_rows(g + 1)
                    project(g)
                hidden(NG - 1)
                project(NG - 1)

            @block.scalar
            def _(act):
                def copy_turned(n):
                    act.wait_ge(turned, n + 2)
                    act.activation(hT[:, :], psh[:, 0, 0:GN], ACT.Copy).then_inc(copied, 1)
                    act.activation(aT[:, :], psh[:, 1, 0:GN], ACT.Copy).then_inc(copied, 1)

                def take_hidden(n):
                    for c in range(2):
                        act.wait_ge(hid_ready, n * 2 + c + 1)
                        act.activation(hid[:, c, :], psh[:, c, 0:GN], ACT.Relu, bias=b1s[:, c:c + 1]).then_inc(hid_copied, 1)

                def take_nbr(n):
                    act.wait_ge(out_ready, n + 1)
                    act.wait_ge(stored, 32 * n + 32)
                    act.activation(nbr[:, :, :], ps[:, 0:GB * 2 * D].rearrange("p (j w) -> p j w", j=GB)[:, :, D:2 * D],
                                   ACT.Copy).then_inc(nbr_ready, 1)
                    act.wait_ge(nbr_ready, n + 2)
                    act.dma_start(rows_of_turn(t.p_d, n), nbr[:, :, :]).then_inc(stored, 16)
                    act.wait_ge(own_ready, n + 2)
                    act.dma_start(rows_of_turn(t.r_d, n), own[:, :, :]).then_inc(stored, 16)

                act.sem_inc(stored, 32)
                act.sem_inc(nbr_ready, 1)
                act.wait_ge(w_in, 80)
                copy_turned(0)
                with act.Fori(0, NG - 1) as g:
                    take_hidden(g)
                    copy_turned(g + 1)
                    take_nbr(g)
                take_hidden(NG - 1)
                take_nbr(NG - 1)
                act.wait_ge(stored, 32 * NG + 32)


def sage_output(nc, t, w_in_, b_in_):
    with room(nc, "sage_output") as (sb, psum, sem):
        ws = sb("ws", [P, D])
        bs = sb("bs", [P, 1])
        rb = sb("rb", [P, 2, GB, D])
        y = sb("y", [P, 2, GB, D])
        z = sb("z", [P, 2, GB, D])
        e = sb("e", [P, 2, GB, D])
        top = sb("top", [P, GB])
        tot = sb("tot", [P, NB])
        lse = sb("lse", [P, NB])
        stats = sb("stats", [P, 2, GB, 6])
        moments = sb("moments", [P, 2, GB, 2])
        mv = sb("mean_var", [P, NB, 2])
        var = sb("var", [P, NB])
        std = sb("std", [P, NB])
        rstd = sb("rstd", [P, NB])
        shift = sb("shift", [P, NB])
        hn = sb("hn", [P, 2, GB, D])
        hT = sb("hT", [P, 2, GN])
        res = sb("res", [P, 2, GN])
        ps = psum("ps_turn", [P, 2, 1024])
        psw = psum("ps_win", [P, 2, 1024])
        w_in, z_ready, exp_ready, tot_ready, lse_ready, x1_ready, x1_stored, var_ready, std_ready, shift_ready = (
            sem(k) for k in ("w_in", "z_ready", "exp_ready", "tot_ready", "lse_ready", "x1_ready", "x1_stored",
                             "var_ready", "std_ready", "shift_ready"))
        scaled, hn_ready_v, hn_ready_s, turned, copied, prod_ready, res_ready, chain_v, go_v = (
            sem(k) for k in ("scaled", "hn_ready_v", "hn_ready_s", "turned", "copied", "prod_ready", "res_ready",
                             "chain_v", "go_v"))
        r_in = [sem(f"r_in{h}") for h in range(2)]
        stored = [sem(f"stored{h}") for h in range(2)]
        full = [P, GB, D]
        OWN = 4

        def of_turn(table, n):
            return table[:, bass.ds(n * GB, GB)]

        with nc.Block() as block:
            @block.sync
            def _(sp):
                sp.dma_start(ws[:, :], w_in_).then_inc(w_in, 16)
                sp.dma_start(bs[:, :], b_in_.rearrange("(k a) -> k a", a=1), allow_slow_non_contiguous=True).then_inc(w_in, 16)

                def load(turn):
                    n, h, g = turn
                    sp.wait_ge(z_ready, n + 1)
                    sp.dma_start(rb[:, h, :, :], rows_of_turn(t.r_d, n)).then_inc(r_in[h], 16)

                def store(turn):
                    n, h, g = turn
                    sp.wait_ge(x1_ready, n + 1)
                    sp.dma_start(rows_of_turn(t.x1_d, n), x_of_turn(t, n)).then_inc(x1_stored, 16)

                in_order(sp, load)
                in_order(sp, store)
                sp.wait_ge(x1_stored, 16 * NG)

            @block.vector
            def _(dve):
                chain = Chain(dve, chain_v)
                link = chain.link
                dve.sem_inc(z_ready, 2)

                def front(turn):
                    n, h, g = turn
                    link(dve.tensor_tensor(y[:, h, :, :], sums_of_turn(t, n, MW)[:, :, 0:D],
                                           bc(of_turn(t.inv, n), 2, full), ALU.mult))
                    dve.wait_ge(r_in[h], 16 * g + 16)
                    link(dve.tensor_tensor(y[:, h, :, :], y[:, h, :, :], rb[:, h, :, :], ALU.add))
                    link(dve.tensor_reduce(top[:, :], y[:, h, :, :], AX_X, ALU.max))
                    dve.wait_ge(exp_ready, n + 1)
                    dve.tensor_tensor(z[:, h, :, :], y[:, h, :, :], bc(top[:, :], 2, full), ALU.subtract).then_inc(z_ready, 1)

                def back(turn):
                    n, h, g = turn
                    link(dve.tensor_tensor(x_of_turn(t, n), z[:, h, :, :], x_of_turn(t, n), ALU.add))
                    dve.wait_ge(exp_ready, n + 3)
                    dve.sem_inc(go_v, 1)
                    dve.tensor_reduce(of_turn(tot, n), e[:, h, :, :], AX_X, ALU.add).then_inc(tot_ready, 1)

                staggered(dve, front, back, chain, 2 * 4)

                def finish(turn):
                    n, h, g = turn
                    x1 = x_of_turn(t, n)
                    dve.tensor_tensor(x1, x1, bc(of_turn(lse, n), 2, full), ALU.subtract).then_inc(x1_ready, 1)
                    dve.wait_ge(x1_ready, n + 1)
                    dve.sem_inc(go_v, 1)
                    for j in range(GB):
                        last = dve.bn_stats(stats[:, h, j, :], x1[:, j, :])
                    link(last)
                    dve.sem_inc(go_v, 1)
                    for j in range(GB):
                        last = dve.bn_aggr(moments[:, h, j, :], stats[:, h, j, :])
                    link(last)
                    link(dve.tensor_copy(of_turn(mv, n), moments[:, h, :, :]))

                dve.wait_ge(lse_ready, 1)
                with chain.turns(NG // 2, 6) as g:
                    finish((g * 2, 0, g))
                    finish((g * 2 + 1, 1, g))
                dve.tensor_scalar(var[:, :], mv[:, :, 1], EPS, None, ALU.add).then_inc(var_ready, 1)
                dve.wait_ge(std_ready, 1)
                link(dve.reciprocal(rstd[:, :], std[:, :]))
                dve.scalar_tensor_tensor(shift[:, :], mv[:, :, 0], -1.0, rstd[:, :], ALU.mult, ALU.mult).then_inc(shift_ready, 1)
                dve.wait_ge(shift_ready, 1)
                dve.sem_inc(copied, 2)

                def normalise(turn):
                    n, h, g = turn
                    scale, bias = of_turn(rstd, n), of_turn(shift, n)
                    dve.wait_ge(turned, n + 1)
                    dve.sem_inc(go_v, 1)
                    for j in range(OWN, GB):
                        last = dve.tensor_scalar(hn[:, h, j, :], x_of_turn(t, n)[:, j, :], scale[:, j:j + 1],
                                                 bias[:, j:j + 1], ALU.mult, ALU.add)
                    last.then_inc(scaled, 1)
                    dve.wait_ge(scaled, n + 1)
                    dve.tensor_scalar(hn[:, h, OWN:GB, :], hn[:, h, OWN:GB, :], 0.0, None, ALU.max).then_inc(hn_ready_v, 1)

                def copy(turn):
                    n, h, g = turn
                    dve.wait_ge(turned, n + 3)
                    dve.wait_ge(prod_ready, n + 1)
                    dve.tensor_copy(hT[:, h, :], ps[:, h, 0:GN]).then_inc(copied, 1)

                staggered(dve, normalise, copy)

            @block.tensor
            def _(pe):
                pe.sem_inc(turned, 2)
                pe.sem_inc(prod_ready, 2)
                pe.wait_ge(w_in, 32)

                def body(turn):
                    n, h, g = turn
                    pe.wait_ge(hn_ready_v, n + 1)
                    pe.wait_ge(hn_ready_s, n + 1)
                    pe.wait_ge(copied, n + 1)
                    for j in range(GB):
                        last = pe.transpose(ps[:, h, P * j:P * j + P], hn[:, h, j, :], t.ident[:, :])
                    last.then_inc(turned, 1)
                    pe.wait_ge(copied, n + 3)
                    pe.wait_ge(res_ready, n + 1)
                    for lo, hi in SPLIT:
                        last = pe.matmul(psw[:, h, lo:hi], ws[:, :], hT[:, h, lo:hi], start=True, stop=True)
                    last.then_inc(prod_ready, 1)

                in_order(pe, body)

            @block.scalar
            def _(act):
                act.sem_inc(exp_ready, 2)
                act.sem_inc(res_ready, 2)
                for h in range(2):
                    act.sem_inc(stored[h], 16)
                act.wait_ge(w_in, 32)

                def exponentials(turn):
                    n, h, g = turn
                    act.wait_ge(z_ready, n + 3)
                    act.wait_ge(tot_ready, n + 1)
                    act.activation(e[:, h, :, :], z[:, h, :, :], ACT.Exp).then_inc(exp_ready, 1)

                act.sem_inc(tot_ready, 2)
                in_order(act, exponentials)
                act.wait_ge(tot_ready, NG + 2)
                act.activation(lse[:, :], tot[:, :], ACT.Ln).then_inc(lse_ready, 1)
                act.wait_ge(var_ready, 1)
                act.activation(std[:, :], var[:, :], ACT.Sqrt).then_inc(std_ready, 1)
                act.wait_ge(shift_ready, 1)

                def front(turn):
                    n, h, g = turn
                    act.wait_ge(turned, n + 1)
                    for j in range(OWN):
                        last = act.activation(hn[:, h, j, :], x_of_turn(t, n)[:, j, :], ACT.Relu,
                                              bias=of_turn(shift, n)[:, j:j + 1], scale=of_turn(rstd, n)[:, j:j + 1])
                    last.then_inc(hn_ready_s, 1)

                def back(turn):
                    n, h, g = turn
                    act.wait_ge(prod_ready, n + 3)
                    act.wait_ge(stored[h], 16 * g + 16)
                    act.activation(res[:, h, :], psw[:, h, 0:GN], ACT.Relu, bias=bs[:, 0:1]).then_inc(res_ready, 1)
                    act.wait_ge(res_ready, n + 3)
                    act.dma_start(t.hT_d[:, bass.ds(n * GN, GN)], res[:, h, :]).then_inc(stored[h], 16)

                staggered(act, front, back)
                for h in range(2):
                    act.wait_ge(stored[h], 16 * (NG // 2) + 16)


SCALE = float(C) ** -0.5


PARTS = ((0, 4), (4, GB))


def conv_project(nc, t, layer, a):
    with room(nc, f"project{layer}") as (sb, psum, sem):
        ws = sb("ws", [P, 3, D])
        bs = sb("bs", [P, 3, D])
        web = sb("web", [P, D])
        hT = sb("hT", [P, 2, GN])
        kv = sb("kv", [P, 2, GB, 2 * D])
        qe = sb("qe", [P, GB, D])
        ps = psum("ps_proj", [P, GB, 512])
        w_in, proj_ready, kv_ready, chain_v, go_v = (
            sem(k) for k in ("w_in", "proj_ready", "kv_ready", "chain_v", "go_v"))
        h_in = [sem(f"h_in{h}") for h in range(2)]
        stored = [sem(f"stored{h}") for h in range(2)]

        with nc.Block() as block:
            @block.sync
            def _(sp):
                for k, name in enumerate(("q", "k", "v")):
                    sp.dma_start(ws[:, k, :], a[f"L1_gnn_W{name}"][layer]).then_inc(w_in, 16)
                    sp.dma_start(bs[:, k, :], a[f"L1_gnn_b{name}"][layer].partition_broadcast(P)).then_inc(w_in, 16)
                sp.dma_start(web[:, :], a["L1_gnn_We"][layer].rearrange("a d -> (a d)").partition_broadcast(P)).then_inc(w_in, 16)
                with sp.Fori(0, NG // 2) as g:
                    for h in range(2):
                        n = g * 2 + h
                        sp.wait_ge(proj_ready, n * 2 + 2)
                        sp.dma_start(hT[:, h, :], t.hT_d[:, bass.ds(n * GN, GN)]).then_inc(h_in[h], 16)

            @block.tensor
            def _(pe):
                pe.wait_ge(w_in, 16 * 7)
                pe.sem_inc(proj_ready, 4)
                with pe.Fori(0, NG // 2) as g:
                    for h in range(2):
                        n = g * 2 + h
                        pe.wait_ge(h_in[h], 16 * g + 16)
                        for s, (lo, hi) in enumerate(PARTS):
                            pe.wait_ge(kv_ready, n * 2 + s + 1)
                            for j in range(lo, hi):
                                last = pe.matmul(ps[:, j, 0:3 * D], hT[:, h, P * j:P * j + P],
                                                 ws[:, :, :].rearrange("k s o -> k (s o)"), start=True, stop=True)
                            last.then_inc(proj_ready, 1)

            @block.vector
            def _(dve):
                chain = Chain(dve, chain_v)
                dve.sem_inc(kv_ready, 2)
                dve.wait_ge(w_in, 16 * 7)
                chain.link(dve.tensor_scalar(bs[:, 0, :], bs[:, 0, :], SCALE, None, ALU.mult))
                with chain.turns(NG // 2, 8) as g:
                    for h in range(2):
                        n = g * 2 + h
                        rows = t.qreg[:, bass.ds(n * (GB * QW), GB * QW)].rearrange("p (j w) -> p j w", w=QW)
                        for s, (lo, hi) in enumerate(PARTS):
                            part = [P, hi - lo, D]
                            dve.wait_ge(proj_ready, n * 2 + s + 5)
                            m = chain.mark(dve.scalar_tensor_tensor(rows[:, lo:hi, 0:D], ps[:, lo:hi, 0:D], SCALE,
                                                                    bc(bs[:, 0, :], 1, part), ALU.mult, ALU.add))
                            if s == 0:
                                dve.wait_ge(stored[h], 16 * g + 16)
                            dve.tensor_tensor(kv[:, h, lo:hi, :], ps[:, lo:hi, D:3 * D],
                                              bc(bs[:, 1:3, :].rearrange("p k d -> p (k d)"), 1, [P, hi - lo, 2 * D]),
                                              ALU.add).then_inc(kv_ready, 1)
                            chain.need(m)
                            chain.link(dve.tensor_tensor(qe[:, lo:hi, :], rows[:, lo:hi, 0:D], bc(web[:, :], 1, part), ALU.mult))
                            dve.sem_inc(go_v, 1)
                            dve.tensor_reduce(rows[:, lo:hi, D:QW], qe[:, lo:hi, :].rearrange("p j (h c) -> p j h c", h=HEADS),
                                              AX_X, ALU.add)

            @block.scalar
            def _(act):
                for h in range(2):
                    act.sem_inc(stored[h], 16)
                with act.Fori(0, NG // 2) as g:
                    for h in range(2):
                        n = g * 2 + h
                        act.wait_ge(kv_ready, n * 2 + 4)
                        act.dma_start(rows_of_turn(t.kv_d, n), kv[:, h, :, :]).then_inc(stored[h], 16)
                for h in range(2):
                    act.wait_ge(stored[h], 16 * (NG // 2) + 16)


def chunk(g, half):
    return g * 2 + half, half, g


PAIR = 2
KP = CH // PAIR
BANKS = 3


def conv_edges(nc, t, tag):
    with room(nc, tag) as (sb, psum, sem):
        HR = HEADS * CH
        kv = sb("kv", [P, RING, 2 * D])
        sel = sb("sel", [P, RING, P])
        selT = sb("selT", [P, KG, GR * P])
        src = sb("src", [P, 2, CH], I32)
        rec = sb("rec", [P, 2, RK * CH])
        blk = sb("blk", [1, 2, CH], I32)
        pen = sb("pen", [HR, 2, PW])
        stp = sb("stp", [HEADS, 2, CH, HK])
        prod = sb("prod", [P, 2, GR, D])
        score = sb("score", [P, HEADS, CH])
        qwe = sb("qwe", [P, HEADS, CH])
        fwd = sb("fwd", [HR, P])
        run = sb("run", [HR, P])
        top = sb("top", [HR, P])
        below = sb("below", [HR, P])
        expo = sb("expo", [HR, P])
        ends = sb("ends", [HR, 2, HEADS])
        fromleft = sb("fromleft", [HEADS, CH + 1])
        fromright = sb("fromright", [HEADS, CH + 1])
        sides = sb("sides", [HEADS, 2, CH])
        picked = sb("picked", [HR, 2, CH])
        side = sb("side", [HR, 2])
        newtop = sb("newtop", [HEADS, 1])
        drop = sb("drop", [HEADS, 1])
        fac = sb("fac", [HEADS, 1])
        facm = sb("facm", [HEADS, HEADS])
        node = sb("node", [HEADS, P])
        rescale = sb("rescale", [P, HEADS])
        pv = sb("pv", [P, CH, HEADS, C + 2])
        away = sb("away", [P, 2, GR, P])
        place = sb("place", [P, 2, CH * P])
        awayT = sb("awayT", [P, 2, GR * P])
        psQ = psum("ps_query", [P, 4, 512])
        psC = psum("ps_sums", [P, BANKS, 512])
        psM = psum("ps_small", [P, 512])
        rows = psM[0:HR, 0:P]
        psEnds = psM[0:HEADS, P:P + 2 * CH]
        psSides = psM[0:HR, 160:160 + 2 * CH]
        psFac = psM[:, 192:192 + HEADS]
        psExp = psM[:, 196:196 + HR]

        rec_in, blk_in, src_in, place_in = (
            [sem(f"{k}{h}") for h in range(2)] for k in ("rec_in", "blk_in", "src_in", "place_in"))
        gathered = [sem(f"gathered{k}") for k in range(2 * KG)]
        go_v, go_p, go_t, chain_v = (sem(k) for k in ("go_v", "go_p", "go_t", "chain_v"))
        scored, rec_used, blk_used, away_ready = (sem(k) for k in ("scored", "rec_used", "blk_used", "away_ready"))
        sel_ready, selT_ready, awayT_ready, place_used, q_ready, q_used = (
            sem(k) for k in ("sel_ready", "selT_ready", "awayT_ready", "place_used", "q_ready", "q_used"))
        rows_ready, ends_ready, ends_summed, sides_ready, sides_spread, drop_ready, fac_exp, fac_ready = (
            sem(k) for k in ("rows_ready", "ends_ready", "ends_summed", "sides_ready", "sides_spread", "drop_ready",
                             "fac_exp", "fac_ready"))
        below_ready, expo_ready, expo_turned, pv_ready, sums_ready, ps_used = (
            sem(k) for k in ("below_ready", "expo_ready", "expo_turned", "pv_ready", "sums_ready", "ps_used"))

        def sums_of(step):
            return psC[:, step // PAIR % BANKS, (step % PAIR) * AW:(step % PAIR) * AW + AW]

        with nc.Block() as block:
            @block.sync
            def _(sp):
                with sp.Fori(0, PAIRS) as g:
                    for h in range(2):
                        c = g * 2 + h
                        sp.wait_ge(place_used, c + 1)
                        sp.dma_start(place[:, h, :], t.place_d[bass.ds(c, 1), :].rearrange("a n -> (a n)")
                                     .partition_broadcast(P)).then_inc(place_in[h], 16)
                        sp.wait_ge(scored, c + 1)
                        sp.dma_start(src[:, h, :], t.src_d[:, bass.ds(c, 1), :]).then_inc(src_in[h], 16)
                        sp.wait_ge(rec_used, c + 1)
                        sp.dma_start(rec[:, h, :], t.edge_d[:, bass.ds(c, 1), :]).then_inc(rec_in[h], 16)
                        for k in range(HEADS):
                            sp.dma_start(pen[CH * k:CH * k + CH, h, :], t.pen_d[bass.ds(c * CH, CH), :]).then_inc(rec_in[h], 16)
                        sp.dma_start(stp[:, h, :, :], t.step_d[bass.ds(c * CH, CH), :].partition_broadcast(HEADS)).then_inc(rec_in[h], 16)
                        sp.wait_ge(blk_used, c + 1)
                        sp.dma_start(blk[:, h, :], t.b_d[bass.ds(c, 1), :]).then_inc(blk_in[h], 16)

            @block.gpsimd
            def _(pool):
                with pool.Fori(0, PAIRS) as g:
                    for h in range(2):
                        c = g * 2 + h
                        pool.wait_ge(src_in[h], 16 * g + 16)
                        for k in range(KG):
                            pool.wait_ge(pv_ready, KG * c + k + 1)
                            pool.sem_inc(go_p, 1)
                            for i in range(GR):
                                j = k * GR + i
                                pool.indirect_dma_start(
                                    kv[:, h * CH + j, :], None, t.kv_d,
                                    bass.IndirectOffsetOnAxis(ap=src[:, h, j:j + 1], axis=0)).then_inc(gathered[h * KG + k], 16)

            @block.vector
            def _(dve):
                chain = Chain(dve, chain_v)
                link, mark, need = chain.link, chain.mark, chain.need
                regs = [dve.alloc_register(f"{tag}_sumblock{i}") for i in range(CH)]
                link(dve.memset(t.acc[:, :], 0.0))
                link(dve.memset(fromleft[:, :], -BIG))
                link(dve.memset(fromright[:, :], -BIG))
                for s, n in ((scored, 2), (rec_used, 2), (blk_used, 2), (pv_ready, 2 * KG), (q_used, 2), (ps_used, 2)):
                    dve.sem_inc(s, n)

                def query(a, k):
                    return psQ[:, 2 * (k % 2):2 * (k % 2) + 2, 0:2 * QW].rearrange("p b (s w) -> p b s w", s=2)

                def multiply(a, k):
                    c, h, g = a
                    lo = h * CH + k * GR
                    dve.wait_ge(q_ready, KG * c + k + 1 + KG)
                    dve.wait_ge(gathered[h * KG + k], 16 * GR * g + 16 * GR)
                    return dve.tensor_tensor(
                        prod[:, k % 2, :, :].rearrange("p (b s) d -> p b s d", s=2), query(a, k)[:, :, :, 0:D],
                        kv[:, lo:lo + GR, 0:D].rearrange("p (b s) d -> p b s d", s=2), ALU.mult)

                def score_sum(a, k):
                    return mark(dve.tensor_reduce(score[:, :, k * GR:k * GR + GR].rearrange("p h i -> p i h"),
                                                  prod[:, k % 2, :, :].rearrange("p i (h c) -> p i h c", h=HEADS),
                                                  AX_X, ALU.add))

                def edge_term(a, k):
                    c, h, g = a
                    w = rec[:, h, CH + k * GR:CH + k * GR + GR].rearrange("p (b s) -> p b s", s=2)
                    return dve.tensor_tensor(qwe[:, :, k * GR:k * GR + GR].rearrange("p h (b s) -> p b s h", s=2),
                                             query(a, k)[:, :, :, D:QW], bc(w, 3, [P, 2, 2, HEADS]), ALU.mult)

                def first_edge_term(a):
                    if a is not None:
                        c, h, g = a
                        dve.wait_ge(rec_in[h], 96 * g + 96)
                        dve.wait_ge(q_ready, KG * c + 1 + KG)
                        edge_term(a, 0)

                def first_scores(a):
                    if a is not None:
                        multiply(a, 0).then_inc(q_used, 1)
                        dve.wait_ge(q_used, KG * a[0] + 1 + 2)
                        score_sum(a, 0)

                def weigh(b, k):
                    c, h, g = b
                    lo, j = h * CH + k * GR, k * GR
                    dve.tensor_tensor(pv[:, j:j + GR, :, 0:C],
                                      kv[:, lo:lo + GR, D:2 * D].rearrange("p i (h c) -> p i h c", h=HEADS),
                                      pv[:, j:j + GR, :, C:C + 1].to_broadcast([P, GR, HEADS, C]),
                                      ALU.mult).then_inc(pv_ready, 1)

                def rescaled(b, at):
                    a = t.acc[:, bass.ds(at[0] * AW, AW)].rearrange("p (h w) -> p h w", h=HEADS)
                    return mark(dve.tensor_tensor(a, a, bc(rescale[:, :], 2, [P, HEADS, C + 2]), ALU.mult))

                def stages(a, b, following):
                    before = [None]

                    def add(k, i):
                        if b is None:
                            return
                        step = k * GR + i
                        j = step // PAIR
                        if step % PAIR == 0:
                            dve.wait_ge(sums_ready, KP * b[0] + (j + 1 + 2 * KP))
                        if step > 0 and step % PAIR == 0:
                            dve.wait_ge(ps_used, KP * b[0] + (j + 2))
                        else:
                            need(before[0])
                        acc = t.acc[:, bass.ds(at[step] * AW, AW)]
                        ins = dve.tensor_tensor(acc, acc, sums_of(step), ALU.add)
                        if step % PAIR < PAIR - 1:
                            before[0] = mark(ins)
                        else:
                            ins.then_inc(ps_used, 1)

                    if a is None:
                        for k in range(KG):
                            weigh(b, k)
                    else:
                        c, h, g = a
                        if b is not None:
                            weigh(b, 0)
                            weigh(b, 1)
                    if b is not None:
                        dve.wait_ge(blk_in[b[1]], 16 * b[2] + 16)
                        dve.sem_inc(go_v, 1)
                        dve.load(regs, blk[0:1, b[1], :])
                        at = [dve.snap(r, min_val=0, max_val=NB - 1) for r in regs]
                        dve.sem_inc(blk_used, 1)
                        before[0] = rescaled(b, at)
                    if a is None:
                        for k in range(KG):
                            for i in range(GR):
                                add(k, i)
                        return
                    m = mark(multiply(a, 1))
                    add(0, 0)
                    need(m)
                    score_sum(a, 1)
                    add(0, 1)
                    edge_term(a, 1).then_inc(q_used, 1)
                    add(0, 2)
                    m = mark(multiply(a, 2))
                    add(0, 3)
                    if b is not None:
                        weigh(b, 2)
                    add(1, 0)
                    need(m)
                    score_sum(a, 2)
                    add(1, 1)
                    edge_term(a, 2).then_inc(q_used, 1)
                    add(1, 2)
                    m = mark(multiply(a, 3))
                    edge_term(a, 3).then_inc(q_used, 1)
                    need(m)
                    r = score_sum(a, 3)
                    add(1, 3)
                    step = [stp[:, h, :, n] for n in range(HK)]
                    dve.wait_ge(q_used, KG * c + KG + 2)
                    need(r)
                    m = mark(dve.tensor_tensor(score[:, :, :], score[:, :, :], qwe[:, :, :], ALU.add))
                    need(m)
                    dve.tensor_tensor(score[:, :, :], score[:, :, :],
                                      bc(rec[:, h, 2 * CH:3 * CH], 1, [P, HEADS, CH]), ALU.add).then_inc(scored, 1)
                    if b is not None:
                        weigh(b, 3)
                    dve.wait_ge(rows_ready, c + 1)
                    m = mark(dve.tensor_tensor_scan(fwd[:, :], pen[:, h, 0:P], rows, -BIG, ALU.add, ALU.max))
                    add(2, 0)
                    need(m)
                    m = mark(dve.tensor_tensor_scan(run[:, ::-1], pen[:, h, P:0:-1], fwd[:, ::-1], -BIG, ALU.add, ALU.max))
                    add(2, 1)
                    need(m)
                    dve.tensor_scalar(ends[:, 0, :], t.hsel[:, :], run[:, P - 1:P], None, ALU.mult)
                    dve.tensor_scalar(ends[:, 1, :], t.hsel[:, :], run[:, 0:1], None, ALU.mult).then_inc(ends_ready, 1)
                    add(2, 2)
                    dve.tensor_scalar(node[:, :], t.iota[0:HEADS, :], step[4][:, 0:1], None, ALU.is_equal)
                    add(2, 3)
                    dve.wait_ge(ends_summed, c + 1)
                    m1 = mark(dve.tensor_tensor_scan(fromleft[:, 1:CH + 1], step[1], psEnds[:, 0:CH], fromleft[:, 0:1],
                                                     ALU.add, ALU.max))
                    m2 = mark(dve.tensor_tensor_scan(fromright[:, CH - 1::-1], step[3][:, ::-1],
                                                     psEnds[:, 2 * CH - 1:CH - 1:-1], -BIG, ALU.add, ALU.max))
                    need(m1)
                    m1 = mark(dve.tensor_tensor(sides[:, 0, :], fromleft[:, 0:CH], step[0], ALU.add))
                    need(m2)
                    dve.tensor_tensor(sides[:, 1, :], fromright[:, 1:CH + 1], step[2], ALU.add).then_inc(sides_ready, 1)
                    need(m1)
                    m = mark(dve.tensor_tensor(newtop[:, :], fromright[:, 0:1], sides[:, 0, 0:1], ALU.max))
                    need(m)
                    m = mark(dve.tensor_tensor(drop[:, :], fromleft[:, 0:1], newtop[:, :], ALU.subtract))
                    add(3, 0)
                    need(m)
                    dve.tensor_scalar(drop[:, :], drop[:, :], 0.0, None, ALU.min).then_inc(drop_ready, 1)
                    dve.tensor_copy(fromleft[:, 0:1], fromleft[:, CH:CH + 1])
                    add(3, 1)
                    dve.wait_ge(sides_spread, c + 1)
                    m = mark(dve.tensor_tensor(picked[:, :, :], psSides.rearrange("p (s t) -> p s t", s=2),
                                               bc(t.tsel[:, :], 1, [HR, 2, CH]), ALU.mult))
                    add(3, 2)
                    need(m)
                    m = mark(dve.tensor_reduce(side[:, :], picked[:, :, :], AX_X, ALU.add))
                    first_edge_term(following)
                    need(m)
                    m = mark(dve.scalar_tensor_tensor(top[:, :], pen[:, h, P + 1:2 * P + 1], side[:, 0:1], run[:, :],
                                                      ALU.add, ALU.max))
                    dve.wait_ge(fac_exp, c + 1)
                    m1 = mark(dve.tensor_scalar(fac[:, :], fac[:, :], -1.0, None, ALU.add))
                    need(m)
                    m = mark(dve.scalar_tensor_tensor(top[:, :], pen[:, h, 2 * P + 1:3 * P + 1], side[:, 1:2], top[:, :],
                                                      ALU.add, ALU.max))
                    need(m1)
                    dve.tensor_scalar(facm[:, :], t.ident[0:HEADS, 0:HEADS], fac[:, 0:1], None, ALU.mult).then_inc(fac_ready, 1)
                    need(m)
                    dve.tensor_tensor(below[:, :], rows, top[:, :], ALU.subtract).then_inc(below_ready, 1)
                    add(3, 3)
                    first_scores(following)
                    dve.wait_ge(expo_turned, c + 1)
                    p = psExp.rearrange("p (h i) -> p i h", h=HEADS)
                    dve.tensor_copy(pv[:, :, :, C], p)
                    dve.tensor_tensor(pv[:, :, :, C + 1], p, bc(rec[:, h, CH:2 * CH], 2, [P, CH, HEADS]), ALU.mult)
                    m = mark(dve.tensor_scalar(rescale[:, :], psFac, 1.0, None, ALU.add))
                    need(m)
                    dve.sem_inc(rec_used, 1)

                first_edge_term(chunk(0, 0))
                first_scores(chunk(0, 0))
                stages(chunk(0, 0), None, chunk(0, 1))
                with chain.turns(PAIRS - 1, 2 * (2 * KG - 1 + 1 + CH - KP + 14)) as g:
                    stages(chunk(g, 1), chunk(g, 0), chunk(g + 1, 0))
                    stages(chunk(g + 1, 0), chunk(g, 1), chunk(g + 1, 1))
                stages(chunk(PAIRS - 1, 1), chunk(PAIRS - 1, 0), None)
                stages(None, chunk(PAIRS - 1, 1), None)

            @block.tensor
            def _(pe):
                pe.sem_inc(q_ready, KG)
                pe.sem_inc(sums_ready, 2 * KP)
                regs = [pe.alloc_register(f"{tag}_queryblock{i}") for i in range(CH)]

                def blocks_of(a):
                    c, h, g = a
                    pe.wait_ge(blk_in[h], 16 * g + 16)
                    pe.sem_inc(go_t, 1)
                    pe.load(regs, blk[0:1, h, :])
                    return loaded()

                def loaded():
                    return [pe.snap(r, min_val=0, max_val=NB - 1) for r in regs]

                def queries(a, k, at):
                    c, h, g = a
                    pe.wait_ge(selT_ready, KG * c + k + 1)
                    pe.wait_ge(q_used, KG * c + k + 1)
                    for i in range(GR):
                        last = pe.matmul(psQ[:, 2 * (k % 2) + i // 2, (i % 2) * QW:(i % 2) * QW + QW],
                                         selT[:, k, P * i:P * i + P],
                                         t.qreg[:, bass.ds(at[k * GR + i] * QW, QW)], start=True, stop=True)
                    last.then_inc(q_ready, 1)

                def sums(b, pairs):
                    if b is None:
                        return
                    c, h, g = b
                    for j in pairs:
                        if j % (GR // PAIR) == 0:
                            k = j // (GR // PAIR)
                            pe.wait_ge(pv_ready, KG * c + k + 1 + 2 * KG)
                            pe.wait_ge(sel_ready, KG * c + k + 1)
                        if j != 2:
                            pe.wait_ge(ps_used, KP * c + (j + 1 if j < 2 else j))
                        for step in range(PAIR * j, PAIR * j + PAIR):
                            last = pe.matmul(sums_of(step), sel[:, h * CH + step, :],
                                             pv[:, step, :, :].rearrange("p h w -> p (h w)"), start=True, stop=True)
                        last.then_inc(sums_ready, 1)

                def stages(a, b, at, following):
                    c = a[0]
                    sums(b, (0, 1))
                    sums(b, (2, 3))
                    queries(a, 3, at)
                    if following is not None:
                        at = blocks_of(following)
                    sums(b, (4, 5))
                    if following is not None:
                        queries(following, 0, at)
                    pe.wait_ge(scored, c + 1 + 2)
                    pe.sem_inc(go_t, 1)
                    pe.transpose(rows, score[:, :, :].rearrange("p h t -> p (h t)"), t.ident[:, :]).then_inc(rows_ready, 1)
                    sums(b, (6,))
                    pe.wait_ge(ends_ready, c + 1)
                    pe.sem_inc(go_t, 1)
                    pe.matmul(psEnds[:, 0:CH], ends[:, 0, :], t.tsel[:, :], start=True, stop=True)
                    pe.matmul(psEnds[:, CH:2 * CH], ends[:, 1, :], t.tsel[:, :], start=True, stop=True).then_inc(ends_summed, 1)
                    sums(b, (7,))
                    pe.wait_ge(sides_ready, c + 1)
                    pe.sem_inc(go_t, 1)
                    pe.matmul(psSides, t.hselT[:, :], sides[:, :, :].rearrange("p s t -> p (s t)"),
                              start=True, stop=True).then_inc(sides_spread, 1)
                    if following is not None:
                        queries(following, 1, at)
                    pe.wait_ge(expo_ready, c + 1)
                    pe.sem_inc(go_t, 1)
                    pe.transpose(psExp, expo[:, :], t.ident[0:HR, 0:HR])
                    pe.wait_ge(fac_ready, c + 1)
                    pe.sem_inc(go_t, 1)
                    pe.matmul(psFac, node[:, :], facm[:, :], start=True, stop=True).then_inc(expo_turned, 1)
                    if following is not None:
                        queries(following, 2, at)
                    return at

                at = blocks_of(chunk(0, 0))
                queries(chunk(0, 0), 0, at)
                queries(chunk(0, 0), 1, at)
                queries(chunk(0, 0), 2, at)
                at = stages(chunk(0, 0), None, at, chunk(0, 1))
                with pe.Fori(0, PAIRS - 1) as g:
                    at = stages(chunk(g, 1), chunk(g, 0), loaded(), chunk(g + 1, 0))
                    at = stages(chunk(g + 1, 0), chunk(g, 1), at, chunk(g + 1, 1))
                stages(chunk(PAIRS - 1, 1), chunk(PAIRS - 1, 0), loaded(), None)
                sums(chunk(PAIRS - 1, 1), range(KP))

            @block.scalar
            def _(act):
                act.sem_inc(place_used, 2)

                def select(a, k):
                    c, h, g = a
                    if k == 0:
                        act.wait_ge(rec_in[h], 96 * g + 96)
                    act.wait_ge(sums_ready, KP * c + (k + 1) * (GR // PAIR))
                    lo = h * CH + k * GR
                    for i in range(GR):
                        j = k * GR + i
                        act.activation(away[:, k % 2, i, :], t.iota[:, :], ACT.Abs, bias=rec[:, h, j:j + 1],
                                       scale=-1.0).then_inc(away_ready, 1)
                    act.wait_ge(away_ready, CH * c + GR * k + GR)
                    act.activation(sel[:, lo:lo + GR, :], away[:, k % 2, :, :], ACT.Relu, bias=1.0,
                                   scale=-1.0).then_inc(sel_ready, 1)

                def select_turned(a, k):
                    c, h, g = a
                    if k == 0:
                        act.wait_ge(place_in[h], 16 * g + 16)
                    act.activation(awayT[:, k % 2, :], place[:, h, k * GR * P:k * GR * P + GR * P], ACT.Abs,
                                   bias=t.minus[:, 0:1]).then_inc(awayT_ready, 1)
                    act.wait_ge(awayT_ready, KG * c + k + 1)
                    act.wait_ge(q_ready, KG * c + k + 1)
                    act.activation(selT[:, k, :], awayT[:, k % 2, :], ACT.Relu, bias=1.0,
                                   scale=-1.0).then_inc(selT_ready, 1)
                    if k == KG - 1:
                        act.sem_inc(place_used, 1)

                def stages(a, following):
                    c, h, g = a
                    if following is not None:
                        for k in range(KG // 2):
                            select_turned(following, k)
                    for k in range(KG):
                        select(a, k)
                    if following is not None:
                        for k in range(KG // 2, KG):
                            select_turned(following, k)
                    act.wait_ge(drop_ready, c + 1)
                    act.activation(fac[:, :], drop[:, :], ACT.Exp).then_inc(fac_exp, 1)
                    act.wait_ge(below_ready, c + 1)
                    act.activation(expo[:, :], below[:, :], ACT.Exp).then_inc(expo_ready, 1)

                for k in range(KG):
                    select_turned(chunk(0, 0), k)
                stages(chunk(0, 0), chunk(0, 1))
                with act.Fori(0, PAIRS - 1) as g:
                    stages(chunk(g, 1), chunk(g + 1, 0))
                    stages(chunk(g + 1, 0), chunk(g + 1, 1))
                stages(chunk(PAIRS - 1, 1), None)


def conv_combine(nc, t, layer, a):
    with room(nc, f"combine{layer}") as (sb, psum, sem):
        web = sb("web", [P, D])
        wbeta = sb("wbeta", [P, 3])
        wcols = sb("wcols", [P, 2])
        wall = sb("wall", [P, 2, P])
        wskip = sb("wskip", [P, D])
        bskip = sb("bskip", [P, 1])
        hT = sb("hT", [P, 2, GN])
        rden = sb("rden", [P, 2, GB, HEADS])
        out = sb("out", [P, 2, GB, HEADS, C])
        xrT = sb("xrT", [P, 2, GN])
        outT = sb("outT", [P, 2, GN])
        gate = sb("gate", [P, 2, GN])
        dif = sb("dif", [P, 2, GN])
        psX = psum("ps_skip", [P, 1024])
        psO = psum("ps_out", [P, 1024])
        psL = psum("ps_logit", [P, 1024])
        w_in, w_ready, out_ready, skip_ready, skip_copied, turned, copied, logit_ready, gate_ready, mixed, chain_v = (
            sem(k) for k in ("w_in", "w_ready", "out_ready", "skip_ready", "skip_copied", "turned", "copied",
                             "logit_ready", "gate_ready", "mixed", "chain_v"))
        h_in = [sem(f"h_in{h}") for h in range(2)]
        full4 = [P, GB, HEADS, C]

        with nc.Block() as block:
            @block.sync
            def _(sp):
                sp.dma_start(web[:, :], a["L1_gnn_We"][layer].rearrange("a d -> (a d)").partition_broadcast(P)).then_inc(w_in, 16)
                sp.dma_start(wbeta[:, :], a["L1_gnn_Wbeta"][layer].rearrange("(k d) a -> d (k a)", k=3),
                             allow_slow_non_contiguous=True).then_inc(w_in, 16)
                sp.dma_start(wskip[:, :], a["L1_gnn_Wskip"][layer]).then_inc(w_in, 16)
                sp.dma_start(bskip[:, :], a["L1_gnn_bskip"][layer].rearrange("(d a) -> d a", a=1),
                             allow_slow_non_contiguous=True).then_inc(w_in, 16)
                with sp.Fori(0, NG // 2) as g:
                    for h in range(2):
                        sp.wait_ge(skip_ready, g * 2 + h + 1)
                        sp.dma_start(hT[:, h, :], t.hT_d[:, bass.ds((g * 2 + h) * GN, GN)]).then_inc(h_in[h], 16)

            @block.vector
            def _(dve):
                chain = Chain(dve, chain_v)
                link = chain.link
                dve.wait_ge(w_in, 64)
                link(dve.tensor_tensor(wcols[:, 0:1], wbeta[:, 0:1], wbeta[:, 2:3], ALU.add))
                link(dve.tensor_tensor(wcols[:, 1:2], wbeta[:, 1:2], wbeta[:, 2:3], ALU.subtract))
                dve.tensor_copy(wall[:, :, :], bc(wcols[:, :], 2, [P, 2, P])).then_inc(w_ready, 1)

                def front(turn):
                    n, h, g = turn
                    s = sums_of_turn(t, n, AW).rearrange("p j (h w) -> p j h w", h=HEADS)
                    o = out[:, h, :, :, :]
                    link(dve.tensor_scalar(rden[:, h, :, :], s[:, :, :, C], 1e-20, None, ALU.max))
                    m = chain.mark(dve.reciprocal(rden[:, h, :, :], rden[:, h, :, :]))
                    dve.wait_ge(turned, n + 1)
                    link(dve.tensor_tensor(o, s[:, :, :, C + 1:C + 2].to_broadcast(full4),
                                           bc(web[:, :].rearrange("p (h c) -> p h c", h=HEADS), 1, full4), ALU.mult))
                    link(dve.tensor_tensor(o, o, s[:, :, :, 0:C], ALU.add))
                    chain.need(m)
                    dve.tensor_tensor(o, o, bc(rden[:, h, :, :], 3, full4), ALU.mult).then_inc(out_ready, 1)

                def back(turn):
                    n, h, g = turn
                    dve.wait_ge(copied, n + 3)
                    dve.wait_ge(skip_copied, n + 3)
                    link(dve.tensor_tensor(dif[:, h, :], xrT[:, h, :], outT[:, h, :], ALU.subtract))
                    dve.wait_ge(gate_ready, n + 2)
                    link(dve.tensor_tensor(dif[:, h, :], dif[:, h, :], gate[:, h, :], ALU.mult))
                    dve.tensor_tensor(t.qreg[:, bass.ds(n * GN, GN)], outT[:, h, :], dif[:, h, :], ALU.add).then_inc(mixed, 1)

                dve.sem_inc(mixed, 2)
                staggered(dve, front, back, chain, 12)

            @block.tensor
            def _(pe):
                pe.sem_inc(skip_ready, 2)
                pe.sem_inc(turned, 2)
                pe.wait_ge(w_in, 64)
                pe.wait_ge(w_ready, 1)

                def body(turn):
                    n, h, g = turn
                    pe.wait_ge(h_in[h], 16 * g + 16)
                    pe.wait_ge(skip_copied, n + 2)
                    for lo, hi in SPLIT:
                        last = pe.matmul(psX[:, lo:hi], wskip[:, :], hT[:, h, lo:hi], start=True, stop=True)
                    last.then_inc(skip_ready, 1)
                    pe.wait_ge(out_ready, n + 1)
                    pe.wait_ge(copied, n + 2)
                    for j in range(GB):
                        last = pe.transpose(psO[:, P * j:P * j + P], out[:, h, j, :, :].rearrange("p h c -> p (h c)"),
                                            t.ident[:, :])
                    last.then_inc(turned, 1)
                    pe.wait_ge(copied, n + 3)
                    pe.wait_ge(gate_ready, n + 1)
                    for lo, hi in SPLIT:
                        pe.matmul(psL[:, lo:hi], wall[:, 0, :], outT[:, h, lo:hi], start=True, stop=False)
                        last = pe.matmul(psL[:, lo:hi], wall[:, 1, :], xrT[:, h, lo:hi], start=False, stop=True)
                    last.then_inc(logit_ready, 1)

                in_order(pe, body)

            @block.scalar
            def _(act):
                act.sem_inc(copied, 2)
                act.sem_inc(skip_copied, 2)
                act.sem_inc(gate_ready, 1)
                act.wait_ge(w_in, 64)

                def body(turn):
                    n, h, g = turn
                    act.wait_ge(skip_ready, n + 3)
                    act.wait_ge(mixed, n + 1)
                    act.activation(xrT[:, h, :], psX[:, 0:GN], ACT.Identity, bias=bskip[:, 0:1]).then_inc(skip_copied, 1)
                    act.wait_ge(turned, n + 3)
                    act.activation(outT[:, h, :], psO[:, 0:GN], ACT.Copy).then_inc(copied, 1)
                    act.wait_ge(logit_ready, n + 1)
                    act.activation(gate[:, h, :], psL[:, 0:GN], ACT.Sigmoid).then_inc(gate_ready, 1)

                in_order(act, body)


STAT = 500
assert N % STAT == 0


def conv_norm(nc, t, layer, a, out):
    final = layer == LAYERS - 1
    with room(nc, f"batch_norm{layer}") as (sb, psum, sem):
        gamma = sb("gamma", [P, 1])
        beta = sb("beta", [P, 1])
        stats = sb("stats", [P, N // STAT, 6])
        mv = sb("mv", [P, 2])
        var = sb("var", [P, 1])
        std = sb("std", [P, 1])
        mul = sb("mul", [P, 1])
        shift = sb("shift", [P, 1])
        hT = sb("hT", [P, 2, GN])
        x1 = sb("x1", [P, 2, GB, D])
        rel = sb("rel", [P, 2, GN])
        new = sb("new", [P, 2, GN])
        res = sb("res", [P, 2, GB, D])
        ps = psum("ps_turn", [P, 2, 1024])
        w_in, var_ready, std_ready, shift_ready, rel_ready, new_ready, turned, res_ready, chain_v = (
            sem(k) for k in ("w_in", "var_ready", "std_ready", "shift_ready", "rel_ready", "new_ready",
                             "turned", "res_ready", "chain_v"))
        h_in, x_in, stored = ([sem(f"{k}{h}") for h in range(2)] for k in ("h_in", "x_in", "stored"))
        result_ready = res_ready if final else new_ready

        with nc.Block() as block:
            @block.sync
            def _(sp):
                sp.dma_start(gamma[:, :], a["L1_gnn_bn_gamma"][layer].rearrange("(d a) -> d a", a=1)).then_inc(w_in, 16)
                sp.dma_start(beta[:, :], a["L1_gnn_bn_beta"][layer].rearrange("(d a) -> d a", a=1)).then_inc(w_in, 16)

                def body(turn):
                    n, h, g = turn
                    sp.wait_ge(result_ready, n + 1)
                    sp.dma_start(hT[:, h, :], t.hT_d[:, bass.ds(n * GN, GN)]).then_inc(h_in[h], 16)
                    if final:
                        sp.dma_start(x1[:, h, :, :], rows_of_turn(t.x1_d, n)).then_inc(x_in[h], 16)

                in_order(sp, body)

            @block.vector
            def _(dve):
                chain = Chain(dve, chain_v)
                link = chain.link
                dve.sem_inc(new_ready, 2)
                if final:
                    dve.sem_inc(res_ready, 2)
                for j in range(N // STAT):
                    last = dve.bn_stats(stats[:, j, :], t.qreg[:, STAT * j:STAT * j + STAT])
                link(last)
                link(dve.bn_aggr(mv[:, :], stats[:, :, :].rearrange("p a b -> p (a b)")))
                dve.tensor_scalar(var[:, :], mv[:, 1:2], EPS, None, ALU.add).then_inc(var_ready, 1)
                dve.wait_ge(std_ready, 1)
                dve.wait_ge(w_in, 32)
                link(dve.reciprocal(mul[:, :], std[:, :]))
                link(dve.tensor_tensor(mul[:, :], mul[:, :], gamma[:, :], ALU.mult))
                link(dve.tensor_tensor(shift[:, :], mv[:, 0:1], mul[:, :], ALU.mult))
                dve.tensor_tensor(shift[:, :], beta[:, :], shift[:, :], ALU.subtract).then_inc(shift_ready, 1)

                def front(turn):
                    n, h, g = turn
                    dve.wait_ge(rel_ready, n + 1)
                    dve.wait_ge(h_in[h], 16 * g + 16)
                    if final:
                        dve.wait_ge(turned, n + 1)
                    else:
                        dve.wait_ge(stored[h], 16 * g + 16)
                    dve.tensor_tensor(new[:, h, :], rel[:, h, :], hT[:, h, :], ALU.add).then_inc(new_ready, 1)

                def back(turn):
                    n, h, g = turn
                    if final:
                        dve.wait_ge(x_in[h], 16 * g + 16)
                        dve.wait_ge(turned, n + 3)
                        dve.wait_ge(stored[h], 16 * g + 16)
                        dve.tensor_tensor(res[:, h, :, :], x1[:, h, :, :],
                                          ps[:, h, 0:GN].rearrange("p (j d) -> p j d", j=GB), ALU.add).then_inc(res_ready, 1)

                staggered(dve, front, back)

            @block.tensor
            def _(pe):
                def body(turn):
                    n, h, g = turn
                    pe.wait_ge(new_ready, n + 3)
                    pe.wait_ge(res_ready, n + 1)
                    for j in range(GB):
                        last = pe.transpose(ps[:, h, P * j:P * j + P], new[:, h, P * j:P * j + P], t.ident[:, :])
                    last.then_inc(turned, 1)

                if final:
                    pe.sem_inc(turned, 2)
                    in_order(pe, body)

            @block.scalar
            def _(act):
                for h in range(2):
                    act.sem_inc(stored[h], 16)
                act.wait_ge(var_ready, 1)
                act.activation(std[:, :], var[:, :], ACT.Sqrt).then_inc(std_ready, 1)
                act.wait_ge(shift_ready, 1)

                def front(turn):
                    n, h, g = turn
                    act.wait_ge(new_ready, n + 1)
                    act.activation(rel[:, h, :], t.qreg[:, bass.ds(n * GN, GN)], ACT.Relu, bias=shift[:, 0:1],
                                   scale=mul[:, 0:1]).then_inc(rel_ready, 1)

                def back(turn):
                    n, h, g = turn
                    act.wait_ge(result_ready, n + 3)
                    if final:
                        act.dma_start(rows_of_turn(out, n), res[:, h, :, :]).then_inc(stored[h], 16)
                    else:
                        act.dma_start(t.hT_d[:, bass.ds(n * GN, GN)], new[:, h, :]).then_inc(stored[h], 16)

                staggered(act, front, back)
                for h in range(2):
                    act.wait_ge(stored[h], 16 * (NG // 2) + 16)


_IN = ["x", "src", "dst", "edge_weight1", "L0_gnn_W1", "L0_gnn_b1", "L0_gnn_W2", "L0_gnn_b2", "L1_gnn_W_in",
       "L1_gnn_b_in", "L1_gnn_Wq", "L1_gnn_bq", "L1_gnn_Wk", "L1_gnn_bk", "L1_gnn_Wv", "L1_gnn_bv", "L1_gnn_We",
       "L1_gnn_Wskip", "L1_gnn_bskip", "L1_gnn_Wbeta", "L1_gnn_bn_gamma", "L1_gnn_bn_beta"]


def lay_out(inputs):
    import numpy as np

    a = {name: np.ascontiguousarray(np.asarray(inputs[name])) for name in _IN}
    x = np.zeros((NP, D), a["x"].dtype)
    x[:N] = a["x"]
    src = np.zeros((STEPS * P,), a["src"].dtype)
    src[:E] = a["src"]
    dst = np.full((STEPS * P,), NP - 1, a["dst"].dtype)
    dst[:E] = a["dst"]
    wgt = np.zeros((STEPS * P,), a["edge_weight1"].dtype)
    wgt[:E] = a["edge_weight1"].reshape(-1)
    a.update(x=x, src=src, dst=dst, edge_weight1=wgt)
    return a


def program(nc, a, out):
    t = Tables()
    with ExitStack() as ctx:
        declare(nc, t, ctx)
        setup_phase(nc, t, a["x"], a["src"], a["dst"], a["edge_weight1"])
        declare_sums(nc, t, ctx)
        sage_edges(nc, t, t.h_d, "first")
        sage_dense(nc, t, a["L0_gnn_W1"], a["L0_gnn_b1"], a["L0_gnn_W2"], a["L0_gnn_b2"])
        sage_edges(nc, t, t.p_d, "second")
        sage_output(nc, t, a["L1_gnn_W_in"], a["L1_gnn_b_in"])
        for layer in range(LAYERS):
            conv_project(nc, t, layer, a)
            conv_edges(nc, t, f"conv{layer}")
            conv_combine(nc, t, layer, a)
            conv_norm(nc, t, layer, a, out)


def kernel(**inputs):
    import numpy as np
    import concourse.bacc as bacc
    from concourse.bass_utils import run_bass_kernel_spmd

    a = lay_out(inputs)
    nc = bacc.Bacc("TRN2", target_bir_lowering=False, num_devices=1)
    aps = {name: nc.dram_tensor(f"in_{name}", v.shape, mybir.dt.from_np(v.dtype), kind="ExternalInput").ap()
           for name, v in a.items()}
    out = nc.dram_tensor("out", [NP, D], F32, kind="ExternalOutput").ap()
    program(nc, aps, out)
    r = run_bass_kernel_spmd(nc, [{f"in_{name}": v for name, v in a.items()}], core_ids=[0])
    return np.asarray(r.results[0]["out"])[:N]
```
